# Optimizing a Trainium2 kernel written in Bass

```python
import numpy as np
import jax
import jax.numpy as jnp

def _softmax(x, axis=-1):
    return jax.nn.softmax(x, axis=axis)

def _gelu(x):
    return jax.nn.gelu(x, approximate=True)

def _silu(x):
    return jax.nn.silu(x)

def _sigmoid(x):
    return jax.nn.sigmoid(x)

def _layernorm(x, axis=-1, eps=1e-05):
    m = jnp.mean(x, axis=axis, keepdims=True)
    v = jnp.var(x, axis=axis, keepdims=True)
    return (x - m) / jnp.sqrt(v + eps)

def _scatter_add(tgt, idx, src, axis=0):
    return tgt.at[idx].add(src)

def _segment_sum(src, seg, n):
    return jax.ops.segment_sum(src, seg, n)
kernel_name = 'mk_decoder_postln_d2_seqx_r4_55ddc0'

def setup_inputs(seed: int=0):
    np.random.seed(seed)
    _w = jnp.asarray

    def _rec_inputs():
        import jax
        import jax.numpy as jnp
        _rk = jax.random.key(seed)
        x = -0.0002928 + 1 * jax.random.normal(jax.random.fold_in(_rk, 1), (2, 1024, 256), jnp.float32)
        _lenS = 1024 - jax.random.randint(jax.random.fold_in(_rk, 7), (2,), 0, max(1, 1024 // 4) + 1, jnp.int32)
        _lenS2 = 64 - jax.random.randint(jax.random.fold_in(_rk, 8), (2,), 0, max(1, 64 // 4) + 1, jnp.int32)
        _ctx_1024P = jax.random.normal(jax.random.fold_in(_rk, 11), (2, 16, 256), jnp.float32)
        _ctx_1024c = jax.random.dirichlet(jax.random.fold_in(_rk, 511), 0.3 * jnp.ones((16,), jnp.float32), (2, 64))
        _ctx_1024t = jnp.einsum('bsk,bkd->bsd', _ctx_1024c, _ctx_1024P)
        _ctx_1024t = _ctx_1024t * jax.lax.rsqrt(jnp.mean(jnp.square(_ctx_1024t)) + 1e-12) * 0.953939
        ctx_1024 = 2.81802e-05 + 1.00001 * (_ctx_1024t + 0.3 * jax.random.normal(jax.random.fold_in(_rk, 611), (2, 64, 256), jnp.float32))
        fside_BxSxS2_0 = -1.47943e-05 + 1.00017 * jax.random.normal(jax.random.fold_in(_rk, 12), (2, 1024, 64), jnp.float32)
        return (x, ctx_1024, fside_BxSxS2_0)
    x, ctx_1024, fside_BxSxS2_0 = _rec_inputs()

    def _L0_attn_setup():
        import jax, jax.numpy as jnp
        import numpy as np
        EMB_DIM = 33
        FREQ = 10.0
        ORDER = 2

        def _hyena_filter(L, D, w1, b1, w2, b2, filt_bias, filt_decay):
            t = jnp.linspace(0.0, 1.0, L)[:, None]
            bands = jnp.linspace(0.0, EMB_DIM - 1.0, EMB_DIM)[None, :]
            pe = jnp.sin(t * bands * FREQ)
            h = jnp.sin(FREQ * (pe @ w1.T + b1)) @ w2.T + b2
            h = h.reshape(L, ORDER, D).transpose(1, 2, 0)
            t_window = jnp.linspace(0.0, 1.0, L)[None, None, :]
            decay = jnp.exp(-jnp.exp(filt_decay)[..., None] * t_window)
            h = h * decay + filt_bias[..., None]
            return h * (1.0 / L)

        def _depthwise_conv3(x, w, b):
            xp = jnp.pad(x, ((0, 0), (0, 0), (1, 1)))
            return w[:, 0, None] * xp[:, :, :-2] + w[:, 1, None] * xp[:, :, 1:-1] + w[:, 2, None] * xp[:, :, 2:] + b[:, None]
        key = jax.random.key(seed)
        ks = jax.random.split(key, 8)
        B, L, D = (2, 1024, 256)
        OD = (ORDER + 1) * D
        std = 0.02
        return {'u': jax.random.normal(ks[0], (B, L, D), jnp.float32), 'w_in': jax.random.normal(ks[1], (OD, D), jnp.float32) * std, 'b_in': jnp.zeros((OD,), jnp.float32), 'conv_w': jax.random.normal(ks[2], (OD, 3), jnp.float32) * std, 'conv_b': jnp.zeros((OD,), jnp.float32), 'w1': jax.random.normal(ks[3], (64, EMB_DIM), jnp.float32) * std, 'b1': jnp.zeros((64,), jnp.float32), 'w2': jax.random.normal(ks[4], (ORDER * D, 64), jnp.float32) * std, 'b2': jnp.zeros((ORDER * D,), jnp.float32), 'filt_bias': jnp.zeros((ORDER, D), jnp.float32), 'filt_decay': jnp.ones((ORDER, D), jnp.float32) * -3.0, 'w_out': jax.random.normal(ks[5], (D, D), jnp.float32) * std, 'b_out': jnp.zeros((D,), jnp.float32)}
    _L0_attn_all = _L0_attn_setup()
    _L0_attn_in = {k: v for k, v in _L0_attn_all.items() if k in ('w_in', 'b_in', 'conv_w', 'conv_b', 'w1', 'b1', 'w2', 'b2', 'filt_bias', 'filt_decay', 'w_out', 'b_out')}
    del _L0_attn_all

    def _L0_xattn_setup():
        import jax, jax.numpy as jnp
        import numpy as np
        B, LQ, ND, D = (4, 256, 1024, 256)
        key = jax.random.key(seed)
        k1, k2, k3, k4, k5, k6 = jax.random.split(key, 6)
        s = 1.0 / np.sqrt(D)
        return {'query': jax.random.normal(k1, (B, LQ, D), dtype=jnp.float32), 'documents': jax.random.normal(k2, (B, ND, D), dtype=jnp.float32), 'Wq': jax.random.uniform(k3, (D, D), dtype=jnp.float32, minval=-s, maxval=s), 'bq': jax.random.uniform(k4, (D,), dtype=jnp.float32, minval=-s, maxval=s), 'Wk': jax.random.uniform(k5, (D, D), dtype=jnp.float32, minval=-s, maxval=s), 'bk': jax.random.uniform(k6, (D,), dtype=jnp.float32, minval=-s, maxval=s)}
    _L0_xattn_all = _L0_xattn_setup()
    _L0_xattn_in = {k: v for k, v in _L0_xattn_all.items() if k in ('Wq', 'bq', 'Wk', 'bk')}
    del _L0_xattn_all

    def _L0_ffn_setup():
        import jax, jax.numpy as jnp
        import numpy as np
        B, T, D = (8, 1024, 256)
        NUM_SLOTS = 64
        TOP_K = 8
        DQ = D // 4
        DH = D // 2

        def _forward(x, slot_init, w1, b1, w2, b2, tau, Wih, Whh, bih, bhh, wq, bq, wk, bk, wv, bv, ln_g, ln_b, wvp, bvp, wo, bo):
            Bx, Tx, Dx = x.shape
            S = jnp.broadcast_to(slot_init[None], (Bx, NUM_SLOTS, Dx)).astype(x.dtype)
            slot_mean = jnp.broadcast_to(S.mean(axis=1, keepdims=True), (Bx, Tx, Dx))
            ctx = jnp.concatenate([x, slot_mean], axis=-1)
            h = jax.nn.gelu(ctx @ w1 + b1, approximate=False)
            route_logits = (h @ w2 + b2) / (jnp.abs(tau) + 0.1)
            topk_vals, topk_idx = jax.lax.top_k(route_logits, TOP_K)
            topk_w = jax.nn.softmax(topk_vals, axis=-1)
            alpha = (jax.nn.one_hot(topk_idx, NUM_SLOTS, dtype=x.dtype) * topk_w[..., None]).sum(axis=-2)
            slot_input = jnp.einsum('bts,btd->bsd', alpha, x)
            denom = alpha.sum(axis=1) + 1e-08
            si = slot_input / denom[..., None]
            gi = si @ Wih.T + bih
            gh = S @ Whh.T + bhh
            i_r, i_z, i_n = jnp.split(gi, 3, axis=-1)
            h_r, h_z, h_n = jnp.split(gh, 3, axis=-1)
            r = jax.nn.sigmoid(i_r + h_r)
            z = jax.nn.sigmoid(i_z + h_z)
            n = jnp.tanh(i_n + r * h_n)
            S_new = (1.0 - z) * n + z * S
            q = S_new @ wq + bq
            k = S_new @ wk + bk
            v = S_new @ wv + bv
            scale = DQ ** (-0.5)
            attn = jax.nn.softmax(jnp.einsum('bsq,btq->bst', q, k) * scale, axis=-1)
            S_comm = jnp.einsum('bst,btd->bsd', attn, v)
            y = S_new + S_comm
            mu = y.mean(axis=-1, keepdims=True)
            var = y.var(axis=-1, keepdims=True)
            y = (y - mu) * jax.lax.rsqrt(var + 1e-05) * ln_g + ln_b
            slot_values = y @ wvp + bvp
            out = jnp.einsum('bts,bsd->btd', alpha, slot_values)
            return out @ wo + bo
        key = jax.random.key(seed)
        ks = jax.random.split(key, 24)
        n = lambda k, shp, s=0.02: jax.random.normal(k, shp, dtype=jnp.float32) * s
        return {'x': jax.random.normal(ks[0], (B, T, D), dtype=jnp.float32), 'slot_init': n(ks[1], (NUM_SLOTS, D)), 'w1': n(ks[2], (2 * D, DH)), 'b1': jnp.zeros((DH,)), 'w2': n(ks[3], (DH, NUM_SLOTS)), 'b2': jnp.zeros((NUM_SLOTS,)), 'tau': jnp.ones((1,)), 'Wih': n(ks[4], (3 * D, D)), 'Whh': n(ks[5], (3 * D, D)), 'bih': jnp.zeros((3 * D,)), 'bhh': jnp.zeros((3 * D,)), 'wq': n(ks[6], (D, DQ)), 'bq': jnp.zeros((DQ,)), 'wk': n(ks[7], (D, DQ)), 'bk': jnp.zeros((DQ,)), 'wv': n(ks[8], (D, D)), 'bv': jnp.zeros((D,)), 'ln_g': jnp.ones((D,)), 'ln_b': jnp.zeros((D,)), 'wvp': n(ks[9], (D, D)), 'bvp': jnp.zeros((D,)), 'wo': n(ks[10], (D, D)), 'bo': jnp.zeros((D,))}
    _L0_ffn_all = _L0_ffn_setup()
    _L0_ffn_in = {k: v for k, v in _L0_ffn_all.items() if k in ('slot_init', 'w1', 'b1', 'w2', 'b2', 'tau', 'Wih', 'Whh', 'bih', 'bhh', 'wq', 'bq', 'wk', 'bk', 'wv', 'bv', 'ln_g', 'ln_b', 'wvp', 'bvp', 'wo', 'bo')}
    del _L0_ffn_all

    def _L1_attn_setup():
        import jax, jax.numpy as jnp
        import numpy as np
        NUM_HEADS = 16
        CHUNK_SIZE = 64
        NEG_INF = -1000000000.0

        def chunk_mask(seq_len, chunk_size):
            idx = jnp.arange(seq_len)
            cid = idx // chunk_size
            future = idx[None, :] > idx[:, None]
            diff_chunk = cid[None, :] != cid[:, None]
            return future & diff_chunk
        key = jax.random.key(seed)
        k1, k2, k3 = jax.random.split(key, 3)
        S, B, E = (512, 2, 256)
        x = jax.random.normal(k1, (S, B, E), dtype=jnp.float32)
        in_proj_w = jax.random.normal(k2, (3 * E, E), dtype=jnp.float32) * E ** (-0.5)
        in_proj_b = jnp.zeros((3 * E,), dtype=jnp.float32)
        out_proj_w = jax.random.normal(k3, (E, E), dtype=jnp.float32) * E ** (-0.5)
        out_proj_b = jnp.zeros((E,), dtype=jnp.float32)
        return {'x': x, 'in_proj_w': in_proj_w, 'in_proj_b': in_proj_b, 'out_proj_w': out_proj_w, 'out_proj_b': out_proj_b}
    _L1_attn_all = _L1_attn_setup()
    _L1_attn_in = {k: v for k, v in _L1_attn_all.items() if k in ('in_proj_w', 'in_proj_b', 'out_proj_w', 'out_proj_b')}
    del _L1_attn_all

    def _L1_xattn_setup():
        import jax, jax.numpy as jnp
        import numpy as np
        D = 256
        key = jax.random.key(seed)
        ks = jax.random.split(key, 13)
        B, S, d = (4, 512, D)
        inp = {'q_in': jax.random.normal(ks[0], (B, S, d), jnp.float32), 'k_in': jax.random.normal(ks[1], (B, S, d), jnp.float32), 'v_in': jax.random.normal(ks[2], (B, S, d), jnp.float32), 'phi_risk': jax.random.normal(ks[3], (B, S, S), jnp.float32), 'phi_prio': jax.random.normal(ks[4], (B, S, S), jnp.float32), 'phi_impl': jax.random.normal(ks[5], (B, S, S), jnp.float32), 'Wq': jax.random.normal(ks[6], (d, d), jnp.float32) / np.sqrt(d), 'bq': jax.random.normal(ks[7], (d,), jnp.float32) * 0.01, 'Wk': jax.random.normal(ks[8], (d, d), jnp.float32) / np.sqrt(d), 'bk': jax.random.normal(ks[9], (d,), jnp.float32) * 0.01, 'Wv': jax.random.normal(ks[10], (d, d), jnp.float32) / np.sqrt(d), 'bv': jax.random.normal(ks[11], (d,), jnp.float32) * 0.01, 'beta_risk': jnp.float32(0.1), 'beta_prio': jnp.float32(0.1), 'beta_impl': jnp.float32(0.1)}
        return inp
    _L1_xattn_all = _L1_xattn_setup()
    _L1_xattn_in = {k: v for k, v in _L1_xattn_all.items() if k in ('Wq', 'bq', 'Wk', 'bk', 'Wv', 'bv', 'beta_risk', 'beta_prio', 'beta_impl')}
    del _L1_xattn_all

    def _L1_ffn_setup():
        import jax, jax.numpy as jnp
        import numpy as np
        H = 256
        I = 128
        E = 32
        TOP_K = 6
        N_GROUP = 8
        TOPK_GROUP = 4
        SCALE = 2.5
        N_SHARED = 2
        SI = I * N_SHARED
        B, S = (2, 256)
        key = jax.random.key(seed)
        ks = jax.random.split(key, 8)
        x = jax.random.normal(ks[0], (B, S, H), jnp.float32)
        gate_weight = jax.random.normal(ks[1], (E, H), jnp.float32) * 0.02
        e_score_correction_bias = jax.random.normal(ks[2], (E,), jnp.float32) * 0.01
        experts_gate_up = jax.random.normal(ks[3], (E, 2 * I, H), jnp.float32) * 0.02
        experts_down = jax.random.normal(ks[4], (E, H, I), jnp.float32) * 0.02
        shared_gate_w = jax.random.normal(ks[5], (SI, H), jnp.float32) * 0.02
        shared_up_w = jax.random.normal(ks[6], (SI, H), jnp.float32) * 0.02
        shared_down_w = jax.random.normal(ks[7], (H, SI), jnp.float32) * 0.02
        return {'x': x, 'gate_weight': gate_weight, 'e_score_correction_bias': e_score_correction_bias, 'experts_gate_up': experts_gate_up, 'experts_down': experts_down, 'shared_gate_w': shared_gate_w, 'shared_up_w': shared_up_w, 'shared_down_w': shared_down_w}
    _L1_ffn_all = _L1_ffn_setup()
    _L1_ffn_in = {k: v for k, v in _L1_ffn_all.items() if k in ('gate_weight', 'e_score_correction_bias', 'experts_gate_up', 'experts_down', 'shared_gate_w', 'shared_up_w', 'shared_down_w')}
    del _L1_ffn_all
    return {'x': x, 'ctx_1024': ctx_1024, 'fside_BxSxS2_0': fside_BxSxS2_0, 'L0_attn_w_in': _L0_attn_in['w_in'], 'L0_attn_b_in': _L0_attn_in['b_in'], 'L0_attn_conv_w': _L0_attn_in['conv_w'], 'L0_attn_conv_b': _L0_attn_in['conv_b'], 'L0_attn_w1': _L0_attn_in['w1'], 'L0_attn_b1': _L0_attn_in['b1'], 'L0_attn_w2': _L0_attn_in['w2'], 'L0_attn_b2': _L0_attn_in['b2'], 'L0_attn_filt_bias': _L0_attn_in['filt_bias'], 'L0_attn_filt_decay': _L0_attn_in['filt_decay'], 'L0_attn_w_out': _L0_attn_in['w_out'], 'L0_attn_b_out': _L0_attn_in['b_out'], 'L0_xattn_Wq': _L0_xattn_in['Wq'], 'L0_xattn_bq': _L0_xattn_in['bq'], 'L0_xattn_Wk': _L0_xattn_in['Wk'], 'L0_xattn_bk': _L0_xattn_in['bk'], 'L0_ffn_slot_init': _L0_ffn_in['slot_init'], 'L0_ffn_w1': _L0_ffn_in['w1'], 'L0_ffn_b1': _L0_ffn_in['b1'], 'L0_ffn_w2': _L0_ffn_in['w2'], 'L0_ffn_b2': _L0_ffn_in['b2'], 'L0_ffn_tau': _L0_ffn_in['tau'], 'L0_ffn_Wih': _L0_ffn_in['Wih'], 'L0_ffn_Whh': _L0_ffn_in['Whh'], 'L0_ffn_bih': _L0_ffn_in['bih'], 'L0_ffn_bhh': _L0_ffn_in['bhh'], 'L0_ffn_wq': _L0_ffn_in['wq'], 'L0_ffn_bq': _L0_ffn_in['bq'], 'L0_ffn_wk': _L0_ffn_in['wk'], 'L0_ffn_bk': _L0_ffn_in['bk'], 'L0_ffn_wv': _L0_ffn_in['wv'], 'L0_ffn_bv': _L0_ffn_in['bv'], 'L0_ffn_ln_g': _L0_ffn_in['ln_g'], 'L0_ffn_ln_b': _L0_ffn_in['ln_b'], 'L0_ffn_wvp': _L0_ffn_in['wvp'], 'L0_ffn_bvp': _L0_ffn_in['bvp'], 'L0_ffn_wo': _L0_ffn_in['wo'], 'L0_ffn_bo': _L0_ffn_in['bo'], 'L1_attn_in_proj_w': _L1_attn_in['in_proj_w'], 'L1_attn_in_proj_b': _L1_attn_in['in_proj_b'], 'L1_attn_out_proj_w': _L1_attn_in['out_proj_w'], 'L1_attn_out_proj_b': _L1_attn_in['out_proj_b'], 'L1_xattn_Wq': _L1_xattn_in['Wq'], 'L1_xattn_bq': _L1_xattn_in['bq'], 'L1_xattn_Wk': _L1_xattn_in['Wk'], 'L1_xattn_bk': _L1_xattn_in['bk'], 'L1_xattn_Wv': _L1_xattn_in['Wv'], 'L1_xattn_bv': _L1_xattn_in['bv'], 'L1_xattn_beta_risk': _L1_xattn_in['beta_risk'], 'L1_xattn_beta_prio': _L1_xattn_in['beta_prio'], 'L1_xattn_beta_impl': _L1_xattn_in['beta_impl'], 'L1_ffn_gate_weight': _L1_ffn_in['gate_weight'], 'L1_ffn_e_score_correction_bias': _L1_ffn_in['e_score_correction_bias'], 'L1_ffn_experts_gate_up': _L1_ffn_in['experts_gate_up'], 'L1_ffn_experts_down': _L1_ffn_in['experts_down'], 'L1_ffn_shared_gate_w': _L1_ffn_in['shared_gate_w'], 'L1_ffn_shared_up_w': _L1_ffn_in['shared_up_w'], 'L1_ffn_shared_down_w': _L1_ffn_in['shared_down_w']}

def reference(x, ctx_1024, fside_BxSxS2_0, L0_attn_w_in, L0_attn_b_in, L0_attn_conv_w, L0_attn_conv_b, L0_attn_w1, L0_attn_b1, L0_attn_w2, L0_attn_b2, L0_attn_filt_bias, L0_attn_filt_decay, L0_attn_w_out, L0_attn_b_out, L0_xattn_Wq, L0_xattn_bq, L0_xattn_Wk, L0_xattn_bk, L0_ffn_slot_init, L0_ffn_w1, L0_ffn_b1, L0_ffn_w2, L0_ffn_b2, L0_ffn_tau, L0_ffn_Wih, L0_ffn_Whh, L0_ffn_bih, L0_ffn_bhh, L0_ffn_wq, L0_ffn_bq, L0_ffn_wk, L0_ffn_bk, L0_ffn_wv, L0_ffn_bv, L0_ffn_ln_g, L0_ffn_ln_b, L0_ffn_wvp, L0_ffn_bvp, L0_ffn_wo, L0_ffn_bo, L1_attn_in_proj_w, L1_attn_in_proj_b, L1_attn_out_proj_w, L1_attn_out_proj_b, L1_xattn_Wq, L1_xattn_bq, L1_xattn_Wk, L1_xattn_bk, L1_xattn_Wv, L1_xattn_bv, L1_xattn_beta_risk, L1_xattn_beta_prio, L1_xattn_beta_impl, L1_ffn_gate_weight, L1_ffn_e_score_correction_bias, L1_ffn_experts_gate_up, L1_ffn_experts_down, L1_ffn_shared_gate_w, L1_ffn_shared_up_w, L1_ffn_shared_down_w):
    import jax
    import jax.numpy as jnp

    def _L0_attn_ref(u, w_in, b_in, conv_w, conv_b, w1, b1, w2, b2, filt_bias, filt_decay, w_out, b_out):
        import jax, jax.numpy as jnp
        import numpy as np
        EMB_DIM = 33
        FREQ = 10.0
        ORDER = 2

        def _hyena_filter(L, D, w1, b1, w2, b2, filt_bias, filt_decay):
            t = jnp.linspace(0.0, 1.0, L)[:, None]
            bands = jnp.linspace(0.0, EMB_DIM - 1.0, EMB_DIM)[None, :]
            pe = jnp.sin(t * bands * FREQ)
            h = jnp.sin(FREQ * (pe @ w1.T + b1)) @ w2.T + b2
            h = h.reshape(L, ORDER, D).transpose(1, 2, 0)
            t_window = jnp.linspace(0.0, 1.0, L)[None, None, :]
            decay = jnp.exp(-jnp.exp(filt_decay)[..., None] * t_window)
            h = h * decay + filt_bias[..., None]
            return h * (1.0 / L)

        def _depthwise_conv3(x, w, b):
            xp = jnp.pad(x, ((0, 0), (0, 0), (1, 1)))
            return w[:, 0, None] * xp[:, :, :-2] + w[:, 1, None] * xp[:, :, 1:-1] + w[:, 2, None] * xp[:, :, 2:] + b[:, None]
        B, L, D = u.shape
        res = u @ w_in.T + b_in
        res = res.transpose(0, 2, 1)
        res = _depthwise_conv3(res, conv_w, conv_b)
        res = res.reshape(B, ORDER + 1, D, L)
        x = res[:, :-1]
        v = res[:, -1]
        h = _hyena_filter(L, D, w1, b1, w2, b2, filt_bias, filt_decay)
        n_fft = 2 * L
        for n in range(ORDER):
            v_fft = jnp.fft.rfft(v, n=n_fft, axis=-1)
            h_fft = jnp.fft.rfft(h[n], n=n_fft, axis=-1)
            y = jnp.fft.irfft(v_fft * h_fft, n=n_fft, axis=-1)[..., :L]
            v = y * x[:, n]
        return v.transpose(0, 2, 1) @ w_out.T + b_out

    def _L0_xattn_ref(query, documents, Wq, bq, Wk, bk):
        import jax, jax.numpy as jnp
        import numpy as np
        B, LQ, ND, D = (4, 256, 1024, 256)
        q = jnp.einsum('bqd,ed->bqe', query, Wq) + bq
        k = jnp.einsum('bnd,ed->bne', documents, Wk) + bk
        scores = jnp.einsum('bqe,bne->bqn', q, k)
        weights = jax.nn.softmax(scores, axis=-1)
        out = jnp.einsum('bqn,bnd->bqd', weights, documents)
        return out

    def _L0_ffn_ref(x, slot_init, w1, b1, w2, b2, tau, Wih, Whh, bih, bhh, wq, bq, wk, bk, wv, bv, ln_g, ln_b, wvp, bvp, wo, bo):
        import jax, jax.numpy as jnp
        import numpy as np
        B, T, D = (8, 1024, 256)
        NUM_SLOTS = 64
        TOP_K = 8
        DQ = D // 4
        DH = D // 2

        def _forward(x, slot_init, w1, b1, w2, b2, tau, Wih, Whh, bih, bhh, wq, bq, wk, bk, wv, bv, ln_g, ln_b, wvp, bvp, wo, bo):
            Bx, Tx, Dx = x.shape
            S = jnp.broadcast_to(slot_init[None], (Bx, NUM_SLOTS, Dx)).astype(x.dtype)
            slot_mean = jnp.broadcast_to(S.mean(axis=1, keepdims=True), (Bx, Tx, Dx))
            ctx = jnp.concatenate([x, slot_mean], axis=-1)
            h = jax.nn.gelu(ctx @ w1 + b1, approximate=False)
            route_logits = (h @ w2 + b2) / (jnp.abs(tau) + 0.1)
            topk_vals, topk_idx = jax.lax.top_k(route_logits, TOP_K)
            topk_w = jax.nn.softmax(topk_vals, axis=-1)
            alpha = (jax.nn.one_hot(topk_idx, NUM_SLOTS, dtype=x.dtype) * topk_w[..., None]).sum(axis=-2)
            slot_input = jnp.einsum('bts,btd->bsd', alpha, x)
            denom = alpha.sum(axis=1) + 1e-08
            si = slot_input / denom[..., None]
            gi = si @ Wih.T + bih
            gh = S @ Whh.T + bhh
            i_r, i_z, i_n = jnp.split(gi, 3, axis=-1)
            h_r, h_z, h_n = jnp.split(gh, 3, axis=-1)
            r = jax.nn.sigmoid(i_r + h_r)
            z = jax.nn.sigmoid(i_z + h_z)
            n = jnp.tanh(i_n + r * h_n)
            S_new = (1.0 - z) * n + z * S
            q = S_new @ wq + bq
            k = S_new @ wk + bk
            v = S_new @ wv + bv
            scale = DQ ** (-0.5)
            attn = jax.nn.softmax(jnp.einsum('bsq,btq->bst', q, k) * scale, axis=-1)
            S_comm = jnp.einsum('bst,btd->bsd', attn, v)
            y = S_new + S_comm
            mu = y.mean(axis=-1, keepdims=True)
            var = y.var(axis=-1, keepdims=True)
            y = (y - mu) * jax.lax.rsqrt(var + 1e-05) * ln_g + ln_b
            slot_values = y @ wvp + bvp
            out = jnp.einsum('bts,bsd->btd', alpha, slot_values)
            return out @ wo + bo
        return _forward(x, slot_init, w1, b1, w2, b2, tau, Wih, Whh, bih, bhh, wq, bq, wk, bk, wv, bv, ln_g, ln_b, wvp, bvp, wo, bo)

    def _L1_attn_ref(x, in_proj_w, in_proj_b, out_proj_w, out_proj_b):
        import jax, jax.numpy as jnp
        import numpy as np
        NUM_HEADS = 16
        CHUNK_SIZE = 64
        NEG_INF = -1000000000.0

        def chunk_mask(seq_len, chunk_size):
            idx = jnp.arange(seq_len)
            cid = idx // chunk_size
            future = idx[None, :] > idx[:, None]
            diff_chunk = cid[None, :] != cid[:, None]
            return future & diff_chunk
        S, B, E = x.shape
        H = NUM_HEADS
        D = E // H
        qkv = x @ in_proj_w.T + in_proj_b
        q, k, v = jnp.split(qkv, 3, axis=-1)
        q = q.reshape(S, B, H, D)
        k = k.reshape(S, B, H, D)
        v = v.reshape(S, B, H, D)
        scale = 1.0 / jnp.sqrt(jnp.asarray(D, dtype=x.dtype))
        scores = jnp.einsum('sbhd,tbhd->bhst', q * scale, k)
        mask = chunk_mask(S, CHUNK_SIZE)
        scores = jnp.where(mask[None, None, :, :], NEG_INF, scores)
        attn = jax.nn.softmax(scores, axis=-1)
        out = jnp.einsum('bhst,tbhd->sbhd', attn, v).reshape(S, B, E)
        return out @ out_proj_w.T + out_proj_b

    def _L1_xattn_ref(q_in, k_in, v_in, phi_risk, phi_prio, phi_impl, Wq, bq, Wk, bk, Wv, bv, beta_risk, beta_prio, beta_impl):
        import jax, jax.numpy as jnp
        import numpy as np
        D = 256
        d = q_in.shape[-1]
        scale = jnp.asarray(d, q_in.dtype) ** (-0.5)
        Q = q_in @ Wq.T + bq
        K = k_in @ Wk.T + bk
        V = v_in @ Wv.T + bv
        att = jnp.einsum('bsd,btd->bst', Q, K) * scale
        att = att + beta_risk * phi_risk + beta_prio * phi_prio - beta_impl * phi_impl
        w = jax.nn.softmax(att, axis=-1)
        return jnp.einsum('bst,btd->bsd', w, V)

    def _L1_ffn_ref(x, gate_weight, e_score_correction_bias, experts_gate_up, experts_down, shared_gate_w, shared_up_w, shared_down_w):
        import jax, jax.numpy as jnp
        import numpy as np
        H = 256
        I = 128
        E = 32
        TOP_K = 6
        N_GROUP = 8
        TOPK_GROUP = 4
        SCALE = 2.5
        N_SHARED = 2
        SI = I * N_SHARED
        B, S = (2, 256)
        b, s, h = x.shape
        xf = x.reshape(-1, h)
        T = xf.shape[0]
        logits = xf.astype(jnp.float32) @ gate_weight.astype(jnp.float32).T
        scores = jax.nn.sigmoid(logits)
        sfc = scores + e_score_correction_bias[None, :]
        gs = E // N_GROUP
        group_scores = sfc.reshape(T, N_GROUP, gs).max(axis=-1)
        _, gidx = jax.lax.top_k(group_scores, TOPK_GROUP)
        gmask = jnp.zeros((T, N_GROUP), bool).at[jnp.arange(T)[:, None], gidx].set(True)
        smask = jnp.repeat(gmask, gs, axis=1)
        masked = jnp.where(smask, sfc, 0.0)
        _, topk_idx = jax.lax.top_k(masked, TOP_K)
        tw = jnp.take_along_axis(scores, topk_idx, axis=1)
        tw = tw / (tw.sum(-1, keepdims=True) + 1e-20)
        tw = (tw * SCALE).astype(xf.dtype)
        combine = jnp.zeros((T, E), xf.dtype).at[jnp.arange(T)[:, None], topk_idx].add(tw)

        def expert_step(acc, inp):
            gu, dn, c = inp
            g = xf @ gu[:I].T
            u = xf @ gu[I:].T
            o = jax.nn.silu(g) * u @ dn.T
            return (acc + c[:, None] * o, None)
        routed, _ = jax.lax.scan(expert_step, jnp.zeros_like(xf), (experts_gate_up, experts_down, combine.T))
        sh = jax.nn.silu(xf @ shared_gate_w.T) * (xf @ shared_up_w.T)
        shared_out = sh @ shared_down_w.T
        return (routed + shared_out).reshape(b, s, h)
    x = _layernorm(x + _L0_attn_ref(x, L0_attn_w_in, L0_attn_b_in, L0_attn_conv_w, L0_attn_conv_b, L0_attn_w1, L0_attn_b1, L0_attn_w2, L0_attn_b2, L0_attn_filt_bias, L0_attn_filt_decay, L0_attn_w_out, L0_attn_b_out), axis=-1)
    x = _layernorm(x + _L0_xattn_ref(x, ctx_1024, L0_xattn_Wq, L0_xattn_bq, L0_xattn_Wk, L0_xattn_bk), axis=-1)
    x = _layernorm(x + _L0_ffn_ref(x, L0_ffn_slot_init, L0_ffn_w1, L0_ffn_b1, L0_ffn_w2, L0_ffn_b2, L0_ffn_tau, L0_ffn_Wih, L0_ffn_Whh, L0_ffn_bih, L0_ffn_bhh, L0_ffn_wq, L0_ffn_bq, L0_ffn_wk, L0_ffn_bk, L0_ffn_wv, L0_ffn_bv, L0_ffn_ln_g, L0_ffn_ln_b, L0_ffn_wvp, L0_ffn_bvp, L0_ffn_wo, L0_ffn_bo), axis=-1)
    x = _layernorm(x + _L1_attn_ref(x, L1_attn_in_proj_w, L1_attn_in_proj_b, L1_attn_out_proj_w, L1_attn_out_proj_b), axis=-1)
    x = _layernorm(x + _L1_xattn_ref(x, ctx_1024, ctx_1024, fside_BxSxS2_0, fside_BxSxS2_0, fside_BxSxS2_0, L1_xattn_Wq, L1_xattn_bq, L1_xattn_Wk, L1_xattn_bk, L1_xattn_Wv, L1_xattn_bv, L1_xattn_beta_risk, L1_xattn_beta_prio, L1_xattn_beta_impl), axis=-1)
    x = _layernorm(x + _L1_ffn_ref(x, L1_ffn_gate_weight, L1_ffn_e_score_correction_bias, L1_ffn_experts_gate_up, L1_ffn_experts_down, L1_ffn_shared_gate_w, L1_ffn_shared_up_w, L1_ffn_shared_down_w), axis=-1)
    return x

_drawn_inputs = setup_inputs


def setup_inputs(seed=0):
    import zlib

    import numpy as np

    out = dict(_drawn_inputs(seed))
    spreads = {'L0_attn_b_in': (0.0, 0.8),
     'L0_attn_conv_b': (0.0, 0.8),
     'L0_attn_b1': (0.0, 0.8),
     'L0_attn_b2': (0.0, 0.8),
     'L0_attn_filt_bias': (0.0, 0.8),
     'L0_attn_filt_decay': (-3.0, 0.6),
     'L0_attn_b_out': (0.0, 0.1),
     'L0_ffn_b1': (0.0, 0.8),
     'L0_ffn_b2': (0.0, 0.657),
     'L0_ffn_bih': (0.0, 0.1),
     'L0_ffn_bhh': (0.0, 0.486),
     'L0_ffn_bq': (0.0, 0.8),
     'L0_ffn_bk': (0.0, 0.8),
     'L0_ffn_bv': (0.0, 0.1),
     'L0_ffn_ln_g': (1.0, 0.6),
     'L0_ffn_ln_b': (0.0, 0.8),
     'L0_ffn_bvp': (0.0, 0.1),
     'L0_ffn_bo': (0.0, 0.1),
     'L1_attn_in_proj_b': (0.0, 0.1),
     'L1_attn_out_proj_b': (0.0, 0.1)}
    factors = {'fside_BxSxS2_0': 3.951,
     'L0_attn_w_in': 8.0,
     'L0_attn_conv_w': 8.0,
     'L0_attn_w1': 8.0,
     'L0_attn_w2': 8.0,
     'L0_attn_w_out': 8.0,
     'L0_xattn_bk': 8.0,
     'L0_ffn_slot_init': 8.0,
     'L0_ffn_w1': 8.0,
     'L0_ffn_w2': 8.0,
     'L0_ffn_Whh': 8.0,
     'L0_ffn_wq': 8.0,
     'L0_ffn_wk': 8.0,
     'L0_ffn_wv': 3.148,
     'L1_xattn_bq': 8.0,
     'L1_xattn_bk': 8.0,
     'L1_xattn_bv': 6.408,
     'L1_ffn_gate_weight': 5.232,
     'L1_ffn_e_score_correction_bias': 8.0,
     'L1_ffn_experts_gate_up': 4.622,
     'L1_ffn_experts_down': 4.653,
     'L1_ffn_shared_gate_w': 3.433,
     'L1_ffn_shared_up_w': 3.348,
     'L1_ffn_shared_down_w': 3.361}
    for name, (base, spread) in spreads.items():
        noise = np.random.default_rng([zlib.crc32(name.encode()), seed]).standard_normal(out[name].shape)
        drawn = base * np.exp(spread * noise) if base else spread * noise
        out[name] = jnp.asarray(drawn.astype(out[name].dtype))
    for name, factor in factors.items():
        out[name] = (out[name] * factor).astype(out[name].dtype)
    return out
```

```python
from contextlib import ExitStack
import math

import numpy as np
import concourse.bass as bass
from concourse import mybir

F32 = mybir.dt.float32
F32R = mybir.dt.float32r
ALU = mybir.AluOpType
ACT = mybir.ActivationFunctionType
AX = mybir.AxisListType

B, L, D = 2, 1024, 256
TOK = B * L
P = 128
TILES = TOK // P
UNITS = TILES // 2
GROUPS = TILES // 4
KD = D // P
BANK = 512
BLOCKS = L // P
CLASSES = BLOCKS
KEYS = 64
SLOTS, TOP_SLOTS = 64, 8
HEADS, HD = 16, 16
EXPERTS, GROUPS_E, TOP_GROUPS, TOP_E = 32, 8, 4, 6
SHARED = 2
ALL_E = EXPERTS + SHARED
EMB = 33
FREQ = 10.0
EPS = 1e-5
LOW, HIGH = -3.0e38, 3.0e38

COLS, _at = {}, 0
for _name, _n in (("b_in", 6), ("conv_w", 18), ("conv_b", 6), ("hy_b1", 1), ("x0_bq", 2), ("x0_bk", 2),
                  ("f_b1", 1), ("f_bq", 1), ("f_bk", 1), ("x1_bq", 2), ("x1_bk", 2)):
    COLS[_name] = (_at, _n)
    _at += _n
NCOLS = _at


class Record:
    pass


class Steps:

    def __init__(self, eng, sem):
        self.eng, self.sem, self.n = eng, sem, 0

    def mark(self, ins):
        ins.then_inc(self.sem, 1)
        self.n += 1
        return self.n

    def wait(self, value=None):
        self.eng.wait_ge(self.sem, self.n if value is None else value)

    def chain(self, ins):
        self.mark(ins)
        self.wait()


def new_semaphore(nc, m, name):
    m.semaphores.append(nc.alloc_semaphore(name))
    return m.semaphores[-1]


def end_layer(nc, m):
    nc.clear_and_free_semaphores(m.semaphores)
    m.semaphores = []
    nc.all_engine_barrier()


def col(m, name, j=0, rows=P):
    at = COLS[name][0] + j
    return m.cols[0:rows, at:at + 1]


def rows_of(vector, n=P):
    return vector.rearrange("(o n) -> o n", o=1).to_broadcast([n, vector.shape[0]])


def chunks(matrix):
    return matrix.rearrange("(k p) n -> p k n", p=P)



def norm_state(nc, m, scope, tag):
    s = Record()
    s.st = scope.enter_context(nc.sbuf_tensor(f"{tag}_st", [P, 2, 2, 6], F32))
    s.mv = scope.enter_context(nc.sbuf_tensor(f"{tag}_mv", [P, UNITS, 2, 2], F32))
    s.std = scope.enter_context(nc.sbuf_tensor(f"{tag}_std", [P, UNITS, 2], F32))
    s.rstd = scope.enter_context(nc.sbuf_tensor(f"{tag}_rstd", [P, UNITS, 2], F32))
    s.shift = scope.enter_context(nc.sbuf_tensor(f"{tag}_shift", [P, UNITS, 2], F32))
    s.out_done, s.summed, s.stats, s.root, s.scaled, s.normed, s.turned, s.xt_done = (
        new_semaphore(nc, m, f"{tag}_{n}") for n in
        ("out_done", "summed", "stats", "root", "scaled", "normed", "turned", "xt_done"))
    return s


def norm_sum(v, dve, m, s, u, bank, first=lambda: None):
    x = m.X[:, 2 * u:2 * u + 2, :]
    if bank is not None:
        v.wait_ge(s.out_done, u + 1)
        first()
        v.tensor_tensor(x, m.PS[:, bank, :].rearrange("p (i d) -> p i d", i=2), x, ALU.add).then_inc(s.summed, 1)
        v.wait_ge(s.summed, u + 1)
    for i in range(2):
        dve.mark(v.bn_stats(s.st[:, u % 2, i, :], m.X[:, 2 * u + i, :]))
    dve.wait()
    for i in range(2):
        v.bn_aggr(s.mv[:, u, i, :], s.st[:, u % 2, i, :]).then_inc(s.stats, 1)


def norm_root(a, m, s, u):
    a.wait_ge(s.stats, 2 * u + 2)
    a.activation(s.std[:, u, :], s.mv[:, u, :, 1], ACT.Sqrt, bias=m.eps[:, 0:1]).then_inc(s.root, 1)


def norm_scale(v, dve, s, u):
    v.wait_ge(s.root, u + 1)
    dve.chain(v.reciprocal(s.rstd[:, u, :], s.std[:, u, :]))
    v.scalar_tensor_tensor(s.shift[:, u, :], s.mv[:, u, :, 0], -1.0, s.rstd[:, u, :],
                           ALU.mult, ALU.mult).then_inc(s.scaled, 1)


def norm_apply(a, m, s, u):
    a.wait_ge(s.scaled, u + 1)
    for i in range(2):
        x = m.X[:, 2 * u + i, :]
        a.activation(x, x, ACT.Identity, bias=s.shift[:, u, i:i + 1],
                     scale=s.rstd[:, u, i:i + 1]).then_inc(s.normed, 1)


def norm_turn(t, m, s, u, banks):
    t.wait_ge(s.normed, 2 * u + 2)
    if u >= 2:
        t.wait_ge(s.xt_done, u - 1)
    out = m.PS[:, banks[u % 2], :].rearrange("p (k i t) -> p k i t", k=KD, i=2)
    for k in range(KD):
        for i in range(2):
            ins = t.transpose(out[:, k, i, :], m.X[:, 2 * u + i, k * P:(k + 1) * P], m.ident[:, :])
    ins.then_inc(s.turned, 1)


def norm_copy(a, m, s, u, banks):
    a.wait_ge(s.turned, u + 1)
    a.activation(m.XT[:, :, 2 * u * P:(2 * u + 2) * P],
                 m.PS[:, banks[u % 2], :].rearrange("p (k t) -> p k t", k=KD), ACT.Identity).then_inc(s.xt_done, 1)



def hyena_project(nc, d, m):
    C = 3 * D // P
    with ExitStack() as scope:
        sem = lambda n: new_semaphore(nc, m, f"pj_{n}")
        W = scope.enter_context(nc.sbuf_tensor("pj_w", [P, KD, 3 * D], F32))
        padded = scope.enter_context(nc.sbuf_tensor("pj_padded", [P, 2, B, L + 2], F32))
        taps = scope.enter_context(nc.sbuf_tensor("pj_taps", [P, 2, B, L], F32))
        loaded, xt_loaded, pads, eps_set = sem("loaded"), [sem(f"xt{g}") for g in range(GROUPS)], sem("pads"), sem("eps")
        product, biased, centre, tapped, turned, placed = (sem(n) for n in (
            "product", "biased", "centre", "tapped", "turned", "placed"))
        xT = chunks(d["xT"])
        with nc.Block(no_gpsimd_drain=True) as block:
            @block.sync
            def _(sp):
                sp.dma_start(W[:, :, :], chunks(d["hy_w_inT"])).then_inc(loaded, 16)
                sp.dma_start(m.XT[:, :, 0:BANK], xT[:, :, 0:BANK]).then_inc(xt_loaded[0], 16)
                sp.dma_start(m.cols[:, :], d["cols"]).then_inc(loaded, 16)
                sp.dma_start(m.ident[:, :], d["ident"]).then_inc(loaded, 16)
                for g in range(1, GROUPS):
                    sp.dma_start(m.XT[:, :, g * BANK:(g + 1) * BANK],
                                 xT[:, :, g * BANK:(g + 1) * BANK]).then_inc(xt_loaded[g], 16)

            @block.gpsimd
            def _(pool):
                pool.memset(padded[:, :, :, 0:1], 0.0).then_inc(pads, 1)
                pool.memset(padded[:, :, :, L + 1:L + 2], 0.0).then_inc(pads, 1)
                pool.memset(m.eps[:, :], EPS).then_inc(eps_set, 1)
                pool.memset(m.ones[:, :], 1.0).then_inc(eps_set, 1)

            @block.tensor
            def _(t):
                def project(c):
                    for g in range(GROUPS):
                        n = GROUPS * c + g
                        if c == 0:
                            t.wait_ge(xt_loaded[g], 16)
                        if n >= 4:
                            t.wait_ge(biased, n - 3)
                        for k in range(KD):
                            ins = t.matmul(m.PS[:, n % 4, :], W[:, k, c * P:(c + 1) * P],
                                           m.XT[:, k, g * BANK:(g + 1) * BANK], start=k == 0, stop=k == KD - 1)
                        ins.then_inc(product, 1)

                def turn(c):
                    t.wait_ge(tapped, 2 * c + 2)
                    for j in range(4):
                        n = 4 * c + j
                        if n >= 4:
                            t.wait_ge(placed, n - 3)
                        for i in range(4):
                            at = (4 * (j % 2) + i) * P
                            ins = t.transpose(m.PS[:, 4 + j, i * P:(i + 1) * P],
                                              taps[:, c % 2, j // 2, at:at + P], m.ident[:, :])
                        ins.then_inc(turned, 1)

                t.wait_ge(loaded, 48)
                project(0)
                for c in range(C):
                    if c + 1 < C:
                        project(c + 1)
                    turn(c)

            @block.scalar
            def _(a):
                a.wait_ge(loaded, 48)
                for c in range(C):
                    for g in range(GROUPS):
                        a.wait_ge(product, GROUPS * c + g + 1)
                        if c >= 2 and g == 0:
                            a.wait_ge(tapped, 2 * c - 2)
                        at = 1 + BANK * (g % 2)
                        a.activation(padded[:, c % 2, g // 2, at:at + BANK], m.PS[:, (GROUPS * c + g) % 4, :],
                                     ACT.Identity, bias=col(m, "b_in", c)).then_inc(biased, 1)
                    a.wait_ge(biased, GROUPS * c + GROUPS)
                    if c >= 2:
                        a.wait_ge(turned, 4 * (c - 1))
                    a.activation(taps[:, c % 2, :, :], padded[:, c % 2, :, 1:L + 1], ACT.Identity,
                                 bias=col(m, "conv_b", c), scale=col(m, "conv_w", 3 * c + 1)).then_inc(centre, 1)

            @block.vector
            def _(v):
                def tap(c):
                    v.wait_ge(centre, c + 1)
                    for n, j in enumerate((0, 2)):
                        if n:
                            v.wait_ge(tapped, 2 * c + 1)
                        v.scalar_tensor_tensor(taps[:, c % 2, :, :], padded[:, c % 2, :, j:j + L],
                                               col(m, "conv_w", 3 * c + j), taps[:, c % 2, :, :],
                                               ALU.mult, ALU.add).then_inc(tapped, 1)

                def place(c):
                    for j in range(4):
                        v.wait_ge(turned, 4 * c + j + 1)
                        at = (j // 2) * D + (c % 2) * P
                        v.tensor_copy(m.V[:, c // 2, 4 * (j % 2):4 * (j % 2) + 4, at:at + P],
                                      m.PS[:, 4 + j, :].rearrange("p (a c) -> p a c", a=4)).then_inc(placed, 1)

                v.wait_ge(pads, 2)
                v.wait_ge(loaded, 48)
                tap(0)
                for c in range(C):
                    if c + 1 < C:
                        tap(c + 1)
                    place(c)


def hyena_filter(nc, d, m):
    H = m.XT[:, :, :].rearrange("p k t -> p (k t)").rearrange("p (a n) -> p a n", n=BANK)
    two_pi = 2 * math.pi
    hi = 6.28125
    mid = float(np.float32(two_pi - hi))
    lo = two_pi - hi - mid
    magic = 1.5 * 2.0 ** 23
    with ExitStack() as scope:
        sem = lambda n: new_semaphore(nc, m, f"fl_{n}")
        sb = lambda n, shape: scope.enter_context(nc.sbuf_tensor(f"fl_{n}", shape, F32))
        pe, w1, w2 = sb("pe", [EMB, L]), sb("w1", [EMB, 64]), sb("w2", [65, 2 * D])
        negt, rate, shift = sb("negt", [P, BLOCKS]), sb("rate", [P, 2 * D]), sb("shift", [P, 2 * D])
        arg, turns, sine, decay = sb("arg", [64, L]), sb("turns", [64, L]), sb("sine", [65, L]), sb("decay", [P, BLOCKS, 2 * D])
        loaded, one, hidden, step, reduced, sined, rated, decayed, taps, filtered = (sem(n) for n in (
            "loaded", "one", "hidden", "step", "reduced", "sined", "rated", "decayed", "taps", "filtered"))
        with nc.Block(no_gpsimd_drain=True) as block:
            @block.sync
            def _(sp):
                for dst, src in ((pe[:, :], d["peT"]), (w1[:, :], d["hy_w1T"]), (w2[0:64, :], d["hy_w2T"]),
                                 (w2[64:65, :], d["hy_b2"].rearrange("(o n) -> o n", o=1)), (negt[:, :], d["negt"]),
                                 (rate[:, :], rows_of(d["hy_decay"])), (shift[:, :], rows_of(d["hy_fbias"]))):
                    sp.dma_start(dst, src).then_inc(loaded, 16)

            @block.tensor
            def _(t):
                t.wait_ge(loaded, 112)
                for g in range(2):
                    t.matmul(m.PS[0:64, g, :], w1[:, :], pe[:, g * BANK:(g + 1) * BANK],
                             start=True, stop=True).then_inc(hidden, 1)
                t.wait_ge(sined, 1)
                t.wait_ge(one, 1)
                for a in range(BLOCKS):
                    if a >= 4:
                        t.wait_ge(filtered, a - 3)
                    t.matmul(m.PS[:, 2 + a % 4, :], sine[:, a * P:(a + 1) * P], w2[:, :],
                             start=True, stop=True).then_inc(taps, 1)

            @block.scalar
            def _(a_):
                a_.wait_ge(loaded, 112)
                a_.activation(rate[:, :], rate[:, :], ACT.Exp).then_inc(rated, 1)
                a_.wait_ge(rated, 1)
                for a in range(BLOCKS):
                    a_.activation(decay[:, a, :], rate[:, :], ACT.Exp, scale=negt[:, a:a + 1]).then_inc(decayed, 1)
                a_.wait_ge(reduced, 1)
                a_.activation(sine[0:64, :], arg[:, :], ACT.Sin).then_inc(sined, 1)

            @block.vector
            def _(v):
                dve = Steps(v, step)
                v.memset(sine[64:65, :], 1.0).then_inc(one, 1)
                v.wait_ge(hidden, 2)
                v.wait_ge(loaded, 112)
                dve.chain(v.tensor_scalar(arg[:, :], m.PS[0:64, 0:2, :], col(m, "hy_b1", 0, 64), FREQ,
                                          ALU.add, ALU.mult))
                dve.chain(v.tensor_scalar(turns[:, :], arg[:, :], 1 / two_pi, magic, ALU.mult, ALU.add))
                dve.chain(v.tensor_scalar(turns[:, :], turns[:, :], magic, None, ALU.subtract))
                for part in (hi, mid, lo):
                    dve.chain(v.scalar_tensor_tensor(arg[:, :], turns[:, :], -part, arg[:, :], ALU.mult, ALU.add))
                pi = float(np.nextafter(np.float32(math.pi), np.float32(0)))
                v.tensor_scalar(arg[:, :], arg[:, :], -pi, pi, ALU.max, ALU.min).then_inc(reduced, 1)
                for a in range(BLOCKS):
                    v.wait_ge(taps, a + 1)
                    v.wait_ge(decayed, a + 1)
                    v.tensor_tensor(H[:, a, :], m.PS[:, 2 + a % 4, :], decay[:, a, :], ALU.mult).then_inc(filtered, 1)
                    v.wait_ge(filtered, a + 1)
                    v.tensor_tensor(H[:, a, :], H[:, a, :], shift[:, :], ALU.add)
    m.H = H



def hyena_convolve(nc, d, m):
    PAIRS = CLASSES // 2
    ORDERS = 2
    U = m.X[:, :, :].rearrange("p (s z) d -> p s (z d)", s=2).rearrange("p s (c r n) -> p s c r n", c=2, r=2)
    Y = m.XT[:, :, :].rearrange("p k t -> p (k t)").rearrange("p (a n) -> p a n", n=BANK)
    angle = lambda a, j: math.pi * a * (2 * j + 1) / 16
    with ExitStack() as scope:
        sem = lambda n: new_semaphore(nc, m, f"cv_{n}")
        sb = lambda n, shape: scope.enter_context(nc.sbuf_tensor(f"cv_{n}", shape, F32))
        FW, IV = sb("fw", [P, CLASSES, 3, P]), sb("iv", [P, CLASSES, 3, P])
        HS = sb("hs", [P, CLASSES, 2, 2 * D])
        EO = sb("eo", [P, 4, BANK])
        T = sb("t", [P, 2, 4, BANK])
        Z = sb("z", [P, 2, 2, BANK])
        Q = sb("q", [P, 4, BANK])
        TM = sb("tm", [P, 3, BANK])
        terms = sem("terms")
        loaded, step, pstep, evens, halves = sem("loaded"), sem("step"), sem("pstep"), sem("evens"), sem("halves")
        spectra, kept, products, joined, inverses, held, sums, added, updated = (sem(n) for n in (
            "spectra", "kept", "products", "joined", "inverses", "held", "sums", "added", "updated"))
        with nc.Block(no_gpsimd_drain=True) as block:
            @block.sync
            def _(sp):
                sp.dma_start(FW[:, :, :, :], d["forward"]).then_inc(loaded, 16)
                sp.dma_start(IV[:, :, :, :], d["inverse"]).then_inc(loaded, 16)

            @block.tensor
            def _(t):
                def complex_product(bank, M, c, re, im, sign):
                    plus, minus = (1, 2) if sign > 0 else (2, 1)
                    t.matmul(m.PS[:, bank, :], M[:, c, 0, :], re, start=True, stop=False)
                    t.matmul(m.PS[:, bank, :], M[:, c, minus, :], im, start=False, stop=True)
                    t.matmul(m.PS[:, bank + 1, :], M[:, c, 0, :], im, start=True, stop=False)
                    return t.matmul(m.PS[:, bank + 1, :], M[:, c, plus, :], re, start=False, stop=True)

                def forward(n):
                    j = n % PAIRS
                    t.wait_ge(halves, 4 * (n + 1))
                    if 0 < n <= PAIRS:
                        t.wait_ge(kept, 4 * n)
                    elif n > PAIRS:
                        t.wait_ge(products, 8 * (n - PAIRS))
                    for i, c in enumerate((j, CLASSES - 1 - j)):
                        ins = complex_product(2 * i, FW, c, U[:, n % 2, i, 0, :], U[:, n % 2, i, 1, :], -1)
                    ins.then_inc(spectra, 1)

                def inverse(n):
                    j, r = n % PAIRS, n - PAIRS
                    t.wait_ge(joined, 4 * (r + 1))
                    if r >= 1:
                        t.wait_ge(held, 4 * r)
                    for i, c in enumerate((j, CLASSES - 1 - j)):
                        ins = complex_product(4 + 2 * i, IV, c, T[:, i, 0, :], T[:, i, 2, :], 1)
                    ins.then_inc(inverses, 1)

                t.wait_ge(loaded, 32)
                for n in range(PAIRS):
                    forward(n)
                for o in range(ORDERS):
                    for s in range(PAIRS + 1):
                        if s < PAIRS:
                            forward(PAIRS * (o + 1) + s)
                        if s >= 1:
                            inverse(PAIRS * (o + 1) + s - 1)

            @block.scalar
            def _(a):
                def scale_evens(n, src):
                    if n >= 1:
                        a.wait_ge(evens, n)
                    for i, block_ in enumerate((2, 4, 6)):
                        a.activation(TM[:, i, :], src(block_), ACT.Copy,
                                     scale=-math.sin(angle(block_, n % PAIRS))).then_inc(terms, 1)

                def keep(n):
                    a.wait_ge(spectra, n + 1)
                    for i, c in enumerate((n, CLASSES - 1 - n)):
                        for r in range(2):
                            a.activation(HS[:, c, r, :], m.PS[:, 2 * i + r, :], ACT.Identity).then_inc(kept, 1)

                def hold(r):
                    a.wait_ge(inverses, r + 1)
                    if r >= 1:
                        a.wait_ge(sums, 4 * r)
                    for i in range(2):
                        for z in range(2):
                            a.activation(Z[:, i, z, :], m.PS[:, 4 + 2 * i + z, :], ACT.Identity).then_inc(held, 1)

                for n in range(PAIRS + 1):
                    if n < PAIRS:
                        scale_evens(n, lambda b: m.H[:, b, :])
                    if n >= 1:
                        keep(n - 1)
                for o in range(ORDERS):
                    if o:
                        a.wait_ge(updated, o)
                    for s in range(PAIRS + 2):
                        if s < PAIRS:
                            scale_evens(PAIRS * (o + 1) + s, lambda b: m.V[:, 2, b, :])
                        if s >= 2:
                            hold(PAIRS * o + s - 2)

            @block.gpsimd
            def _(pool):
                own = Steps(pool, pstep)

                def evens_im(n):
                    if n >= 1:
                        pool.wait_ge(halves, 4 * n)
                    pool.wait_ge(terms, 3 * (n + 1))
                    own.chain(pool.tensor_tensor(EO[:, 2, :], TM[:, 0, :], TM[:, 1, :], ALU.add))
                    pool.tensor_tensor(EO[:, 2, :], EO[:, 2, :], TM[:, 2, :], ALU.add).then_inc(evens, 1)

                def join(r):
                    pool.wait_ge(products, 8 * (r + 1))
                    for i in range(2):
                        pool.tensor_tensor(T[:, i, 0, :], T[:, i, 0, :], T[:, i, 1, :], ALU.subtract).then_inc(joined, 1)
                        pool.tensor_tensor(T[:, i, 2, :], T[:, i, 2, :], T[:, i, 3, :], ALU.add).then_inc(joined, 1)

                def sum_pair(r):
                    pool.wait_ge(held, 4 * (r + 1))
                    if r >= 1:
                        pool.wait_ge(added, 16 * r)
                    for z, op, to in ((0, ALU.add, 0), (1, ALU.subtract, 2), (0, ALU.subtract, 1), (1, ALU.add, 3)):
                        pool.tensor_tensor(Q[:, to, :], Z[:, 0, z, :], Z[:, 1, z, :], op).then_inc(sums, 1)

                for n in range(PAIRS):
                    evens_im(n)
                for o in range(ORDERS):
                    for s in range(PAIRS + 2):
                        if s < PAIRS:
                            evens_im(PAIRS * (o + 1) + s)
                        if 1 <= s <= PAIRS:
                            join(PAIRS * o + s - 1)
                        if s >= 2:
                            sum_pair(PAIRS * o + s - 2)

            @block.vector
            def _(v):
                dve = Steps(v, step)

                def split(n, src):
                    j = n % PAIRS
                    cos, sin = lambda a: math.cos(angle(a, j)), lambda a: -math.sin(angle(a, j))
                    if n >= 1:
                        v.wait_ge(halves, 4 * n)
                    dve.mark(v.scalar_tensor_tensor(EO[:, 0, :], src(2), cos(2), src(0), ALU.mult, ALU.add))
                    dve.mark(v.tensor_scalar(EO[:, 1, :], src(1), cos(1), None, ALU.mult))
                    dve.mark(v.tensor_scalar(EO[:, 3, :], src(1), sin(1), None, ALU.mult))
                    for a in (3, 5, 7):
                        dve.wait()
                        if a < 7:
                            dve.mark(v.scalar_tensor_tensor(EO[:, 0, :], src(a + 1), cos(a + 1), EO[:, 0, :], ALU.mult, ALU.add))
                        dve.mark(v.scalar_tensor_tensor(EO[:, 1, :], src(a), cos(a), EO[:, 1, :], ALU.mult, ALU.add))
                        dve.mark(v.scalar_tensor_tensor(EO[:, 3, :], src(a), sin(a), EO[:, 3, :], ALU.mult, ALU.add))
                    dve.wait()
                    if n >= 2:
                        v.wait_ge(spectra, n - 1)
                    v.tensor_tensor(U[:, n % 2, 0, 0, :], EO[:, 0, :], EO[:, 1, :], ALU.add).then_inc(halves, 1)
                    v.tensor_tensor(U[:, n % 2, 1, 0, :], EO[:, 0, :], EO[:, 1, :], ALU.subtract).then_inc(halves, 1)
                    v.wait_ge(evens, n + 1)
                    v.tensor_tensor(U[:, n % 2, 0, 1, :], EO[:, 3, :], EO[:, 2, :], ALU.add).then_inc(halves, 1)
                    v.tensor_tensor(U[:, n % 2, 1, 1, :], EO[:, 3, :], EO[:, 2, :], ALU.subtract).then_inc(halves, 1)

                def multiply(r):
                    o, j = r // PAIRS, r % PAIRS
                    v.wait_ge(spectra, PAIRS + r + 1)
                    if r >= 1:
                        v.wait_ge(inverses, r)
                    else:
                        v.wait_ge(kept, 4 * PAIRS)
                    for i, c in enumerate((j, CLASSES - 1 - j)):
                        h = [HS[:, c, z, o * D:(o + 1) * D].unsqueeze(1).to_broadcast([P, B, D]) for z in range(2)]
                        for to, (vz, hz) in enumerate(((0, 0), (1, 1), (0, 1), (1, 0))):
                            v.tensor_tensor(T[:, i, to, :].rearrange("p (b n) -> p b n", b=B),
                                            m.PS[:, 2 * i + vz, :].rearrange("p (b n) -> p b n", b=B),
                                            h[hz], ALU.mult).then_inc(products, 1)

                def gather(r):
                    j = r % PAIRS
                    v.wait_ge(sums, 4 * (r + 1))
                    for a in range(BLOCKS):
                        q = Q[:, a % 2, :]
                        if j == 0:
                            v.tensor_scalar(Y[:, a, :], q, math.cos(angle(a, j)), None, ALU.mult).then_inc(added, 1)
                        else:
                            v.scalar_tensor_tensor(Y[:, a, :], q, math.cos(angle(a, j)), Y[:, a, :],
                                                   ALU.mult, ALU.add).then_inc(added, 1)
                    for a in range(BLOCKS):
                        v.wait_ge(added, 16 * r + BLOCKS + a - 7 if a else 16 * r + BLOCKS)
                        v.scalar_tensor_tensor(Y[:, a, :], Q[:, 2 + a % 2, :], -math.sin(angle(a, j)), Y[:, a, :],
                                               ALU.mult, ALU.add).then_inc(added, 1)

                for n in range(PAIRS):
                    split(n, lambda a: m.H[:, a, :])
                for o in range(ORDERS):
                    for s in range(PAIRS + 2):
                        if s < PAIRS:
                            split(PAIRS * (o + 1) + s, lambda a: m.V[:, 2, a, :])
                        if 1 <= s <= PAIRS:
                            multiply(PAIRS * o + s - 1)
                        if s >= 2:
                            gather(PAIRS * o + s - 2)
                    v.wait_ge(added, 16 * PAIRS * (o + 1))
                    v.tensor_tensor(m.V[:, 2, :, :], Y, m.V[:, o, :, :], ALU.mult).then_inc(updated, 1)
                    v.wait_ge(updated, o + 1)


def hyena_out(nc, d, m):
    banks = (4, 5)
    with ExitStack() as scope:
        sem = lambda n: new_semaphore(nc, m, f"ho_{n}")
        W = scope.enter_context(nc.sbuf_tensor("ho_w", [P, KD, D], F32))
        bias = scope.enter_context(nc.sbuf_tensor("ho_bias", [P, D], F32))
        s = norm_state(nc, m, scope, "ho")
        loaded, step, biased, vturned, vcopied = (sem(n) for n in ("loaded", "step", "biased", "vturned", "vcopied"))
        xl = [sem(f"x{u}") for u in range(4)]
        x = d["x"].rearrange("(i p) d -> p i d", p=P)
        with nc.Block(no_gpsimd_drain=True) as block:
            @block.sync
            def _(sp):
                sp.dma_start(bias[:, :], rows_of(d["hy_b_out"])).then_inc(loaded, 16)
                sp.dma_start(W[:, :, :], chunks(d["hy_w_outT"])).then_inc(loaded, 16)
                for g in range(4):
                    sp.dma_start(m.X[:, 4 * g:4 * g + 4, :], x[:, 4 * g:4 * g + 4, :]).then_inc(xl[g], 16)

            @block.gpsimd
            def _(pool):
                pool.wait_ge(loaded, 32)
                for u in range(UNITS):
                    pool.wait_ge(xl[u // 2], 16)
                    xu = m.X[:, 2 * u:2 * u + 2, :]
                    pool.tensor_tensor(xu, xu, bias[:, :].unsqueeze(1).to_broadcast([P, 2, D]), ALU.add).then_inc(biased, 1)

            @block.tensor
            def _(t):
                def turn(u):
                    if u >= 2:
                        t.wait_ge(vcopied, u - 1)
                    b, a = u // 4, 2 * (u % 4)
                    for k in range(KD):
                        for i in range(2):
                            at = b * D + k * P
                            ins = t.transpose(m.PS[:, 6 + u % 2, (2 * k + i) * P:(2 * k + i + 1) * P],
                                              m.V[:, 2, a + i, at:at + P], m.ident[:, :])
                    ins.then_inc(vturned, 1)

                def project(u):
                    t.wait_ge(vcopied, u + 1)
                    if u >= 4:
                        t.wait_ge(s.summed, u - 3)
                    for i in range(2):
                        for k in range(KD):
                            ins = t.matmul(m.PS[:, u % 4, i * D:(i + 1) * D],
                                           m.XT[:, k, (2 * u + i) * P:(2 * u + i + 1) * P], W[:, k, :],
                                           start=k == 0, stop=k == KD - 1)
                    ins.then_inc(s.out_done, 1)

                t.wait_ge(loaded, 32)
                for u in range(UNITS + 3):
                    if u < UNITS:
                        turn(u)
                    if 1 <= u <= UNITS:
                        project(u - 1)
                    if u >= 3:
                        norm_turn(t, m, s, u - 3, banks)

            @block.scalar
            def _(a):
                for u in range(UNITS + 3):
                    if u < UNITS:
                        a.wait_ge(vturned, u + 1)
                        a.activation(m.XT[:, :, 2 * u * P:(2 * u + 2) * P],
                                     m.PS[:, 6 + u % 2, :].rearrange("p (k t) -> p k t", k=KD),
                                     ACT.Identity).then_inc(vcopied, 1)
                    if 1 <= u <= UNITS:
                        norm_root(a, m, s, u - 1)
                    if 2 <= u <= UNITS + 1:
                        norm_apply(a, m, s, u - 2)
                    if u >= 3:
                        norm_copy(a, m, s, u - 3, banks)

            @block.vector
            def _(v):
                dve = Steps(v, step)
                for u in range(UNITS + 1):
                    if u < UNITS:
                        v.wait_ge(biased, u + 1)
                        norm_sum(v, dve, m, s, u, u % 4)
                    if u >= 1:
                        norm_scale(v, dve, s, u - 1)



def cross_attend(nc, d, m, layer):
    BK = B * KEYS
    tag = f"x{layer}"
    bias_q, bias_k = f"x{layer}_bq", f"x{layer}_bk"
    turn_banks = (6, 7)
    with ExitStack() as scope:
        sem = lambda n: new_semaphore(nc, m, f"{tag}_{n}")
        sb = lambda n, shape: scope.enter_context(nc.sbuf_tensor(f"{tag}_{n}", shape, F32))
        WkT, Wq, ctxT = sb("wkT", [P, KD, D]), sb("wq", [P, KD, D]), sb("ctxT", [P, KD, BK])
        KT, A, bqk, VAL = sb("kT", [P, KD, BK]), sb("a", [P, KD, BK]), sb("bqk", [1, BK]), sb("val", [P, D])
        S, mx, den = sb("s", [P, 2, 4, KEYS]), sb("mx", [P, 2, 4]), sb("den", [P, 2, 4])
        W, WT = sb("w", [P, TILES, BK]), sb("wT", [P, 2, BANK])
        s = norm_state(nc, m, scope, tag)
        loaded, zeroed, step, keys, keyed, folded, ready, scored, shifted, raised, weighted, wturned, wcopied = (
            sem(n) for n in ("loaded", "zeroed", "step", "keys", "keyed", "folded", "ready", "scored", "shifted",
                             "raised", "weighted", "wturned", "wcopied"))
        n_loads = 4
        if layer:
            WvT, bv, beta, table = sb("wvT", [P, KD, D]), sb("bv", [P, D]), sb("beta", [P, 3]), sb("table", [P, TILES, KEYS])
            n_loads = 7
            biased, valued, betas, tabled = sem("biased"), sem("valued"), sem("betas"), sem("tabled")
        with nc.Block(no_gpsimd_drain=True) as block:
            @block.sync
            def _(sp):
                sp.dma_start(WkT[:, :, :], chunks(d[f"wkT{layer}"])).then_inc(loaded, 16)
                sp.dma_start(ctxT[:, :, :], chunks(d["ctxT"])).then_inc(loaded, 16)
                sp.dma_start(Wq[:, :, :], chunks(d[f"wq{layer}"])).then_inc(loaded, 16)
                if layer:
                    sp.dma_start(WvT[:, :, :], chunks(d["wvT"])).then_inc(loaded, 16)
                    sp.dma_start(bv[:, :], rows_of(d["bv"])).then_inc(loaded, 16)
                    sp.dma_start(beta[:, :], rows_of(d["betas"])).then_inc(loaded, 16)
                    sp.dma_start(table[:, :, :], d["table"].rearrange("(i p) n -> p i n", p=P)).then_inc(loaded, 16)
                else:
                    sp.dma_start(VAL[:, :], d["ctx"]).then_inc(loaded, 16)

            @block.gpsimd
            def _(pool):
                pool.memset(W[:, :, :], 0.0).then_inc(zeroed, 1)
                if layer:
                    pool.wait_ge(loaded, 16 * n_loads)
                    pool.tensor_tensor(beta[:, 0:1], beta[:, 0:1], beta[:, 1:2], ALU.add).then_inc(betas, 1)
                    pool.wait_ge(betas, 1)
                    pool.tensor_tensor(beta[:, 0:1], beta[:, 0:1], beta[:, 2:3], ALU.subtract).then_inc(betas, 1)
                    pool.wait_ge(betas, 2)
                    pool.tensor_scalar(table[:, :, :], table[:, :, :], beta[:, 0:1], 0.0, ALU.mult, ALU.add).then_inc(tabled, 1)

            @block.tensor
            def _(t):
                t.wait_ge(loaded, 16 * n_loads)
                for e in range(KD):
                    for k in range(KD):
                        ins = t.matmul(m.PS[:, 0, e * BK:(e + 1) * BK], WkT[:, k, e * P:(e + 1) * P], ctxT[:, k, :],
                                       start=k == 0, stop=k == KD - 1)
                ins.then_inc(keys, 1)
                if layer:
                    for k in range(KD):
                        ins = t.matmul(m.PS[:, 3, 0:D], ctxT[:, k, :], WvT[:, k, :], start=k == 0, stop=k == KD - 1)
                    ins.then_inc(valued, 1)
                t.wait_ge(keyed, KD)
                for k in range(KD):
                    for e in range(KD):
                        t.matmul(m.PS[:, 1, k * BK:(k + 1) * BK], Wq[:, e, k * P:(k + 1) * P], KT[:, e, :],
                                 start=e == 0, stop=e == KD - 1)
                for e in range(KD):
                    ins = t.matmul(m.PS[0:1, 2, 0:BK], col(m, bias_q, e), KT[:, e, :], start=e == 0, stop=e == KD - 1)
                ins.then_inc(folded, 1)

                def scores(g):
                    if g >= 2:
                        t.wait_ge(shifted, g - 1)
                    b = g // 2
                    for i in range(4):
                        out = m.PS[:, g % 2, i * KEYS:(i + 1) * KEYS]
                        at = (4 * g + i) * P
                        for k in range(KD):
                            t.matmul(out, m.XT[:, k, at:at + P], A[:, k, b * KEYS:(b + 1) * KEYS], start=k == 0, stop=False)
                        ins = t.matmul(out, m.ones[0:1, :], bqk[0:1, b * KEYS:(b + 1) * KEYS], start=False, stop=True)
                    ins.then_inc(scored, 1)

                def attend(g):
                    t.wait_ge(weighted, g + 1)
                    if g >= 1:
                        t.wait_ge(wcopied, g)
                    for i in range(4):
                        ins = t.transpose(m.PS[:, 2, i * P:(i + 1) * P], W[:, 4 * g + i, :], m.ident[:, :])
                    ins.then_inc(wturned, 1)
                    t.wait_ge(wcopied, g + 1)
                    for u in (2 * g, 2 * g + 1):
                        if u >= 3:
                            t.wait_ge(s.summed, u - 2)
                        for i in range(2):
                            at = (2 * (u % 2) + i) * P
                            ins = t.matmul(m.PS[:, 3 + u % 3, i * D:(i + 1) * D], WT[:, g % 2, at:at + P], VAL[:, :],
                                           start=True, stop=True)
                        ins.then_inc(s.out_done, 1)

                t.wait_ge(ready, 3)
                if layer:
                    t.wait_ge(biased, 1)
                for g in range(GROUPS + 2):
                    if g < GROUPS:
                        scores(g)
                    if 1 <= g <= GROUPS:
                        attend(g - 1)
                    if g >= 2:
                        for u in (2 * g - 4, 2 * g - 3):
                            norm_turn(t, m, s, u, turn_banks)

            @block.scalar
            def _(a):
                a.wait_ge(keys, 1)
                for e in range(KD):
                    a.activation(KT[:, e, :], m.PS[:, 0, e * BK:(e + 1) * BK], ACT.Identity,
                                 bias=col(m, bias_k, e)).then_inc(keyed, 1)
                a.wait_ge(folded, 1)
                for k in range(KD):
                    a.activation(A[:, k, :], m.PS[:, 1, k * BK:(k + 1) * BK], ACT.Identity).then_inc(ready, 1)
                a.activation(bqk[0:1, :], m.PS[0:1, 2, 0:BK], ACT.Identity).then_inc(ready, 1)
                for g in range(GROUPS + 2):
                    if g < GROUPS:
                        a.wait_ge(shifted, g + 1)
                        a.activation(S[:, g % 2, :, :], S[:, g % 2, :, :], ACT.Exp).then_inc(raised, 1)
                    if 1 <= g <= GROUPS:
                        a.wait_ge(wturned, g)
                        a.activation(WT[:, (g - 1) % 2, :], m.PS[:, 2, :], ACT.Identity).then_inc(wcopied, 1)
                        for u in (2 * g - 2, 2 * g - 1):
                            norm_root(a, m, s, u)
                        for u in (2 * g - 2, 2 * g - 1):
                            norm_apply(a, m, s, u)
                    if g >= 2:
                        for u in (2 * g - 4, 2 * g - 3):
                            norm_copy(a, m, s, u, turn_banks)

            @block.vector
            def _(v):
                dve = Steps(v, step)
                if layer:
                    v.wait_ge(loaded, 16 * n_loads)
                    v.wait_ge(valued, 1)
                    v.tensor_tensor(VAL[:, :], m.PS[:, 3, 0:D], bv[:, :], ALU.add).then_inc(biased, 1)
                    v.wait_ge(tabled, 1)
                v.wait_ge(zeroed, 1)

                def shift(g):
                    v.wait_ge(scored, g + 1)
                    sg = S[:, g % 2, :, :]
                    raw = m.PS[:, g % 2, 0:4 * KEYS].rearrange("p (i n) -> p i n", i=4)
                    if layer:
                        dve.chain(v.scalar_tensor_tensor(sg, raw, float(D) ** -0.5, table[:, 4 * g:4 * g + 4, :],
                                                         ALU.mult, ALU.add))
                        raw = sg
                    dve.chain(v.tensor_reduce(mx[:, g % 2, :], raw, AX.X, ALU.max))
                    v.tensor_tensor(sg, raw, mx[:, g % 2, :].unsqueeze(2).to_broadcast([P, 4, KEYS]),
                                    ALU.subtract).then_inc(shifted, 1)

                def weigh(g):
                    v.wait_ge(raised, g + 1)
                    sg, b = S[:, g % 2, :, :], g // 2
                    dve.chain(v.tensor_reduce(den[:, g % 2, :], sg, AX.X, ALU.add))
                    dve.chain(v.reciprocal(den[:, g % 2, :], den[:, g % 2, :]))
                    v.tensor_tensor(W[:, 4 * g:4 * g + 4, b * KEYS:(b + 1) * KEYS], sg,
                                    den[:, g % 2, :].unsqueeze(2).to_broadcast([P, 4, KEYS]), ALU.mult).then_inc(weighted, 1)

                for g in range(GROUPS + 1):
                    if g < GROUPS:
                        shift(g)
                    if g >= 1:
                        for u in (2 * g - 2, 2 * g - 1):
                            norm_sum(v, dve, m, s, u, 3 + u % 3)
                    if g < GROUPS:
                        weigh(g)
                    if g >= 1:
                        for u in (2 * g - 2, 2 * g - 1):
                            norm_scale(v, dve, s, u)


def cross_attend_0(nc, d, m):
    cross_attend(nc, d, m, 0)


def cross_attend_1(nc, d, m):
    cross_attend(nc, d, m, 1)



def slot_mixer(nc, d, m):
    with ExitStack() as scope:
        m.AL = scope.enter_context(nc.sbuf_tensor("AL", [P, TILES, B * SLOTS], F32))
        m.AT = scope.enter_context(nc.sbuf_tensor("AT", [P, TOK], F32))
        m.SO = scope.enter_context(nc.sbuf_tensor("SO", [P, D], F32))
        for part in SLOT_PARTS:
            part(nc, d, m)


def slot_route(nc, d, m):
    with ExitStack() as scope:
        sem = lambda n: new_semaphore(nc, m, f"sr_{n}")
        sb = lambda n, shape: scope.enter_context(nc.sbuf_tensor(f"sr_{n}", shape, F32))
        w1, w1m, w2, b2 = sb("w1", [P, KD, P]), sb("w1m", [P, KD, P]), sb("w2", [P, SLOTS]), sb("b2", [P, SLOTS])
        slots, tau, mean, bias = sb("slots", [SLOTS, D]), sb("tau", [P, 1]), sb("mean", [P, KD]), sb("bias", [P, 1])
        h, lg, rest = sb("h", [P, 2, BANK]), sb("lg", [P, 2, 4, SLOTS]), sb("rest", [P, 2, 4, SLOTS])
        top, ex, den = sb("top", [P, 2, 4, 8]), sb("ex", [P, 2, 4, SLOTS]), sb("den", [P, 2, 4])
        loaded, zeroed, step, summed, meaned, biasing, biased, hidden, active, routed, shifted, raised, weighted, turned, copied = (
            sem(n) for n in ("loaded", "zeroed", "step", "summed", "meaned", "biasing", "biased", "hidden", "active",
                             "routed", "shifted", "raised", "weighted", "turned", "copied"))
        tau_step = sem("tau")
        with nc.Block(no_gpsimd_drain=True) as block:
            @block.sync
            def _(sp):
                for dst, src in ((w1m[:, :, :], chunks(d["f_w1"][D:2 * D, :])), (w1[:, :, :], chunks(d["f_w1"][0:D, :])),
                                 (slots[:, :], d["slots2"][0:SLOTS, :]), (w2[:, :], d["f_w2"]), (b2[:, :], rows_of(d["f_b2"])),
                                 (tau[:, :], rows_of(d["f_tau"]))):
                    sp.dma_start(dst, src).then_inc(loaded, 16)

            @block.gpsimd
            def _(pool):
                pool.memset(m.AL[:, :, :], 0.0).then_inc(zeroed, 1)

            @block.tensor
            def _(t):
                t.wait_ge(loaded, 96)
                for k in range(KD):
                    ins = t.matmul(m.PS[:, 5, k:k + 1], slots[:, k * P:(k + 1) * P], m.ones[0:SLOTS, 0:1], start=True, stop=True)
                ins.then_inc(summed, 1)
                t.wait_ge(meaned, 1)
                for k in range(KD):
                    ins = t.matmul(m.PS[:, 4, 0:1], w1m[:, k, :], mean[:, k:k + 1], start=k == 0, stop=k == KD - 1)
                ins.then_inc(biasing, 1)

                def hide(g):
                    if g >= 2:
                        t.wait_ge(active, g - 1)
                    for k in range(KD):
                        ins = t.matmul(m.PS[:, g % 2, :], w1[:, k, :], m.XT[:, k, g * BANK:(g + 1) * BANK],
                                       start=k == 0, stop=k == KD - 1)
                    ins.then_inc(hidden, 1)

                def route(g):
                    t.wait_ge(active, g + 1)
                    if g >= 2:
                        t.wait_ge(step, R_STEPS * (g - 2) + 1)
                    for i in range(4):
                        ins = t.matmul(m.PS[:, 2 + g % 2, i * SLOTS:(i + 1) * SLOTS], h[:, g % 2, i * P:(i + 1) * P],
                                       w2[:, :], start=True, stop=True)
                    ins.then_inc(routed, 1)

                def collect(g):
                    t.wait_ge(weighted, g + 1)
                    if g >= 1:
                        t.wait_ge(copied, g)
                    else:
                        t.wait_ge(biased, 1)
                    for i in range(4):
                        ins = t.transpose(m.PS[:, 4, i * P:(i + 1) * P], m.AL[:, 4 * g + i, :], m.ident[:, :])
                    ins.then_inc(turned, 1)
                    for i in range(4 * g, 4 * g + 4):
                        first, last = i == 0, i == TILES - 1
                        t.matmul(m.PS[:, 6, 0:D], m.AL[:, i, :], m.X[:, i, :], start=first, stop=last)
                        t.matmul(m.PS[:, 7, 0:1], m.AL[:, i, :], m.ones[:, 0:1], start=first, stop=last)

                for g in range(GROUPS + 2):
                    if g < GROUPS:
                        hide(g)
                    if 1 <= g <= GROUPS:
                        route(g - 1)
                    if g >= 2:
                        collect(g - 2)

            @block.scalar
            def _(a):
                a.wait_ge(loaded, 96)
                a.activation(tau[:, :], tau[:, :], ACT.Abs).then_inc(tau_step, 1)
                a.wait_ge(summed, 1)
                a.activation(mean[:, :], m.PS[:, 5, 0:KD], ACT.Copy, scale=1.0 / SLOTS).then_inc(meaned, 1)
                a.wait_ge(biasing, 1)
                a.activation(bias[:, :], m.PS[:, 4, 0:1], ACT.Identity, bias=col(m, "f_b1")).then_inc(biased, 1)
                a.wait_ge(biased, 1)
                for g in range(GROUPS + 2):
                    if g < GROUPS:
                        a.wait_ge(hidden, g + 1)
                        if g >= 2:
                            a.wait_ge(routed, g - 1)
                        a.activation(h[:, g % 2, :], m.PS[:, g % 2, :], ACT.Gelu, bias=bias[:, 0:1]).then_inc(active, 1)
                    if 1 <= g <= GROUPS:
                        a.wait_ge(shifted, g)
                        e = ex[:, (g - 1) % 2, :, :]
                        a.activation(e, e, ACT.Exp).then_inc(raised, 1)
                    if g >= 2:
                        a.wait_ge(turned, g - 1)
                        a.activation(m.AT[:, (g - 2) * BANK:(g - 1) * BANK], m.PS[:, 4, :], ACT.Identity).then_inc(copied, 1)

            @block.vector
            def _(v):
                dve = Steps(v, step)
                v.wait_ge(loaded, 96)
                v.wait_ge(zeroed, 1)
                v.wait_ge(tau_step, 1)
                v.tensor_scalar(tau[:, :], tau[:, :], 0.1, None, ALU.add).then_inc(tau_step, 1)
                v.wait_ge(tau_step, 2)
                v.reciprocal(tau[:, :], tau[:, :]).then_inc(tau_step, 1)
                v.wait_ge(tau_step, 3)

                def pick(g):
                    v.wait_ge(routed, g + 1)
                    q, before = g % 2, dve.n
                    wide = lambda x: x.unsqueeze(2).to_broadcast([P, 4, SLOTS])
                    dve.chain(v.tensor_tensor(lg[:, q, :, :], m.PS[:, 2 + q, 0:4 * SLOTS].rearrange("p (i n) -> p i n", i=4),
                                              b2[:, :].unsqueeze(1).to_broadcast([P, 4, SLOTS]), ALU.add))
                    dve.chain(v.tensor_scalar(lg[:, q, :, :], lg[:, q, :, :], tau[:, 0:1], None, ALU.mult))
                    for i in range(4):
                        dve.mark(v.max(top[:, q, i, :], lg[:, q, i, :]))
                    dve.wait()
                    v.tensor_tensor(ex[:, q, :, :], lg[:, q, :, :], wide(top[:, q, :, 0]), ALU.subtract).then_inc(shifted, 1)
                    for i in range(4):
                        dve.mark(v.match_replace(rest[:, q, i, :], top[:, q, i, :], lg[:, q, i, :], LOW))
                    dve.wait()
                    dve.chain(v.tensor_tensor(rest[:, q, :, :], rest[:, q, :, :], lg[:, q, :, :], ALU.not_equal))
                    v.wait_ge(raised, g + 1)
                    dve.chain(v.tensor_tensor(ex[:, q, :, :], ex[:, q, :, :], rest[:, q, :, :], ALU.mult))
                    dve.chain(v.tensor_reduce(den[:, q, :], ex[:, q, :, :], AX.X, ALU.add))
                    dve.chain(v.reciprocal(den[:, q, :], den[:, q, :]))
                    b = g // 2
                    v.tensor_tensor(m.AL[:, 4 * g:4 * g + 4, b * SLOTS:(b + 1) * SLOTS], ex[:, q, :, :], wide(den[:, q, :]),
                                    ALU.mult).then_inc(weighted, 1)
                    assert dve.n - before == R_STEPS

                for g in range(GROUPS):
                    pick(g)


R_STEPS = 14


def slot_update(nc, d, m):
    R = B * SLOTS
    with ExitStack() as scope:
        sem = lambda n: new_semaphore(nc, m, f"su_{n}")
        sb = lambda n, shape: scope.enter_context(nc.sbuf_tensor(f"su_{n}", shape, F32))
        WihT, WhhT, slots, slotsT = sb("wih", [P, KD, 3 * D]), sb("whh", [P, KD, 3 * D]), sb("slots", [P, D]), sb("slotsT", [P, KD, R])
        bih, bhh = sb("bih", [P, 3 * D]), sb("bhh", [P, 3 * D])
        wq, wk, wv, wvp, wo = sb("wq", [P, KD, 64]), sb("wk", [P, KD, 64]), sb("wv", [P, KD, D]), sb("wvp", [P, KD, D]), sb("wo", [P, KD, D])
        bv, ln_g, ln_b, bvp, bo = (sb(n, [P, D]) for n in ("bv", "ln_g", "ln_b", "bvp", "bo"))
        den, si, siT, rz, hn, new, newT = sb("den", [P, 1]), sb("si", [P, D]), sb("siT", [P, KD, R]), sb("rz", [P, 2 * D]), sb("hn", [P, D]), sb("new", [P, D]), sb("newT", [P, KD, R])
        qT, kT, val, mx, ex, sm = sb("qT", [64, R]), sb("kT", [64, R]), sb("val", [P, D]), sb("mx", [P, 1]), sb("ex", [P, SLOTS]), sb("sm", [P, 1])
        AB, ABT, y, st, mv, std = sb("ab", [P, R]), sb("abT", [P, R]), sb("y", [P, D]), sb("st", [P, 6]), sb("mv", [P, 2]), sb("std", [P, 1])
        yT, sv, svT = sb("yT", [P, KD, R]), sb("sv", [P, D]), sb("svT", [P, KD, R])
        loaded, step, zeroed, bo_added = sem("loaded"), sem("step"), sem("zeroed"), sem("bo_added")
        names = ("si", "si_turned", "siT", "gates", "rz_in", "rz", "cell_in", "cell", "new", "new_turned", "newT", "qkv",
                 "qk", "val", "scores", "top", "exps", "ab", "ab_turned", "abT", "comm", "stats", "root", "y",
                 "y_turned", "yT", "values", "sv", "sv_turned", "svT", "out")
        made = {n: sem(n) for n in names}
        loads = ((slotsT[:, :, :], chunks(d["slotsT2"])), (WhhT[:, :, :], chunks(d["f_whhT"])), (WihT[:, :, :], chunks(d["f_wihT"])),
                 (bih[:, :], rows_of(d["f_bih"])), (bhh[:, :], rows_of(d["f_bhh"])), (slots[:, :], d["slots2"]),
                 (wq[:, :, :], chunks(d["f_wq"])), (wk[:, :, :], chunks(d["f_wk"])), (wv[:, :, :], chunks(d["f_wv"])),
                 (bv[:, :], rows_of(d["f_bv"])), (ln_g[:, :], rows_of(d["f_ln_g"])), (ln_b[:, :], rows_of(d["f_ln_b"])),
                 (wvp[:, :, :], chunks(d["f_wvp"])), (bvp[:, :], rows_of(d["f_bvp"])), (wo[:, :, :], chunks(d["f_wo"])),
                 (bo[:, :], rows_of(d["f_bo"])))
        with nc.Block(no_gpsimd_drain=True) as block:
            @block.sync
            def _(sp):
                for dst, src in loads:
                    sp.dma_start(dst, src).then_inc(loaded, 16)

            @block.gpsimd
            def _(pool):
                pool.memset(AB[:, :], 0.0).then_inc(zeroed, 1)
                pool.wait_ge(loaded, 16 * len(loads))
                pool.tensor_tensor(m.X[:, :, :], m.X[:, :, :], bo[:, :].unsqueeze(1).to_broadcast([P, TILES, D]),
                                   ALU.add).then_inc(bo_added, 1)

            @block.tensor
            def _(t):
                def turn(src, bank, done):
                    for k in range(KD):
                        ins = t.transpose(m.PS[:, bank, k * R:(k + 1) * R], src[:, k * P:(k + 1) * P], m.ident[:, :])
                    ins.then_inc(done, 1)

                t.wait_ge(loaded, 16 * len(loads))
                for k in range(KD):
                    t.matmul(m.PS[:, 3, 0:D], slotsT[:, k, :], WhhT[:, k, 2 * D:3 * D], start=k == 0, stop=k == KD - 1)
                for k in range(KD):
                    t.matmul(m.PS[:, 1, :], slotsT[:, k, :], WhhT[:, k, 0:2 * D], start=k == 0, stop=False)
                t.wait_ge(made["si"], 1)
                turn(si, 0, made["si_turned"])
                t.wait_ge(made["siT"], 1)
                for k in range(KD):
                    t.matmul(m.PS[:, 1, :], siT[:, k, :], WihT[:, k, 0:2 * D], start=False, stop=k == KD - 1)
                for k in range(KD):
                    ins = t.matmul(m.PS[:, 2, 0:D], siT[:, k, :], WihT[:, k, 2 * D:3 * D], start=k == 0, stop=k == KD - 1)
                ins.then_inc(made["gates"], 1)
                t.wait_ge(made["new"], 1)
                turn(new, 4, made["new_turned"])
                t.wait_ge(made["newT"], 1)
                for n, w in enumerate((wq, wk)):
                    for k in range(KD):
                        t.matmul(m.PS[0:64, 5, n * R:(n + 1) * R], w[:, k, :], newT[:, k, :], start=k == 0, stop=k == KD - 1)
                for k in range(KD):
                    ins = t.matmul(m.PS[:, 2, 0:D], newT[:, k, :], wv[:, k, :], start=k == 0, stop=k == KD - 1)
                ins.then_inc(made["qkv"], 1)
                t.wait_ge(made["qk"], 2)
                for b in range(B):
                    part = slice(b * SLOTS, (b + 1) * SLOTS)
                    ins = t.matmul(m.PS[part, 3, 0:SLOTS], qT[:, part], kT[:, part], start=True, stop=True)
                ins.then_inc(made["scores"], 1)
                t.wait_ge(made["ab"], 2)
                t.transpose(m.PS[:, 0, 0:R], AB[:, :], m.ident[:, :]).then_inc(made["ab_turned"], 1)
                t.wait_ge(made["abT"], 1)
                t.wait_ge(made["val"], 1)
                t.matmul(m.PS[:, 1, 0:D], ABT[:, :], val[:, :], start=True, stop=True).then_inc(made["comm"], 1)
                t.wait_ge(made["y"], 1)
                turn(y, 4, made["y_turned"])
                t.wait_ge(made["yT"], 1)
                for k in range(KD):
                    ins = t.matmul(m.PS[:, 2, 0:D], yT[:, k, :], wvp[:, k, :], start=k == 0, stop=k == KD - 1)
                ins.then_inc(made["values"], 1)
                t.wait_ge(made["sv"], 1)
                turn(sv, 5, made["sv_turned"])
                t.wait_ge(made["svT"], 1)
                for k in range(KD):
                    ins = t.matmul(m.PS[:, 3, 0:D], svT[:, k, :], wo[:, k, :], start=k == 0, stop=k == KD - 1)
                ins.then_inc(made["out"], 1)

            @block.scalar
            def _(a):
                def copy_turned(dst, bank, turned, done):
                    a.wait_ge(turned, 1)
                    a.activation(dst, m.PS[:, bank, 0:KD * R].rearrange("p (k r) -> p k r", k=KD), ACT.Identity).then_inc(done, 1)

                copy_turned(siT[:, :, :], 0, made["si_turned"], made["siT"])
                a.wait_ge(made["rz_in"], 1)
                a.activation(rz[:, :], rz[:, :], ACT.Sigmoid).then_inc(made["rz"], 1)
                a.wait_ge(made["cell_in"], 1)
                a.activation(hn[:, :], hn[:, :], ACT.Tanh).then_inc(made["cell"], 1)
                copy_turned(newT[:, :, :], 4, made["new_turned"], made["newT"])
                a.wait_ge(made["qkv"], 1)
                for n, (dst, bias) in enumerate(((qT, "f_bq"), (kT, "f_bk"))):
                    a.activation(dst[:, :], m.PS[0:64, 5, n * R:(n + 1) * R], ACT.Identity, bias=col(m, bias, 0, 64)).then_inc(made["qk"], 1)
                a.wait_ge(made["top"], 1)
                a.activation(ex[:, :], m.PS[:, 3, 0:SLOTS], ACT.Exp, bias=mx[:, 0:1], scale=0.125, accum_out=sm[:, 0:1]).then_inc(made["exps"], 1)
                a.wait_ge(made["ab_turned"], 1)
                a.activation(ABT[:, :], m.PS[:, 0, 0:R], ACT.Identity).then_inc(made["abT"], 1)
                a.wait_ge(made["stats"], 1)
                a.activation(std[:, :], mv[:, 1:2], ACT.Sqrt, bias=m.eps[:, 0:1]).then_inc(made["root"], 1)
                copy_turned(yT[:, :, :], 4, made["y_turned"], made["yT"])
                copy_turned(svT[:, :, :], 5, made["sv_turned"], made["svT"])

            @block.vector
            def _(v):
                dve = Steps(v, step)
                tt = v.tensor_tensor
                dve.chain(v.tensor_scalar(den[:, :], m.PS[:, 7, 0:1], 1e-8, None, ALU.add))
                dve.chain(v.reciprocal(den[:, :], den[:, :]))
                v.tensor_scalar(si[:, :], m.PS[:, 6, 0:D], den[:, 0:1], None, ALU.mult).then_inc(made["si"], 1)
                v.wait_ge(loaded, 16 * len(loads))
                dve.chain(tt(bih[:, 0:2 * D], bih[:, 0:2 * D], bhh[:, 0:2 * D], ALU.add))
                v.wait_ge(made["gates"], 1)
                tt(rz[:, :], m.PS[:, 1, :], bih[:, 0:2 * D], ALU.add).then_inc(made["rz_in"], 1)
                dve.mark(tt(hn[:, :], m.PS[:, 3, 0:D], bhh[:, 2 * D:3 * D], ALU.add))
                dve.chain(tt(y[:, :], m.PS[:, 2, 0:D], bih[:, 2 * D:3 * D], ALU.add))
                v.wait_ge(made["rz"], 1)
                dve.chain(tt(hn[:, :], hn[:, :], rz[:, 0:D], ALU.mult))
                tt(hn[:, :], hn[:, :], y[:, :], ALU.add).then_inc(made["cell_in"], 1)
                v.wait_ge(made["cell"], 1)
                dve.chain(tt(new[:, :], slots[:, :], hn[:, :], ALU.subtract))
                dve.chain(tt(new[:, :], new[:, :], rz[:, D:2 * D], ALU.mult))
                tt(new[:, :], new[:, :], hn[:, :], ALU.add).then_inc(made["new"], 1)
                v.wait_ge(made["qkv"], 1)
                tt(val[:, :], m.PS[:, 2, 0:D], bv[:, :], ALU.add).then_inc(made["val"], 1)
                v.wait_ge(made["scores"], 1)
                dve.chain(v.tensor_reduce(mx[:, :], m.PS[:, 3, 0:SLOTS], AX.X, ALU.max))
                v.tensor_scalar(mx[:, :], mx[:, :], -0.125, None, ALU.mult).then_inc(made["top"], 1)
                v.wait_ge(made["exps"], 1)
                v.wait_ge(zeroed, 1)
                dve.chain(v.reciprocal(sm[:, :], sm[:, :]))
                for b in range(B):
                    part = slice(b * SLOTS, (b + 1) * SLOTS)
                    v.tensor_scalar(AB[part, part], ex[part, :], sm[part, 0:1], None, ALU.mult).then_inc(made["ab"], 1)
                v.wait_ge(made["comm"], 1)
                v.wait_ge(made["new"], 1)
                dve.chain(tt(y[:, :], m.PS[:, 1, 0:D], new[:, :], ALU.add))
                dve.chain(v.bn_stats(st[:, :], y[:, :]))
                v.bn_aggr(mv[:, :], st[:, :]).then_inc(made["stats"], 1)
                v.wait_ge(made["root"], 1)
                dve.chain(v.reciprocal(std[:, :], std[:, :]))
                v.wait_ge(made["stats"], 1)
                dve.chain(v.tensor_scalar(y[:, :], y[:, :], mv[:, 0:1], std[:, 0:1], ALU.subtract, ALU.mult))
                dve.chain(tt(y[:, :], y[:, :], ln_g[:, :], ALU.mult))
                tt(y[:, :], y[:, :], ln_b[:, :], ALU.add).then_inc(made["y"], 1)
                v.wait_ge(made["values"], 1)
                tt(sv[:, :], m.PS[:, 2, 0:D], bvp[:, :], ALU.add).then_inc(made["sv"], 1)
                v.wait_ge(bo_added, 1)
                v.wait_ge(made["out"], 1)
                v.tensor_copy(m.SO[:, :], m.PS[:, 3, 0:D])


def slot_out(nc, d, m):
    banks = (4, 5)
    with ExitStack() as scope:
        s = norm_state(nc, m, scope, "so")
        step = new_semaphore(nc, m, "so_step")
        with nc.Block(no_gpsimd_drain=True) as block:
            @block.tensor
            def _(t):
                for u in range(UNITS + 2):
                    if u < UNITS:
                        if u >= 4:
                            t.wait_ge(s.summed, u - 3)
                        for i in range(2):
                            at = (2 * u + i) * P
                            ins = t.matmul(m.PS[:, u % 4, i * D:(i + 1) * D], m.AT[:, at:at + P], m.SO[:, :], start=True, stop=True)
                        ins.then_inc(s.out_done, 1)
                    if u >= 2:
                        norm_turn(t, m, s, u - 2, banks)

            @block.scalar
            def _(a):
                norm_scalar_side(a, m, s, banks)

            @block.vector
            def _(v):
                norm_vector_side(v, Steps(v, step), m, s)


SLOT_PARTS = [slot_route, slot_update, slot_out]


def norm_scalar_side(a, m, s, banks):
    for u in range(UNITS + 2):
        if u < UNITS:
            norm_root(a, m, s, u)
        if 1 <= u <= UNITS:
            norm_apply(a, m, s, u - 1)
        if u >= 2:
            norm_copy(a, m, s, u - 2, banks)


def norm_vector_side(v, dve, m, s):
    for u in range(UNITS + 1):
        if u < UNITS:
            norm_sum(v, dve, m, s, u, u % 4)
        if u >= 1:
            norm_scale(v, dve, s, u - 1)



def axis_attend(nc, d, m):
    J = TILES // B
    with ExitStack() as outer:
        OT = outer.enter_context(nc.sbuf_tensor("OT", [P, KD, TOK], F32))
        with ExitStack() as scope:
            sem = lambda n: new_semaphore(nc, m, f"aa_{n}")
            sb = lambda n, shape: scope.enter_context(nc.sbuf_tensor(f"aa_{n}", shape, F32))
            W, bias = sb("w", [P, KD, 3 * D]), sb("bias", [P, 3 * D])
            qk, val = sb("qk", [P, 2, B, 2 * D]), sb("val", [P, 2, B, D])
            prod, S, mx, den = sb("prod", [P, 2, B, B, D]), sb("s", [P, 2, B, B, HEADS]), sb("mx", [P, 2, B, HEADS]), sb("den", [P, 2, B, HEADS])
            pv, out = sb("pv", [P, B, B, D]), sb("out", [P, 2, B, D])
            loaded, step, projected, biased, shifted, raised, weighted, mixed, attended, turned, copied = (sem(n) for n in (
                "loaded", "step", "projected", "biased", "shifted", "raised", "weighted", "mixed", "attended", "turned", "copied"))
            OTv = OT[:, :, :].rearrange("p k (s j t) -> p k s j t", s=B, j=J)
            with nc.Block(no_gpsimd_drain=True) as block:
                @block.sync
                def _(sp):
                    sp.dma_start(W[:, :, :], chunks(d["a_inT"])).then_inc(loaded, 16)
                    sp.dma_start(bias[:, :], rows_of(d["a_in_b"])).then_inc(loaded, 16)

                @block.tensor
                def _(t):
                    def project(j):
                        if j >= 2:
                            t.wait_ge(biased, 3 * (j - 1))
                        at = 3 * (j % 2)
                        for s in range(B):
                            tile = (j + J * s) * P
                            for k in range(KD):
                                t.matmul(m.PS[:, at + s, :], m.XT[:, k, tile:tile + P], W[:, k, 0:2 * D], start=k == 0, stop=k == KD - 1)
                            for k in range(KD):
                                ins = t.matmul(m.PS[:, at + 2, s * D:(s + 1) * D], m.XT[:, k, tile:tile + P], W[:, k, 2 * D:3 * D],
                                               start=k == 0, stop=k == KD - 1)
                        ins.then_inc(projected, 1)

                    def turn(j):
                        t.wait_ge(attended, j + 1)
                        if j >= 2:
                            t.wait_ge(copied, j - 1)
                        for k in range(KD):
                            for s in range(B):
                                ins = t.transpose(m.PS[:, 6 + j % 2, (2 * k + s) * P:(2 * k + s + 1) * P],
                                                  out[:, j % 2, s, k * P:(k + 1) * P], m.ident[:, :])
                        ins.then_inc(turned, 1)

                    t.wait_ge(loaded, 32)
                    for j in range(J + 2):
                        if j < J:
                            project(j)
                        if j >= 2:
                            turn(j - 2)

                @block.scalar
                def _(a):
                    for j in range(J + 2):
                        if j < J:
                            a.wait_ge(shifted, j + 1)
                            a.activation(S[:, j % 2], S[:, j % 2], ACT.Exp, scale=float(HD) ** -0.5).then_inc(raised, 1)
                        if j >= 2:
                            a.wait_ge(turned, j - 1)
                            a.activation(OTv[:, :, :, j - 2, :], m.PS[:, 6 + j % 2, :].rearrange("p (k s t) -> p k s t", k=KD, s=B),
                                         ACT.Identity).then_inc(copied, 1)

                @block.gpsimd
                def _(pool):
                    for j in range(J):
                        pool.wait_ge(weighted, j + 1)
                        if j >= 1:
                            pool.wait_ge(attended, j)
                        for s in range(B):
                            pool.tensor_tensor(pv[:, s, :, :].rearrange("p t (h c) -> p t h c", h=HEADS),
                                               S[:, j % 2, s, :, :].unsqueeze(3).to_broadcast([P, B, HEADS, HD]),
                                               val[:, j % 2, :, :].rearrange("p t (h c) -> p t h c", h=HEADS), ALU.mult).then_inc(mixed, 1)
                        pool.wait_ge(mixed, 2 * (j + 1))
                        if j >= 2:
                            pool.wait_ge(turned, j - 1)
                        pool.tensor_tensor(out[:, j % 2], pv[:, :, 0, :], pv[:, :, 1, :], ALU.add).then_inc(attended, 1)

                @block.vector
                def _(v):
                    dve = Steps(v, step)
                    v.wait_ge(loaded, 32)

                    def score(j):
                        q = j % 2
                        v.wait_ge(projected, j + 1)
                        if j >= 2:
                            v.wait_ge(attended, j - 1)
                        v.tensor_tensor(qk[:, q, :, :], m.PS[:, 3 * q:3 * q + 2, :],
                                        bias[:, 0:2 * D].unsqueeze(1).to_broadcast([P, B, 2 * D]), ALU.add).then_inc(biased, 2)
                        v.tensor_tensor(val[:, q, :, :], m.PS[:, 3 * q + 2, :].rearrange("p (s n) -> p s n", s=B),
                                        bias[:, 2 * D:].unsqueeze(1).to_broadcast([P, B, D]), ALU.add).then_inc(biased, 1)
                        v.wait_ge(biased, 3 * (j + 1))
                        for s in range(B):
                            dve.mark(v.tensor_tensor(prod[:, q, s, :, :], qk[:, q, s, 0:D].unsqueeze(1).to_broadcast([P, B, D]),
                                                     qk[:, q, :, D:2 * D], ALU.mult))
                        dve.wait()
                        dve.chain(v.tensor_reduce(S[:, q].rearrange("p s t h -> p (s t h)"),
                                                  prod[:, q].rearrange("p s t (h c) -> p (s t h) c", h=HEADS), AX.X, ALU.add))
                        dve.chain(v.tensor_tensor(mx[:, q, :, :], S[:, q, :, 0, :], S[:, q, :, 1, :], ALU.max))
                        v.tensor_tensor(S[:, q], S[:, q], mx[:, q, :, :].unsqueeze(2).to_broadcast([P, B, B, HEADS]),
                                        ALU.subtract).then_inc(shifted, 1)

                    def weigh(j):
                        q = j % 2
                        v.wait_ge(raised, j + 1)
                        dve.chain(v.tensor_tensor(den[:, q, :, :], S[:, q, :, 0, :], S[:, q, :, 1, :], ALU.add))
                        dve.chain(v.reciprocal(den[:, q, :, :], den[:, q, :, :]))
                        v.tensor_tensor(S[:, q], S[:, q], den[:, q, :, :].unsqueeze(2).to_broadcast([P, B, B, HEADS]),
                                        ALU.mult).then_inc(weighted, 1)

                    for j in range(J + 1):
                        if j < J:
                            score(j)
                        if j >= 1:
                            weigh(j - 1)
        axis_out(nc, d, m, OT)


def axis_out(nc, d, m, OT):
    banks = (4, 5)
    with ExitStack() as scope:
        sem = lambda n: new_semaphore(nc, m, f"ao_{n}")
        W = scope.enter_context(nc.sbuf_tensor("ao_w", [P, KD, D], F32))
        bias = scope.enter_context(nc.sbuf_tensor("ao_bias", [P, D], F32))
        s = norm_state(nc, m, scope, "ao")
        loaded, step, biased = sem("loaded"), sem("step"), sem("biased")
        with nc.Block(no_gpsimd_drain=True) as block:
            @block.sync
            def _(sp):
                sp.dma_start(bias[:, :], rows_of(d["a_out_b"])).then_inc(loaded, 16)
                sp.dma_start(W[:, :, :], chunks(d["a_outT"])).then_inc(loaded, 16)

            @block.gpsimd
            def _(pool):
                pool.wait_ge(loaded, 32)
                for u in range(UNITS):
                    xu = m.X[:, 2 * u:2 * u + 2, :]
                    pool.tensor_tensor(xu, xu, bias[:, :].unsqueeze(1).to_broadcast([P, 2, D]), ALU.add).then_inc(biased, 1)

            @block.tensor
            def _(t):
                t.wait_ge(loaded, 32)
                for u in range(UNITS + 2):
                    if u < UNITS:
                        if u >= 4:
                            t.wait_ge(s.summed, u - 3)
                        for i in range(2):
                            at = (2 * u + i) * P
                            for k in range(KD):
                                ins = t.matmul(m.PS[:, u % 4, i * D:(i + 1) * D], OT[:, k, at:at + P], W[:, k, :],
                                               start=k == 0, stop=k == KD - 1)
                        ins.then_inc(s.out_done, 1)
                    if u >= 2:
                        norm_turn(t, m, s, u - 2, banks)

            @block.scalar
            def _(a):
                norm_scalar_side(a, m, s, banks)

            @block.vector
            def _(v):
                dve = Steps(v, step)
                for u in range(UNITS + 1):
                    if u < UNITS:
                        v.wait_ge(biased, u + 1)
                        norm_sum(v, dve, m, s, u, u % 4)
                    if u >= 1:
                        norm_scale(v, dve, s, u - 1)



def expert_route(nc, d, m):
    GS = EXPERTS // GROUPS_E
    with ExitStack() as scope:
        sem = lambda n: new_semaphore(nc, m, f"er_{n}")
        sb = lambda n, shape: scope.enter_context(nc.sbuf_tensor(f"er_{n}", shape, F32))
        gate, ebias = sb("gate", [P, KD, EXPERTS]), sb("ebias", [P, EXPERTS])
        score, biased_score = sb("score", [P, TILES, EXPERTS]), sb("biased", [P, TILES, EXPERTS])
        group, group_rest, group_top = sb("group", [P, TILES, 12]), sb("group_rest", [P, TILES, 12]), sb("group_top", [P, TILES, 8])
        masked, rest, top, den = sb("masked", [P, TILES, EXPERTS + 2]), sb("rest", [P, TILES, EXPERTS + 2]), sb("top", [P, TILES, 8]), sb("den", [P, TILES])
        loaded, step, logits, scored = sem("loaded"), sem("step"), sem("logits"), sem("scored")
        x_high, x_low = sem("x_high"), sem("x_low")
        with nc.Block(no_gpsimd_drain=True) as block:
            @block.gpsimd
            def _(pool):
                for g in range(GROUPS):
                    part = slice(g * BANK, (g + 1) * BANK)
                    pool.wait_ge(x_high, g + 1)
                    pool.tensor_tensor(m.XS[1][:, :, part], m.XT[:, :, part], m.XS[0][:, :, part].bitcast(F32),
                                       ALU.subtract).then_inc(x_low, 1)

            @block.sync
            def _(sp):
                sp.dma_start(gate[:, :, :], chunks(d["gateT"])).then_inc(loaded, 16)
                sp.dma_start(ebias[:, :], rows_of(d["e_bias"])).then_inc(loaded, 16)

            @block.tensor
            def _(t):
                t.wait_ge(loaded, 32)
                for i in range(TILES):
                    for k in range(KD):
                        ins = t.matmul(m.PS[:, 0, i * EXPERTS:(i + 1) * EXPERTS], m.XT[:, k, i * P:(i + 1) * P], gate[:, k, :],
                                       start=k == 0, stop=k == KD - 1)
                ins.then_inc(logits, 1)

            @block.scalar
            def _(a):
                for g in range(GROUPS):
                    part = slice(g * BANK, (g + 1) * BANK)
                    a.activation(m.XS[0][:, :, part], m.XT[:, :, part], ACT.Copy).then_inc(x_high, 1)
                a.wait_ge(logits, 1)
                a.activation(score[:, :, :], m.PS[:, 0, :].rearrange("p (i e) -> p i e", i=TILES), ACT.Sigmoid).then_inc(scored, 1)

            @block.vector
            def _(v):
                dve = Steps(v, step)
                v.memset(m.C[:, :, EXPERTS:ALL_E], 1.0)
                dve.mark(v.memset(group[:, :, GROUPS_E:12], LOW))
                dve.mark(v.memset(masked[:, :, EXPERTS:EXPERTS + 2], LOW))
                v.wait_ge(loaded, 32)
                v.wait_ge(scored, 1)
                dve.chain(v.tensor_tensor(biased_score[:, :, :], score[:, :, :],
                                          ebias[:, :].unsqueeze(1).to_broadcast([P, TILES, EXPERTS]), ALU.add))
                dve.chain(v.tensor_reduce(group[:, :, 0:GROUPS_E], biased_score[:, :, :].rearrange("p i (g e) -> p i g e", g=GROUPS_E),
                                          AX.X, ALU.max))
                for i in range(TILES):
                    dve.mark(v.max(group_top[:, i, :], group[:, i, 0:GROUPS_E]))
                dve.wait()
                dve.chain(v.memset(group_top[:, :, TOP_GROUPS:8], LOW))
                for i in range(TILES):
                    dve.mark(v.match_replace(group_rest[:, i, :], group_top[:, i, :], group[:, i, :], HIGH))
                dve.wait()
                dve.chain(v.tensor_tensor(group_rest[:, :, :], group_rest[:, :, :], group[:, :, :], ALU.not_equal))
                dve.chain(v.tensor_tensor(masked[:, :, 0:EXPERTS].rearrange("p i (g e) -> p i g e", g=GROUPS_E),
                                          biased_score[:, :, :].rearrange("p i (g e) -> p i g e", g=GROUPS_E),
                                          group_rest[:, :, 0:GROUPS_E].unsqueeze(3).to_broadcast([P, TILES, GROUPS_E, GS]), ALU.mult))
                dve.chain(v.tensor_scalar(masked[:, :, 0:EXPERTS], masked[:, :, 0:EXPERTS], 0.0, None, ALU.add))
                for i in range(TILES):
                    dve.mark(v.max(top[:, i, :], masked[:, i, 0:EXPERTS]))
                dve.wait()
                dve.chain(v.memset(top[:, :, TOP_E:8], LOW))
                for i in range(TILES):
                    dve.mark(v.match_replace(rest[:, i, :], top[:, i, :], masked[:, i, :], HIGH))
                dve.wait()
                dve.chain(v.tensor_tensor(rest[:, :, 0:EXPERTS], rest[:, :, 0:EXPERTS], masked[:, :, 0:EXPERTS], ALU.not_equal))
                dve.chain(v.tensor_tensor(score[:, :, :], score[:, :, :], rest[:, :, 0:EXPERTS], ALU.mult))
                dve.chain(v.tensor_reduce(den[:, :], score[:, :, :], AX.X, ALU.add))
                dve.chain(v.tensor_scalar(den[:, :], den[:, :], 1e-20, None, ALU.add))
                dve.chain(v.reciprocal(den[:, :], den[:, :]))
                dve.chain(v.tensor_scalar(den[:, :], den[:, :], 2.5, None, ALU.mult))
                v.wait_ge(x_low, GROUPS)
                v.tensor_tensor(m.C[:, :, 0:EXPERTS], score[:, :, :], den[:, :].unsqueeze(2).to_broadcast([P, TILES, EXPERTS]), ALU.mult)


def experts(nc, d, m):
    ROUNDS = ALL_E // 2
    UPR = 2 * GROUPS
    PARTS = ((0, 0), (0, 1), (1, 0))
    with ExitStack() as scope:
        sem = lambda n: new_semaphore(nc, m, f"ex_{n}")
        sb = lambda n, shape, dt=F32: scope.enter_context(nc.sbuf_tensor(f"ex_{n}", shape, dt))
        GU, DN = [sb(f"gu{h}", [P, KD, 2 * P]) for h in range(2)], [sb(f"dn{h}", [P, D]) for h in range(2)]
        GUS = [[sb(f"gu{h}{z}", [P, KD, 2 * P], F32R) for z in ("high", "low")] for h in range(2)]
        DNS = [[sb(f"dn{h}{z}", [P, D], F32R) for z in ("high", "low")] for h in range(2)]
        SI, H = sb("si", [P, 2, BANK]), sb("h", [P, 2, BANK])
        HS = [sb(f"h{z}", [P, 2, BANK], F32R) for z in ("high", "low")]
        w_loaded, w_high, w_split = ([sem(f"{n}{h}") for h in range(2)] for n in ("loaded", "high", "split"))
        gu_done, silu_done, prod_done, high_done, h_done, down_done, acc_done = (
            sem(n) for n in ("gu", "silu", "prod", "high", "h", "down", "acc"))
        with nc.Block(no_gpsimd_drain=True) as block:
            @block.sync
            def _(sp):
                def load(it, h):
                    sp.dma_start(GU[h][:, :, :], d["guT"][2 * it + h].rearrange("(k p) n -> p k n", p=P)).then_inc(w_loaded[h], 16)
                    sp.dma_start(DN[h][:, :], d["dnT"][2 * it + h]).then_inc(w_loaded[h], 16)

                load(0, 0)
                load(0, 1)
                with sp.Fori(1, ROUNDS) as it:
                    for h in range(2):
                        sp.wait_ge(w_split[h], 2 * it)
                        load(it, h)

            @block.gpsimd
            def _(pool):
                def low_part(it, h):
                    pool.wait_ge(w_high[h], 2 * it + 2)
                    for dst, src in ((GUS[h], GU[h]), (DNS[h], DN[h])):
                        pool.tensor_tensor(dst[1][:], src[:], dst[0][:].bitcast(F32), ALU.subtract).then_inc(w_split[h], 1)

                with pool.Fori(0, ROUNDS) as it:
                    for h in range(2):
                        low_part(it, h)

            @block.tensor
            def _(t):
                def gate_up(it, u, first=False):
                    h, g = divmod(u, GROUPS)
                    if g == 0:
                        t.wait_ge(w_split[h], 2 * it + 2)
                    if not first:
                        t.wait_ge(prod_done, it * UPR + (u - 1))
                    for part in range(2):
                        for k in range(KD):
                            for n, (w, x) in enumerate(PARTS):
                                ins = t.matmul(m.PS[:, 2 * part + u % 2, :], GUS[h][w][:, k, part * P:(part + 1) * P],
                                               m.XS[x][:, k, g * BANK:(g + 1) * BANK],
                                               start=k == 0 and n == 0, stop=k == KD - 1 and n == 2)
                    ins.then_inc(gu_done, 1)

                def down(it, u):
                    h = u // GROUPS
                    n = it * UPR + u
                    t.wait_ge(h_done, n + 1)
                    t.wait_ge(acc_done, n + 1)
                    for i in range(4):
                        for z, (a_, w) in enumerate(PARTS):
                            ins = t.matmul(m.PS[:, 4 + 2 * (u % 2) + i // 2, (i % 2) * D:(i % 2 + 1) * D],
                                           HS[a_][:, u % 2, i * P:(i + 1) * P], DNS[h][w][:, :], start=z == 0, stop=z == 2)
                    ins.then_inc(down_done, 1)

                def unit(it, u, ahead=True):
                    if u + 2 < UPR:
                        gate_up(it, u + 2)
                    elif ahead:
                        gate_up(it + 1, u + 2 - UPR)
                    down(it, u)

                gate_up(0, 0, first=True)
                gate_up(0, 1, first=True)
                with t.Fori(0, ROUNDS - 1) as it:
                    for u in range(UPR):
                        unit(it, u)
                for u in range(UPR):
                    unit(ROUNDS - 1, u, ahead=False)

            @block.scalar
            def _(a):
                def silu(it, u):
                    a.wait_ge(gu_done, it * UPR + (u + 1))
                    a.activation(SI[:, u % 2, :], m.PS[:, u % 2, :], ACT.Silu).then_inc(silu_done, 1)

                def high(it, u):
                    a.wait_ge(prod_done, it * UPR + (u + 1))
                    a.activation(HS[0][:, u % 2, :], H[:, u % 2, :], ACT.Copy).then_inc(high_done, 1)

                def weights_high(it, h, first=False):
                    if not first:
                        a.wait_ge(down_done, it * UPR - (UPR - GROUPS * (h + 1)))
                    a.wait_ge(w_loaded[h], it * 32 + 32)
                    for dst, src in ((GUS[h][0], GU[h]), (DNS[h][0], DN[h])):
                        a.activation(dst[:], src[:], ACT.Copy).then_inc(w_high[h], 1)

                def turn(it, first=False, last=False):
                    for u in range(UPR):
                        if u + 1 < UPR:
                            silu(it, u + 1)
                        elif not last:
                            silu(it + 1, 0)
                        high(it, u)
                        if u == 0 and not first:
                            weights_high(it, 1)
                        if u == GROUPS and not last:
                            weights_high(it + 1, 0)

                weights_high(0, 0, first=True)
                weights_high(0, 1, first=True)
                silu(0, 0)
                turn(0, first=True)
                with a.Fori(1, ROUNDS - 1) as it:
                    turn(it)
                turn(ROUNDS - 1, last=True)

            @block.vector
            def _(v):
                def product(it, u):
                    v.wait_ge(silu_done, it * UPR + (u + 1))
                    v.tensor_tensor(H[:, u % 2, :], m.PS[:, 2 + u % 2, :], SI[:, u % 2, :], ALU.mult).then_inc(prod_done, 1)

                def low(it, u):
                    v.wait_ge(high_done, it * UPR + (u + 1))
                    v.tensor_tensor(HS[1][:, u % 2, :], H[:, u % 2, :], HS[0][:, u % 2, :].bitcast(F32),
                                    ALU.subtract).then_inc(h_done, 1)

                def accumulate(it, u):
                    h, g = divmod(u, GROUPS)
                    v.wait_ge(down_done, it * UPR + (u + 1))
                    for i in range(4):
                        x = m.X[:, 4 * g + i, :]
                        ins = v.scalar_tensor_tensor(x, m.PS[:, 4 + 2 * (u % 2) + i // 2, (i % 2) * D:(i % 2 + 1) * D],
                                                     m.C[:, 4 * g + i, bass.ds(2 * it + h, 1)], x, ALU.mult, ALU.add)
                    ins.then_inc(acc_done, 1)

                def unit(it, u, ahead=True):
                    if u + 1 < UPR:
                        product(it, u + 1)
                    elif ahead:
                        product(it + 1, 0)
                    accumulate(it, u)
                    if u + 1 < UPR:
                        low(it, u + 1)
                    elif ahead:
                        low(it + 1, 0)

                v.sem_inc(acc_done, 2)
                product(0, 0)
                low(0, 0)
                with v.Fori(0, ROUNDS - 1) as it:
                    for u in range(UPR):
                        unit(it, u)
                for u in range(UPR):
                    unit(ROUNDS - 1, u, ahead=False)


def last_norm(nc, d, m):
    out = d["out"].rearrange("(i p) d -> p i d", p=P)
    with ExitStack() as scope:
        s = norm_state(nc, m, scope, "ln")
        step, stored = new_semaphore(nc, m, "ln_step"), new_semaphore(nc, m, "ln_stored")
        with nc.Block(no_gpsimd_drain=True) as block:
            @block.sync
            def _(sp):
                for u in range(0, UNITS, 2):
                    sp.wait_ge(s.normed, 2 * u + 4)
                    sp.dma_start(out[:, 2 * u:2 * u + 4, :], m.X[:, 2 * u:2 * u + 4, :]).then_inc(stored, 16)
                sp.wait_ge(stored, 16 * UNITS // 2)

            @block.scalar
            def _(a):
                for u in range(UNITS + 1):
                    if u < UNITS:
                        norm_root(a, m, s, u)
                    if u >= 1:
                        norm_apply(a, m, s, u - 1)

            @block.vector
            def _(v):
                dve = Steps(v, step)
                for u in range(UNITS + 1):
                    if u < UNITS:
                        norm_sum(v, dve, m, s, u, None)
                    if u >= 1:
                        norm_scale(v, dve, s, u - 1)


STAGES = [hyena_project, hyena_filter, hyena_convolve, hyena_out, cross_attend_0, slot_mixer, axis_attend,
          cross_attend_1, expert_route, experts, last_norm]


def build(nc, d):
    with ExitStack() as mem:
        m = Record()
        m.semaphores = []
        sb = lambda n, shape: mem.enter_context(nc.sbuf_tensor(n, shape, F32))
        m.X, m.XT = sb("X", [P, TILES, D]), sb("XT", [P, KD, TOK])
        m.ident, m.cols, m.eps, m.ones = sb("ident", [P, P]), sb("cols", [P, NCOLS]), sb("eps", [P, 1]), sb("ones", [P, P])
        m.PS = mem.enter_context(nc.psum_tensor("PS", [P, 8, BANK], F32))
        with ExitStack() as hyena:
            m.V = hyena.enter_context(nc.sbuf_tensor("V", [P, 3, BLOCKS, B * D], F32))
            for stage in STAGES[:4]:
                stage(nc, d, m)
        m.C = sb("C", [P, TILES, ALL_E])
        for stage in STAGES[4:6]:
            stage(nc, d, m)
        end_layer(nc, m)
        for stage in STAGES[6:8]:
            stage(nc, d, m)
        m.XS = [mem.enter_context(nc.sbuf_tensor(f"XT_{z}", [P, KD, TOK], F32R)) for z in ("high", "low")]
        for stage in STAGES[8:]:
            stage(nc, d, m)


def constants():
    f4 = np.float32
    t = np.arange(L, dtype=f4) / f4(L - 1)
    bands = np.arange(EMB, dtype=f4)
    arg = ((t[:, None] * bands[None, :]).astype(f4) * f4(FREQ)).astype(f4)
    peT = np.sin(arg.astype(np.float64)).astype(f4).T
    negt = -t.reshape(BLOCKS, P).T
    p, r, c = np.arange(P)[:, None, None], np.arange(P)[None, None, :], np.arange(CLASSES)[None, :, None]
    turn = (p * (2 * (c + 16 * r) + 1)) % (4 * L) * (np.pi / (2 * L))
    forward = np.stack([np.cos(turn), np.sin(turn), -np.sin(turn)], axis=2)
    inverse = np.ascontiguousarray(forward.transpose(3, 1, 2, 0)) / (L * L)
    return {"peT": peT, "negt": negt, "forward": forward, "inverse": inverse, "ident": np.eye(P)}


def expert_gates(g):
    own = g["L1_ffn_experts_gate_up"].transpose(0, 2, 1)
    gate, up = (g[f"L1_ffn_shared_{n}_w"].reshape(SHARED, P, D) for n in ("gate", "up"))
    return np.concatenate([own, np.concatenate([gate, up], axis=1).transpose(0, 2, 1)])


def expert_downs(g):
    own = g["L1_ffn_experts_down"].transpose(0, 2, 1)
    return np.concatenate([own, g["L1_ffn_shared_down_w"].T.reshape(SHARED, P, D)])


def kernel(**inputs):
    import concourse.bacc as bacc
    from concourse.bass_utils import run_bass_kernel_spmd

    g = {k: np.asarray(v) for k, v in inputs.items()}
    cols = np.zeros((P, NCOLS), np.float32)
    for name, source in (("b_in", "L0_attn_b_in"), ("conv_b", "L0_attn_conv_b"), ("hy_b1", "L0_attn_b1"),
                         ("x0_bq", "L0_xattn_bq"), ("x0_bk", "L0_xattn_bk"), ("f_b1", "L0_ffn_b1"),
                         ("f_bq", "L0_ffn_bq"), ("f_bk", "L0_ffn_bk"), ("x1_bq", "L1_xattn_bq"), ("x1_bk", "L1_xattn_bk")):
        at, n = COLS[name]
        part = g[source].reshape(n, -1).T
        cols[:part.shape[0], at:at + n] = part
    at, n = COLS["conv_w"]
    cols[:, at:at + n] = g["L0_attn_conv_w"].reshape(6, P, 3).transpose(1, 0, 2).reshape(P, 18)
    x = g["x"].reshape(TOK, D)
    arrays = {
        "x": x, "xT": x.T, "cols": cols,
        "hy_w_inT": g["L0_attn_w_in"].T, "hy_w1T": g["L0_attn_w1"].T, "hy_w2T": g["L0_attn_w2"].T,
        "hy_b2": g["L0_attn_b2"], "hy_decay": g["L0_attn_filt_decay"].reshape(-1),
        "hy_fbias": g["L0_attn_filt_bias"].reshape(-1), "hy_w_outT": g["L0_attn_w_out"].T, "hy_b_out": g["L0_attn_b_out"],
        "ctx": g["ctx_1024"].reshape(B * KEYS, D), "ctxT": g["ctx_1024"].reshape(B * KEYS, D).T,
        "wkT0": g["L0_xattn_Wk"].T, "wq0": g["L0_xattn_Wq"], "wkT1": g["L1_xattn_Wk"].T, "wq1": g["L1_xattn_Wq"],
        "wvT": g["L1_xattn_Wv"].T, "bv": g["L1_xattn_bv"], "table": g["fside_BxSxS2_0"].reshape(TOK, KEYS),
        "betas": np.stack([g[f"L1_xattn_beta_{n}"].reshape(()) for n in ("risk", "prio", "impl")]),
        "slots2": np.tile(g["L0_ffn_slot_init"], (B, 1)), "slotsT2": np.tile(g["L0_ffn_slot_init"], (B, 1)).T,
        "f_wihT": g["L0_ffn_Wih"].T, "f_whhT": g["L0_ffn_Whh"].T,
        **{f"f_{n}": g[f"L0_ffn_{n}"] for n in ("w1", "w2", "b2", "tau", "bih", "bhh", "wq", "wk", "wv", "bv",
                                                "ln_g", "ln_b", "wvp", "bvp", "wo", "bo")},
        "a_inT": g["L1_attn_in_proj_w"].T, "a_in_b": g["L1_attn_in_proj_b"],
        "a_outT": g["L1_attn_out_proj_w"].T, "a_out_b": g["L1_attn_out_proj_b"],
        "gateT": g["L1_ffn_gate_weight"].T, "e_bias": g["L1_ffn_e_score_correction_bias"],
        "guT": expert_gates(g), "dnT": expert_downs(g),
        **constants(),
    }
    nc = bacc.Bacc("TRN2", target_bir_lowering=False, num_devices=1)
    d, fed = {}, {}
    for name, a in arrays.items():
        fed[f"in_{name}"] = np.ascontiguousarray(a, dtype=np.float32)
        d[name] = nc.dram_tensor(f"in_{name}", fed[f"in_{name}"].shape, F32, kind="ExternalInput").ap()
    d["out"] = nc.dram_tensor("out", (TOK, D), F32, kind="ExternalOutput").ap()
    build(nc, d)
    r = run_bass_kernel_spmd(nc, [fed], core_ids=[0])
    return r.results[0]["out"].reshape(B, L, D)
```

```python
from contextlib import ExitStack
import math

import numpy as np
import concourse.bass as bass
from concourse import mybir

F32 = mybir.dt.float32
F32R = mybir.dt.float32r
ALU = mybir.AluOpType
ACT = mybir.ActivationFunctionType
AX = mybir.AxisListType

B, L, D = 2, 1024, 256
TOK = B * L
P = 128
TILES = TOK // P
UNITS = TILES // 2
GROUPS = TILES // 4
KD = D // P
BANK = 512
BLOCKS = L // P
CLASSES = BLOCKS
KEYS = 64
SLOTS, TOP_SLOTS = 64, 8
HEADS, HD = 16, 16
EXPERTS, GROUPS_E, TOP_GROUPS, TOP_E = 32, 8, 4, 6
SHARED = 2
ALL_E = EXPERTS + SHARED
EMB = 33
FREQ = 10.0
EPS = 1e-5
LOW, HIGH = -3.0e38, 3.0e38

COLS, _at = {}, 0
for _name, _n in (("b_in", 6), ("conv_w", 18), ("conv_b", 6), ("hy_b1", 1), ("x0_bq", 2), ("x0_bk", 2),
                  ("f_b1", 1), ("f_bq", 1), ("f_bk", 1), ("x1_bq", 2), ("x1_bk", 2)):
    COLS[_name] = (_at, _n)
    _at += _n
NCOLS = _at


class Record:
    pass


class Steps:

    def __init__(self, eng, sem):
        self.eng, self.sem, self.n = eng, sem, 0

    def mark(self, ins):
        ins.then_inc(self.sem, 1)
        self.n += 1
        return self.n

    def wait(self, value=None):
        self.eng.wait_ge(self.sem, self.n if value is None else value)

    def chain(self, ins):
        self.mark(ins)
        self.wait()


def new_semaphore(nc, m, name):
    m.semaphores.append(nc.alloc_semaphore(name))
    return m.semaphores[-1]


def end_layer(nc, m):
    nc.clear_and_free_semaphores(m.semaphores)
    m.semaphores = []
    nc.all_engine_barrier()


def col(m, name, j=0, rows=P):
    at = COLS[name][0] + j
    return m.cols[0:rows, at:at + 1]


def rows_of(vector, n=P):
    return vector.rearrange("(o n) -> o n", o=1).to_broadcast([n, vector.shape[0]])


def chunks(matrix):
    return matrix.rearrange("(k p) n -> p k n", p=P)



def norm_state(nc, m, scope, tag):
    s = Record()
    s.st = scope.enter_context(nc.sbuf_tensor(f"{tag}_st", [P, 2, 2, 6], F32))
    s.mv = scope.enter_context(nc.sbuf_tensor(f"{tag}_mv", [P, UNITS, 2, 2], F32))
    s.std = scope.enter_context(nc.sbuf_tensor(f"{tag}_std", [P, UNITS, 2], F32))
    s.rstd = scope.enter_context(nc.sbuf_tensor(f"{tag}_rstd", [P, UNITS, 2], F32))
    s.shift = scope.enter_context(nc.sbuf_tensor(f"{tag}_shift", [P, UNITS, 2], F32))
    s.out_done, s.summed, s.stats, s.root, s.scaled, s.normed, s.turned, s.xt_done = (
        new_semaphore(nc, m, f"{tag}_{n}") for n in
        ("out_done", "summed", "stats", "root", "scaled", "normed", "turned", "xt_done"))
    return s


def norm_sum(v, dve, m, s, u, bank, first=lambda: None):
    x = m.X[:, 2 * u:2 * u + 2, :]
    if bank is not None:
        v.wait_ge(s.out_done, u + 1)
        first()
        v.tensor_tensor(x, m.PS[:, bank, :].rearrange("p (i d) -> p i d", i=2), x, ALU.add).then_inc(s.summed, 1)
        v.wait_ge(s.summed, u + 1)
    for i in range(2):
        dve.mark(v.bn_stats(s.st[:, u % 2, i, :], m.X[:, 2 * u + i, :]))
    dve.wait()
    for i in range(2):
        v.bn_aggr(s.mv[:, u, i, :], s.st[:, u % 2, i, :]).then_inc(s.stats, 1)


def norm_root(a, m, s, u):
    a.wait_ge(s.stats, 2 * u + 2)
    a.activation(s.std[:, u, :], s.mv[:, u, :, 1], ACT.Sqrt, bias=m.eps[:, 0:1]).then_inc(s.root, 1)


def norm_scale(v, dve, s, u):
    v.wait_ge(s.root, u + 1)
    dve.chain(v.reciprocal(s.rstd[:, u, :], s.std[:, u, :]))
    v.scalar_tensor_tensor(s.shift[:, u, :], s.mv[:, u, :, 0], -1.0, s.rstd[:, u, :],
                           ALU.mult, ALU.mult).then_inc(s.scaled, 1)


def norm_apply(a, m, s, u):
    a.wait_ge(s.scaled, u + 1)
    for i in range(2):
        x = m.X[:, 2 * u + i, :]
        a.activation(x, x, ACT.Identity, bias=s.shift[:, u, i:i + 1],
                     scale=s.rstd[:, u, i:i + 1]).then_inc(s.normed, 1)


def norm_turn(t, m, s, u, banks):
    t.wait_ge(s.normed, 2 * u + 2)
    if u >= 2:
        t.wait_ge(s.xt_done, u - 1)
    out = m.PS[:, banks[u % 2], :].rearrange("p (k i t) -> p k i t", k=KD, i=2)
    for k in range(KD):
        for i in range(2):
            ins = t.transpose(out[:, k, i, :], m.X[:, 2 * u + i, k * P:(k + 1) * P], m.ident[:, :])
    ins.then_inc(s.turned, 1)


def norm_copy(a, m, s, u, banks):
    a.wait_ge(s.turned, u + 1)
    a.activation(m.XT[:, :, 2 * u * P:(2 * u + 2) * P],
                 m.PS[:, banks[u % 2], :].rearrange("p (k t) -> p k t", k=KD), ACT.Identity).then_inc(s.xt_done, 1)



def hyena_prepare(nc, d, m):
    C = 3 * D // P
    H = m.H
    two_pi = 2 * math.pi
    hi = 6.28125
    mid = float(np.float32(two_pi - hi))
    lo = two_pi - hi - mid
    magic = 1.5 * 2.0 ** 23
    with ExitStack() as scope:
        sem = lambda n: new_semaphore(nc, m, f"pj_{n}")
        sb = lambda n, shape: scope.enter_context(nc.sbuf_tensor(f"pj_{n}", shape, F32))
        W, padded, taps = sb("w", [P, KD, 3 * D]), sb("padded", [P, 2, B, L + 2]), sb("taps", [P, 2, B, L])
        pe, w1, w2 = sb("pe", [EMB, L]), sb("w1", [EMB, 64]), sb("w2", [65, 2 * D])
        negt, rate, shift = sb("negt", [P, BLOCKS]), sb("rate", [P, 2 * D]), sb("shift", [P, 2 * D])
        arg, sine, decay = sb("arg", [64, L]), sb("sine", [65, L]), sb("decay", [P, 4, 2 * D])
        turns = sine[0:64, :]
        loaded, xt_loaded, pads, eps_set = sem("loaded"), [sem(f"xt{g}") for g in range(GROUPS)], sem("pads"), sem("eps")
        product, biased, centre, tapped, turned, placed = (sem(n) for n in (
            "product", "biased", "centre", "tapped", "turned", "placed"))
        mlp_loaded, rate_loaded, out_loaded = sem("mlp_loaded"), sem("rate_loaded"), sem("out_loaded")
        one, hidden, step, reduced, sined, rated, decayed, drawn, filtered = (sem(n) for n in (
            "one", "hidden", "step", "reduced", "sined", "rated", "decayed", "drawn", "filtered"))
        xT = chunks(d["xT"])
        with nc.Block(no_gpsimd_drain=True) as block:
            @block.sync
            def _(sp):
                sp.dma_start(pe[:, :], d["peT"]).then_inc(mlp_loaded, 16)
                sp.dma_start(w1[:, :], d["hy_w1T"]).then_inc(mlp_loaded, 16)
                sp.dma_start(m.cols[:, :], d["cols"]).then_inc(mlp_loaded, 16)
                sp.dma_start(W[:, :, :], chunks(d["hy_w_inT"])).then_inc(loaded, 16)
                sp.dma_start(m.XT[:, :, 0:BANK], xT[:, :, 0:BANK]).then_inc(xt_loaded[0], 16)
                sp.dma_start(rate[:, :], rows_of(d["hy_decay"])).then_inc(rate_loaded, 16)
                sp.dma_start(negt[:, :], d["negt"]).then_inc(rate_loaded, 16)
                for g in range(1, GROUPS):
                    sp.dma_start(m.XT[:, :, g * BANK:(g + 1) * BANK],
                                 xT[:, :, g * BANK:(g + 1) * BANK]).then_inc(xt_loaded[g], 16)
                sp.dma_start(w2[0:64, :], d["hy_w2T"]).then_inc(out_loaded, 16)
                sp.dma_start(w2[64:65, :], d["hy_b2"].rearrange("(o n) -> o n", o=1)).then_inc(out_loaded, 16)
                sp.dma_start(shift[:, :], rows_of(d["hy_fbias"])).then_inc(out_loaded, 16)
                sp.dma_start(m.ident[:, :], d["ident"]).then_inc(loaded, 16)
                sp.dma_start(m.FW[:, :, :, :], d["forward"]).then_inc(m.transforms_loaded, 16)
                sp.dma_start(m.IV[:, :, :, :], d["inverse"]).then_inc(m.transforms_loaded, 16)

            @block.gpsimd
            def _(pool):
                pool.memset(padded[:, :, :, 0:1], 0.0).then_inc(pads, 1)
                pool.memset(padded[:, :, :, L + 1:L + 2], 0.0).then_inc(pads, 1)
                pool.memset(m.eps[:, :], EPS).then_inc(eps_set, 1)
                pool.memset(m.ones[:, :], 1.0).then_inc(eps_set, 1)

            @block.tensor
            def _(t):
                def project(c):
                    for g in range(GROUPS):
                        n = GROUPS * c + g
                        if c == 0:
                            t.wait_ge(xt_loaded[g], 16)
                        if n >= 4:
                            t.wait_ge(biased, n - 3)
                        for k in range(KD):
                            ins = t.matmul(m.PS[:, n % 4, :], W[:, k, c * P:(c + 1) * P],
                                           m.XT[:, k, g * BANK:(g + 1) * BANK], start=k == 0, stop=k == KD - 1)
                        ins.then_inc(product, 1)

                def turn(c):
                    t.wait_ge(tapped, 2 * c + 2)
                    for j in range(4):
                        n = 4 * c + j
                        if n >= 4:
                            t.wait_ge(placed, n - 3)
                        else:
                            t.wait_ge(filtered, 5 + j)
                        for i in range(4):
                            at = (4 * (j % 2) + i) * P
                            ins = t.transpose(m.PS[:, 4 + j, i * P:(i + 1) * P],
                                              taps[:, c % 2, j // 2, at:at + P], m.ident[:, :])
                        ins.then_inc(turned, 1)

                t.wait_ge(mlp_loaded, 48)
                for g in range(2):
                    t.matmul(m.PS[0:64, 4 + g, :], w1[:, :], pe[:, g * BANK:(g + 1) * BANK],
                             start=True, stop=True).then_inc(hidden, 1)
                t.wait_ge(loaded, 32)
                project(0)
                t.wait_ge(sined, 1)
                t.wait_ge(one, 1)
                t.wait_ge(out_loaded, 48)
                for a in range(BLOCKS):
                    if a >= 4:
                        t.wait_ge(filtered, a - 3)
                    t.matmul(m.PS[:, 4 + a % 4, :], sine[:, a * P:(a + 1) * P], w2[:, :],
                             start=True, stop=True).then_inc(drawn, 1)
                for c in range(C):
                    if c + 1 < C:
                        project(c + 1)
                    turn(c)

            @block.scalar
            def _(a):
                def decays(first):
                    for i in range(first, first + 4):
                        if i >= 4:
                            a.wait_ge(filtered, i - 3)
                        a.activation(decay[:, i % 4, :], rate[:, :], ACT.Exp, scale=negt[:, i:i + 1]).then_inc(decayed, 1)

                def bias(c):
                    for g in range(GROUPS):
                        a.wait_ge(product, GROUPS * c + g + 1)
                        if c >= 2 and g == 0:
                            a.wait_ge(tapped, 2 * c - 2)
                        at = 1 + BANK * (g % 2)
                        a.activation(padded[:, c % 2, g // 2, at:at + BANK], m.PS[:, (GROUPS * c + g) % 4, :],
                                     ACT.Identity, bias=col(m, "b_in", c)).then_inc(biased, 1)

                a.wait_ge(rate_loaded, 32)
                a.activation(rate[:, :], rate[:, :], ACT.Exp).then_inc(rated, 1)
                a.wait_ge(rated, 1)
                decays(0)
                a.wait_ge(reduced, 1)
                a.activation(sine[0:64, :], arg[:, :], ACT.Sin).then_inc(sined, 1)
                a.wait_ge(loaded, 32)
                for c in range(C):
                    bias(c)
                    if c == 0:
                        decays(4)
                    a.wait_ge(biased, GROUPS * c + GROUPS)
                    if c >= 2:
                        a.wait_ge(turned, 4 * (c - 1))
                    a.activation(taps[:, c % 2, :, :], padded[:, c % 2, :, 1:L + 1], ACT.Identity,
                                 bias=col(m, "conv_b", c), scale=col(m, "conv_w", 3 * c + 1)).then_inc(centre, 1)

            @block.vector
            def _(v):
                dve = Steps(v, step)

                def tap(c):
                    v.wait_ge(centre, c + 1)
                    for n, j in enumerate((0, 2)):
                        if n:
                            v.wait_ge(tapped, 2 * c + 1)
                        v.scalar_tensor_tensor(taps[:, c % 2, :, :], padded[:, c % 2, :, j:j + L],
                                               col(m, "conv_w", 3 * c + j), taps[:, c % 2, :, :],
                                               ALU.mult, ALU.add).then_inc(tapped, 1)

                def place(c):
                    for j in range(4):
                        v.wait_ge(turned, 4 * c + j + 1)
                        at = (j // 2) * D + (c % 2) * P
                        v.tensor_copy(m.V[:, c // 2, 4 * (j % 2):4 * (j % 2) + 4, at:at + P],
                                      m.PS[:, 4 + j, :].rearrange("p (a c) -> p a c", a=4)).then_inc(placed, 1)

                v.memset(sine[64:65, :], 1.0).then_inc(one, 1)
                v.wait_ge(hidden, 2)
                v.wait_ge(mlp_loaded, 48)
                dve.chain(v.tensor_scalar(arg[:, :], m.PS[0:64, 4:6, :], col(m, "hy_b1", 0, 64), FREQ,
                                          ALU.add, ALU.mult))
                dve.chain(v.tensor_scalar(turns, arg[:, :], 1 / two_pi, magic, ALU.mult, ALU.add))
                dve.chain(v.tensor_scalar(turns, turns, magic, None, ALU.subtract))
                for part in (hi, mid, lo):
                    dve.chain(v.scalar_tensor_tensor(arg[:, :], turns, -part, arg[:, :], ALU.mult, ALU.add))
                pi = float(np.nextafter(np.float32(math.pi), np.float32(0)))
                v.tensor_scalar(arg[:, :], arg[:, :], -pi, pi, ALU.max, ALU.min).then_inc(reduced, 1)
                v.wait_ge(out_loaded, 48)
                for a in range(BLOCKS):
                    v.wait_ge(drawn, a + 1)
                    v.wait_ge(decayed, a + 1)
                    v.tensor_tensor(H[:, a, :], m.PS[:, 4 + a % 4, :], decay[:, a % 4, :], ALU.mult).then_inc(filtered, 1)
                v.wait_ge(filtered, BLOCKS)
                v.tensor_tensor(H[:, :, :], H[:, :, :], shift[:, :].unsqueeze(1).to_broadcast([P, BLOCKS, 2 * D]), ALU.add)
                v.wait_ge(pads, 2)
                v.wait_ge(loaded, 32)
                tap(0)
                for c in range(C):
                    if c + 1 < C:
                        tap(c + 1)
                    place(c)



def hyena_convolve(nc, d, m):
    PAIRS = CLASSES // 2
    ORDERS = 2
    ORDER = (0, 3, 1, 2)
    pairs_of = lambda flat: flat.rearrange("p (s c r n) -> p s c r n", s=2, c=2, r=2)
    UF, UV = pairs_of(m.XT[:, :, :].rearrange("p k t -> p (k t)")), pairs_of(m.X[:, :, :].rearrange("p i d -> p (i d)"))
    U = lambda n: (UV if n >= PAIRS else UF)[:, n % 2]
    Y = m.XT[:, :, :].rearrange("p k t -> p (k t)").rearrange("p (a n) -> p a n", n=BANK)
    cos = lambda a, j: math.cos(math.pi * a * (2 * j + 1) / 16)
    sin = lambda a, j: math.sin(math.pi * a * (2 * j + 1) / 16)
    UPDATES = (4, 6, 2, 0, 1, 3, 5, 7)
    SUM_OPS = (ALU.add, ALU.subtract, ALU.subtract, ALU.add)
    remade = lambda o, a: BLOCKS * (o - 1) + UPDATES.index(a) + 1
    with ExitStack() as scope:
        sem = lambda n: new_semaphore(nc, m, f"cv_{n}")
        sb = lambda n, shape: scope.enter_context(nc.sbuf_tensor(f"cv_{n}", shape, F32))
        FW, IV = m.FW, m.IV
        HS = sb("hs", [P, CLASSES, 2, 2 * D])
        SUMS = sb("sums", [P, 11, BANK])
        W4, PLUS, MINUS, C0, S1, S0, C1 = (SUMS[:, i, :] for i in range(7))
        OD = [SUMS[:, 7 + i, :] for i in range(4)]
        G = [SUMS[:, i, :] for i in range(8)]
        ODD = sb("odd", [P, 2, BANK])
        T = sb("t", [P, 2, 4, BANK])
        Z = sb("z", [P, 2, 2, BANK])
        Q = sb("q", [P, 2, 4, BANK])
        pstep = sem("pstep")
        evens_scaled, odds_scaled, mixed, evened, odd_summed, folded, halves = (sem(n) for n in (
            "evens_scaled", "odds_scaled", "mixed", "evened", "odd_summed", "folded", "halves"))
        spectra, kept, products, joined, inverses, held, sums, combined, added, updated = (sem(n) for n in (
            "spectra", "kept", "products", "joined", "inverses", "held", "sums", "combined", "added", "updated"))
        classes = lambda n: (ORDER[n % PAIRS], CLASSES - 1 - ORDER[n % PAIRS])
        source = lambda tr: (lambda a: m.V[:, 2, a, :]) if tr else (lambda a: m.H[:, a, :])
        with nc.Block(no_gpsimd_drain=True) as block:
            @block.tensor
            def _(t):
                def complex_product(bank, M, c, re, im, sign):
                    plus, minus = (1, 2) if sign > 0 else (2, 1)
                    t.matmul(m.PS[:, bank, :], M[:, c, 0, :], re, start=True, stop=False)
                    t.matmul(m.PS[:, bank, :], M[:, c, minus, :], im, start=False, stop=True)
                    t.matmul(m.PS[:, bank + 1, :], M[:, c, 0, :], im, start=True, stop=False)
                    return t.matmul(m.PS[:, bank + 1, :], M[:, c, plus, :], re, start=False, stop=True)

                def forward(n):
                    t.wait_ge(halves, 4 * (n + 1))
                    for i, c in enumerate(classes(n)):
                        if 0 < n <= PAIRS:
                            t.wait_ge(kept, 4 * n - 2 + 2 * i)
                        elif n > PAIRS:
                            t.wait_ge(products, 8 * (n - PAIRS) - 4 + 4 * i)
                        complex_product(2 * i, FW, c, U(n)[:, i, 0, :], U(n)[:, i, 1, :], -1).then_inc(spectra, 1)

                def inverse(r):
                    for i, c in enumerate(classes(r)):
                        t.wait_ge(joined, 4 * r + 2 * i + 2)
                        if r >= 1:
                            t.wait_ge(held, 4 * r - 2 + 2 * i)
                        complex_product(4 + 2 * i, IV, c, T[:, i, 0, :], T[:, i, 2, :], 1).then_inc(inverses, 1)

                t.wait_ge(m.transforms_loaded, 32)
                for n in range(PAIRS):
                    forward(n)
                for o in range(ORDERS):
                    for s in range(PAIRS + 1):
                        if s < PAIRS:
                            forward(PAIRS * (o + 1) + s)
                        if s >= 1:
                            inverse(PAIRS * o + s - 1)

            @block.scalar
            def _(a):
                def scale_evens(tr):
                    v = source(tr)
                    if tr == 1:
                        a.wait_ge(evened, 2 * PAIRS)
                    for dst, block_, factor in ((W4, 4, math.sqrt(0.5)), (S1, 6, sin(2, 0)), (C1, 6, cos(2, 0))):
                        if tr >= 2:
                            a.wait_ge(updated, remade(tr - 1, block_))
                        a.activation(dst, v(block_), ACT.Copy, scale=factor).then_inc(evens_scaled, 1)

                def scale_odds(k):
                    tr, j = k // 2, k % 2
                    v = source(tr)
                    if tr >= 2:
                        a.wait_ge(updated, remade(tr - 1, 3))
                    if k >= 1:
                        a.wait_ge(folded, 4 * k)
                    for dst, block_, factor in ((OD[0], 1, cos(1, j)), (OD[1], 3, cos(3, j)),
                                                (OD[2], 1, -sin(1, j)), (OD[3], 3, -sin(3, j))):
                        a.activation(dst, v(block_), ACT.Copy, scale=factor).then_inc(odds_scaled, 1)

                def keep(n):
                    for i, c in enumerate(classes(n)):
                        a.wait_ge(spectra, 2 * n + i + 1)
                        for r in range(2):
                            a.activation(HS[:, c, r, :], m.PS[:, 2 * i + r, :], ACT.Identity).then_inc(kept, 1)

                def hold(r):
                    for i in range(2):
                        a.wait_ge(inverses, 2 * r + i + 1)
                        if r >= 1 and i == 0:
                            a.wait_ge(sums, 4 * r)
                        for z in range(2):
                            a.activation(Z[:, i, z, :], m.PS[:, 4 + 2 * i + z, :], ACT.Identity).then_inc(held, 1)

                scale_evens(0)
                scale_odds(0)
                keep(0)
                scale_odds(1)
                keep(1)
                keep(2)
                scale_evens(1)
                scale_odds(2)
                keep(3)
                for o in range(ORDERS):
                    if o:
                        scale_evens(o + 1)
                        scale_odds(2 * (o + 1))
                    scale_odds(2 * (o + 1) + 1)
                    for s in range(PAIRS):
                        hold(PAIRS * o + s)

            @block.gpsimd
            def _(pool):
                own = Steps(pool, pstep)

                def start_evens(tr):
                    pool.wait_ge(evens_scaled, 3 * tr + 1)
                    if tr >= 2:
                        pool.wait_ge(updated, remade(tr - 1, 0))
                    own.mark(pool.tensor_tensor(PLUS, source(tr)(0), W4, ALU.add))
                    own.mark(pool.tensor_tensor(MINUS, source(tr)(0), W4, ALU.subtract))

                def even_sums(n):
                    if n % PAIRS == 0:
                        own.wait()
                    if n % PAIRS in (0, 2):
                        pool.wait_ge(mixed, 4 * (n // PAIRS) + 2 + n % PAIRS)
                    if n >= 2:
                        pool.wait_ge(spectra, 2 * (n - 1))
                    re, im = (U(n)[:, 1, z, :] for z in range(2))
                    j = ORDER[n % PAIRS]
                    base, c, s = (PLUS, C0, S0) if j in (0, 3) else (MINUS, C1, S1)
                    pool.tensor_tensor(re, base, c, ALU.add if j < 2 else ALU.subtract).then_inc(evened, 1)
                    pool.tensor_tensor(im, s, W4, ALU.add if j < 2 else ALU.subtract).then_inc(evened, 1)

                def join(r):
                    for i in range(2):
                        pool.wait_ge(products, 8 * r + 4 * i + 4)
                        pool.tensor_tensor(T[:, i, 0, :], T[:, i, 0, :], T[:, i, 1, :], ALU.subtract).then_inc(joined, 1)
                        pool.tensor_tensor(T[:, i, 2, :], T[:, i, 2, :], T[:, i, 3, :], ALU.add).then_inc(joined, 1)

                def sum_pair(r, which=(0, 1, 2, 3)):
                    pool.wait_ge(held, 4 * (r + 1))
                    if r >= 2:
                        pool.wait_ge(combined, 8 * (r // 2))
                    for to in which:
                        pool.tensor_tensor(Q[:, r % 2, to, :], Z[:, 0, to // 2, :], Z[:, 1, to // 2, :],
                                           SUM_OPS[to]).then_inc(sums, 1)

                start_evens(0)
                for n in range(PAIRS):
                    even_sums(n)
                for o in range(ORDERS):
                    n, r = PAIRS * (o + 1), PAIRS * o
                    start_evens(o + 1)
                    even_sums(n)
                    even_sums(n + 1)
                    join(r)
                    even_sums(n + 2)
                    join(r + 1)
                    even_sums(n + 3)
                    sum_pair(r)
                    join(r + 2)
                    sum_pair(r + 1)
                    join(r + 3)
                    sum_pair(r + 2)
                    sum_pair(r + 3, (0, 2))

            @block.vector
            def _(v):
                def mix_evens(tr):
                    src = source(tr)(2)
                    v.wait_ge(evens_scaled, 3 * tr + 3)
                    if tr:
                        v.wait_ge(evened, 2 * PAIRS * tr)
                    v.scalar_tensor_tensor(C0, src, cos(2, 0), S1, ALU.mult, ALU.add).then_inc(mixed, 1)
                    v.scalar_tensor_tensor(S0, src, sin(2, 0), C1, ALU.mult, ALU.add).then_inc(mixed, 1)
                    v.wait_ge(mixed, 4 * tr + 2)
                    v.scalar_tensor_tensor(S1, src, cos(2, 0), S1, ALU.mult, ALU.subtract).then_inc(mixed, 1)
                    v.scalar_tensor_tensor(C1, src, sin(2, 0), C1, ALU.mult, ALU.subtract).then_inc(mixed, 1)

                def sum_odds(k):
                    tr, j = k // 2, k % 2
                    v.wait_ge(odds_scaled, 4 * (k + 1))
                    for dst, block_, factor in ((OD[0], 5, cos(5, j)), (OD[1], 7, cos(7, j)),
                                                (OD[2], 5, -sin(5, j)), (OD[3], 7, -sin(7, j))):
                        v.scalar_tensor_tensor(dst, source(tr)(block_), factor, dst, ALU.mult, ALU.add).then_inc(odd_summed, 1)
                    v.wait_ge(odd_summed, 4 * (k + 1))

                def split(n):
                    if n % 2 == 0:
                        sum_odds(n // 2)
                    if n:
                        v.wait_ge(halves, 4 * n)
                    for z in range(2):
                        if n % 2 == 0:
                            ins = v.tensor_tensor(ODD[:, z, :], OD[2 * z], OD[2 * z + 1], ALU.add)
                        else:
                            ins = v.tensor_tensor(ODD[:, z, :], OD[3 - 2 * z], OD[2 - 2 * z], ALU.subtract)
                        ins.then_inc(folded, 1)
                    v.wait_ge(folded, 2 * n + 2)
                    v.wait_ge(evened, 2 * n + 2)
                    one, two = U(n)[:, 0, :, :], U(n)[:, 1, :, :]
                    v.tensor_tensor(one[:, 0, :], two[:, 0, :], ODD[:, 0, :], ALU.add).then_inc(halves, 1)
                    v.tensor_tensor(one[:, 1, :], ODD[:, 1, :], two[:, 1, :], ALU.subtract).then_inc(halves, 1)
                    v.wait_ge(halves, 4 * n + 2)
                    v.tensor_tensor(two[:, 0, :], two[:, 0, :], ODD[:, 0, :], ALU.subtract).then_inc(halves, 1)
                    v.tensor_tensor(two[:, 1, :], ODD[:, 1, :], two[:, 1, :], ALU.add).then_inc(halves, 1)

                def multiply(r):
                    o = r // PAIRS
                    if r == 0:
                        v.wait_ge(kept, 4 * PAIRS)
                    for i, c in enumerate(classes(r)):
                        v.wait_ge(spectra, 2 * (PAIRS + r) + i + 1)
                        if r >= 1:
                            v.wait_ge(inverses, 2 * r - 1 + i)
                        h = [HS[:, c, z, o * D:(o + 1) * D].unsqueeze(1).to_broadcast([P, B, D]) for z in range(2)]
                        for to, (vz, hz) in enumerate(((0, 0), (1, 1), (0, 1), (1, 0))):
                            v.tensor_tensor(T[:, i, to, :].rearrange("p (b n) -> p b n", b=B),
                                            m.PS[:, 2 * i + vz, :].rearrange("p (b n) -> p b n", b=B),
                                            h[hz], ALU.mult).then_inc(products, 1)

                def combine(k):
                    if k % 2:
                        v.wait_ge(held, 16 * (k // 2 + 1))
                        for to in (1, 3):
                            v.tensor_tensor(Q[:, 1, to, :], Z[:, 0, to // 2, :], Z[:, 1, to // 2, :],
                                            SUM_OPS[to]).then_inc(sums, 1)
                    v.wait_ge(sums, 8 * (k + 1))
                    if k:
                        v.wait_ge(added, 15 * k)
                    one, two = ([Q[:, i, z, :] for z in range(4)] for i in range(2))
                    for to, (x, op, y) in enumerate((
                            (one[0], ALU.add, two[0]), (one[0], ALU.subtract, two[0]),
                            (one[2], ALU.add, two[2]), (one[2], ALU.subtract, two[2]),
                            (one[1], ALU.subtract, two[3]), (two[1], ALU.subtract, one[3]),
                            (one[1], ALU.add, two[3]), (two[1], ALU.add, one[3]))):
                        v.tensor_tensor(G[to], x, y, op).then_inc(combined, 1)

                def gather(k):
                    j, new = k % 2, k % 2 == 0
                    v.wait_ge(combined, 8 * (k + 1))
                    firsts = ((4, 0, cos(4, j)), (6, 1, cos(6, j)), (2, 1, cos(2, j)), (1, 4, cos(1, j)),
                              (3, 6, cos(3, j)), (5, 4, cos(5, j)), (7, 6, cos(7, j)))
                    seconds = ((4, 3, -sin(4, j)), (6, 2, -sin(6, j)), (2, 2, -sin(2, j)), (1, 5, sin(1, j)),
                               (3, 7, -sin(3, j)), (5, 5, sin(5, j)), (7, 7, -sin(7, j)))
                    for a, g, factor in firsts:
                        if new:
                            v.tensor_scalar(Y[:, a, :], G[g], factor, None, ALU.mult).then_inc(added, 1)
                        else:
                            v.scalar_tensor_tensor(Y[:, a, :], G[g], factor, Y[:, a, :], ALU.mult, ALU.add).then_inc(added, 1)
                    for n, (a, g, factor) in enumerate(seconds):
                        v.wait_ge(added, 15 * k + n + 1)
                        v.scalar_tensor_tensor(Y[:, a, :], G[g], factor, Y[:, a, :], ALU.mult, ALU.add).then_inc(added, 1)
                    if new:
                        v.tensor_copy(Y[:, 0, :], G[0]).then_inc(added, 1)
                    else:
                        v.tensor_tensor(Y[:, 0, :], Y[:, 0, :], G[0], ALU.add).then_inc(added, 1)

                def update(o):
                    v.wait_ge(added, 30 * (o + 1))
                    for a in UPDATES:
                        v.tensor_tensor(m.V[:, 2, a, :], Y[:, a, :], m.V[:, o, a, :], ALU.mult).then_inc(updated, 1)
                    v.wait_ge(updated, BLOCKS * (o + 1))

                mix_evens(0)
                for n in range(PAIRS):
                    split(n)
                for o in range(ORDERS):
                    at = PAIRS * (o + 1)
                    mix_evens(o + 1)
                    split(at)
                    split(at + 1)
                    multiply(at - PAIRS)
                    split(at + 2)
                    multiply(at - PAIRS + 1)
                    split(at + 3)
                    multiply(at - PAIRS + 2)
                    multiply(at - PAIRS + 3)
                    combine(2 * o)
                    gather(2 * o)
                    combine(2 * o + 1)
                    gather(2 * o + 1)
                    update(o)


def hyena_out(nc, d, m):
    banks = (4, 5)
    with ExitStack() as scope:
        sem = lambda n: new_semaphore(nc, m, f"ho_{n}")
        W = scope.enter_context(nc.sbuf_tensor("ho_w", [P, KD, D], F32))
        bias = scope.enter_context(nc.sbuf_tensor("ho_bias", [P, D], F32))
        s = norm_state(nc, m, scope, "ho")
        loaded, step, biased, vturned, vcopied = (sem(n) for n in ("loaded", "step", "biased", "vturned", "vcopied"))
        xl = [sem(f"x{u}") for u in range(4)]
        x = d["x"].rearrange("(i p) d -> p i d", p=P)
        with nc.Block(no_gpsimd_drain=True) as block:
            @block.sync
            def _(sp):
                sp.dma_start(bias[:, :], rows_of(d["hy_b_out"])).then_inc(loaded, 16)
                sp.dma_start(W[:, :, :], chunks(d["hy_w_outT"])).then_inc(loaded, 16)
                for g in range(4):
                    sp.dma_start(m.X[:, 4 * g:4 * g + 4, :], x[:, 4 * g:4 * g + 4, :]).then_inc(xl[g], 16)

            @block.gpsimd
            def _(pool):
                pool.wait_ge(loaded, 32)
                for u in range(UNITS):
                    pool.wait_ge(xl[u // 2], 16)
                    xu = m.X[:, 2 * u:2 * u + 2, :]
                    pool.tensor_tensor(xu, xu, bias[:, :].unsqueeze(1).to_broadcast([P, 2, D]), ALU.add).then_inc(biased, 1)

            @block.tensor
            def _(t):
                def turn(u):
                    if u >= 2:
                        t.wait_ge(vcopied, u - 1)
                    b, a = u // 4, 2 * (u % 4)
                    for k in range(KD):
                        for i in range(2):
                            at = b * D + k * P
                            ins = t.transpose(m.PS[:, 6 + u % 2, (2 * k + i) * P:(2 * k + i + 1) * P],
                                              m.V[:, 2, a + i, at:at + P], m.ident[:, :])
                    ins.then_inc(vturned, 1)

                def project(u):
                    t.wait_ge(vcopied, u + 1)
                    if u >= 4:
                        t.wait_ge(s.summed, u - 3)
                    for i in range(2):
                        for k in range(KD):
                            ins = t.matmul(m.PS[:, u % 4, i * D:(i + 1) * D],
                                           m.XT[:, k, (2 * u + i) * P:(2 * u + i + 1) * P], W[:, k, :],
                                           start=k == 0, stop=k == KD - 1)
                    ins.then_inc(s.out_done, 1)

                t.wait_ge(loaded, 32)
                for u in range(UNITS + 3):
                    if u < UNITS:
                        turn(u)
                    if 1 <= u <= UNITS:
                        project(u - 1)
                    if u >= 3:
                        norm_turn(t, m, s, u - 3, banks)

            @block.scalar
            def _(a):
                for u in range(UNITS + 3):
                    if u < UNITS:
                        a.wait_ge(vturned, u + 1)
                        a.activation(m.XT[:, :, 2 * u * P:(2 * u + 2) * P],
                                     m.PS[:, 6 + u % 2, :].rearrange("p (k t) -> p k t", k=KD),
                                     ACT.Identity).then_inc(vcopied, 1)
                    if 1 <= u <= UNITS:
                        norm_root(a, m, s, u - 1)
                    if 2 <= u <= UNITS + 1:
                        norm_apply(a, m, s, u - 2)
                    if u >= 3:
                        norm_copy(a, m, s, u - 3, banks)

            @block.vector
            def _(v):
                dve = Steps(v, step)
                for u in range(UNITS + 1):
                    if u < UNITS:
                        v.wait_ge(biased, u + 1)
                        norm_sum(v, dve, m, s, u, u % 4)
                    if u >= 1:
                        norm_scale(v, dve, s, u - 1)



def cross_attend(nc, d, m, layer):
    BK = B * KEYS
    tag = f"x{layer}"
    bias_q, bias_k = f"x{layer}_bq", f"x{layer}_bk"
    turn_banks = (6, 7)
    with ExitStack() as scope:
        sem = lambda n: new_semaphore(nc, m, f"{tag}_{n}")
        sb = lambda n, shape: scope.enter_context(nc.sbuf_tensor(f"{tag}_{n}", shape, F32))
        WkT, Wq, ctxT = sb("wkT", [P, KD, D]), sb("wq", [P, KD, D]), sb("ctxT", [P, KD, BK])
        KT, A, bqk, VAL = sb("kT", [P, KD, BK]), sb("a", [P, KD, BK]), sb("bqk", [1, BK]), sb("val", [P, D])
        S, mx, den = sb("s", [P, 2, 4, KEYS]), sb("mx", [P, 2, 4]), sb("den", [P, 2, 4])
        W, WT = sb("w", [P, TILES, BK]), sb("wT", [P, 2, BANK])
        s = norm_state(nc, m, scope, tag)
        loaded, zeroed, step, keys, keyed, folded, ready, scored, shifted, raised, weighted, wturned, wcopied = (
            sem(n) for n in ("loaded", "zeroed", "step", "keys", "keyed", "folded", "ready", "scored", "shifted",
                             "raised", "weighted", "wturned", "wcopied"))
        n_loads = 4
        if layer:
            WvT, bv, beta, table = sb("wvT", [P, KD, D]), sb("bv", [P, D]), sb("beta", [P, 3]), sb("table", [P, TILES, KEYS])
            n_loads = 7
            biased, valued, betas, tabled = sem("biased"), sem("valued"), sem("betas"), sem("tabled")
        with nc.Block(no_gpsimd_drain=True) as block:
            @block.sync
            def _(sp):
                sp.dma_start(WkT[:, :, :], chunks(d[f"wkT{layer}"])).then_inc(loaded, 16)
                sp.dma_start(ctxT[:, :, :], chunks(d["ctxT"])).then_inc(loaded, 16)
                sp.dma_start(Wq[:, :, :], chunks(d[f"wq{layer}"])).then_inc(loaded, 16)
                if layer:
                    sp.dma_start(WvT[:, :, :], chunks(d["wvT"])).then_inc(loaded, 16)
                    sp.dma_start(bv[:, :], rows_of(d["bv"])).then_inc(loaded, 16)
                    sp.dma_start(beta[:, :], rows_of(d["betas"])).then_inc(loaded, 16)
                    sp.dma_start(table[:, :, :], d["table"].rearrange("(i p) n -> p i n", p=P)).then_inc(loaded, 16)
                    sp.dma_start(m.gate[:, :, :], chunks(d["gateT"])).then_inc(m.gate_loaded, 16)
                    for h in range(2):
                        load_expert(sp, d, m, 0, h)
                else:
                    sp.dma_start(VAL[:, :], d["ctx"]).then_inc(loaded, 16)

            @block.gpsimd
            def _(pool):
                pool.memset(W[:, :, :], 0.0).then_inc(zeroed, 1)
                if layer:
                    pool.wait_ge(loaded, 16 * n_loads)
                    pool.tensor_tensor(beta[:, 0:1], beta[:, 0:1], beta[:, 1:2], ALU.add).then_inc(betas, 1)
                    pool.wait_ge(betas, 1)
                    pool.tensor_tensor(beta[:, 0:1], beta[:, 0:1], beta[:, 2:3], ALU.subtract).then_inc(betas, 1)
                    pool.wait_ge(betas, 2)
                    pool.tensor_scalar(table[:, :, :], table[:, :, :], beta[:, 0:1], 0.0, ALU.mult, ALU.add).then_inc(tabled, 1)
                    for h in range(2):
                        weights_low(pool, m, 0, h)
                    for g in range(GROUPS - 1):
                        x_low(pool, m, g)

            @block.tensor
            def _(t):
                t.wait_ge(loaded, 16 * n_loads)
                for e in range(KD):
                    for k in range(KD):
                        ins = t.matmul(m.PS[:, 0, e * BK:(e + 1) * BK], WkT[:, k, e * P:(e + 1) * P], ctxT[:, k, :],
                                       start=k == 0, stop=k == KD - 1)
                ins.then_inc(keys, 1)
                if layer:
                    for k in range(KD):
                        ins = t.matmul(m.PS[:, 3, 0:D], ctxT[:, k, :], WvT[:, k, :], start=k == 0, stop=k == KD - 1)
                    ins.then_inc(valued, 1)
                t.wait_ge(keyed, KD)
                for k in range(KD):
                    for e in range(KD):
                        t.matmul(m.PS[:, 1, k * BK:(k + 1) * BK], Wq[:, e, k * P:(k + 1) * P], KT[:, e, :],
                                 start=e == 0, stop=e == KD - 1)
                for e in range(KD):
                    ins = t.matmul(m.PS[0:1, 2, 0:BK], col(m, bias_q, e), KT[:, e, :], start=e == 0, stop=e == KD - 1)
                ins.then_inc(folded, 1)

                def scores(g):
                    if g >= 2:
                        t.wait_ge(shifted, g - 1)
                    b = g // 2
                    for i in range(4):
                        out = m.PS[:, g % 2, i * KEYS:(i + 1) * KEYS]
                        at = (4 * g + i) * P
                        for k in range(KD):
                            t.matmul(out, m.XT[:, k, at:at + P], A[:, k, b * KEYS:(b + 1) * KEYS], start=k == 0, stop=False)
                        ins = t.matmul(out, m.ones[0:1, :], bqk[0:1, b * KEYS:(b + 1) * KEYS], start=False, stop=True)
                    ins.then_inc(scored, 1)

                def attend(g):
                    t.wait_ge(weighted, g + 1)
                    if g >= 1:
                        t.wait_ge(wcopied, g)
                    for i in range(4):
                        ins = t.transpose(m.PS[:, 2, i * P:(i + 1) * P], W[:, 4 * g + i, :], m.ident[:, :])
                    ins.then_inc(wturned, 1)
                    t.wait_ge(wcopied, g + 1)
                    for u in (2 * g, 2 * g + 1):
                        if u >= 3:
                            t.wait_ge(s.summed, u - 2)
                        for i in range(2):
                            at = (2 * (u % 2) + i) * P
                            ins = t.matmul(m.PS[:, 3 + u % 3, i * D:(i + 1) * D], WT[:, g % 2, at:at + P], VAL[:, :],
                                           start=True, stop=True)
                        ins.then_inc(s.out_done, 1)

                t.wait_ge(ready, 3)
                if layer:
                    t.wait_ge(biased, 1)
                for g in range(GROUPS + 2):
                    if g < GROUPS:
                        scores(g)
                    if 1 <= g <= GROUPS:
                        attend(g - 1)
                    if g >= 2:
                        for u in (2 * g - 4, 2 * g - 3):
                            norm_turn(t, m, s, u, turn_banks)
                    if layer and g >= GROUPS:
                        t.wait_ge(m.gate_loaded, 16)
                        for n in range(3 * (g - GROUPS), 3 + g - GROUPS):
                            t.wait_ge(s.xt_done, 2 * n + 2)
                            gate_logits(t, m, n, 0)

            @block.scalar
            def _(a):
                if layer:
                    for h in range(2):
                        weights_high(a, m, 0, h)
                a.wait_ge(keys, 1)
                for e in range(KD):
                    a.activation(KT[:, e, :], m.PS[:, 0, e * BK:(e + 1) * BK], ACT.Identity,
                                 bias=col(m, bias_k, e)).then_inc(keyed, 1)
                a.wait_ge(folded, 1)
                for k in range(KD):
                    a.activation(A[:, k, :], m.PS[:, 1, k * BK:(k + 1) * BK], ACT.Identity).then_inc(ready, 1)
                a.activation(bqk[0:1, :], m.PS[0:1, 2, 0:BK], ACT.Identity).then_inc(ready, 1)
                for g in range(GROUPS + 2):
                    if g < GROUPS:
                        a.wait_ge(shifted, g + 1)
                        a.activation(S[:, g % 2, :, :], S[:, g % 2, :, :], ACT.Exp).then_inc(raised, 1)
                    if 1 <= g <= GROUPS:
                        a.wait_ge(wturned, g)
                        a.activation(WT[:, (g - 1) % 2, :], m.PS[:, 2, :], ACT.Identity).then_inc(wcopied, 1)
                        for u in (2 * g - 2, 2 * g - 1):
                            norm_root(a, m, s, u)
                        for u in (2 * g - 2, 2 * g - 1):
                            norm_apply(a, m, s, u)
                    if g >= 2:
                        for u in (2 * g - 4, 2 * g - 3):
                            norm_copy(a, m, s, u, turn_banks)
                        if layer:
                            a.wait_ge(s.xt_done, 2 * g - 2)
                            x_high(a, m, g - 2)
                if layer:
                    a.wait_ge(m.logits, GROUPS)
                    a.activation(m.score[:, :, :], m.PS[:, 0, :].rearrange("p (i e) -> p i e", i=TILES),
                                 ACT.Sigmoid).then_inc(m.scored, 1)

            @block.vector
            def _(v):
                dve = Steps(v, step)
                if layer:
                    v.wait_ge(loaded, 16 * n_loads)
                    v.wait_ge(valued, 1)
                    v.tensor_tensor(VAL[:, :], m.PS[:, 3, 0:D], bv[:, :], ALU.add).then_inc(biased, 1)
                    v.wait_ge(tabled, 1)
                v.wait_ge(zeroed, 1)

                def shift(g):
                    v.wait_ge(scored, g + 1)
                    sg = S[:, g % 2, :, :]
                    raw = m.PS[:, g % 2, 0:4 * KEYS].rearrange("p (i n) -> p i n", i=4)
                    if layer:
                        dve.chain(v.scalar_tensor_tensor(sg, raw, float(D) ** -0.5, table[:, 4 * g:4 * g + 4, :],
                                                         ALU.mult, ALU.add))
                        raw = sg
                    dve.chain(v.tensor_reduce(mx[:, g % 2, :], raw, AX.X, ALU.max))
                    v.tensor_tensor(sg, raw, mx[:, g % 2, :].unsqueeze(2).to_broadcast([P, 4, KEYS]),
                                    ALU.subtract).then_inc(shifted, 1)

                def weigh(g):
                    v.wait_ge(raised, g + 1)
                    sg, b = S[:, g % 2, :, :], g // 2
                    dve.chain(v.tensor_reduce(den[:, g % 2, :], sg, AX.X, ALU.add))
                    dve.chain(v.reciprocal(den[:, g % 2, :], den[:, g % 2, :]))
                    v.tensor_tensor(W[:, 4 * g:4 * g + 4, b * KEYS:(b + 1) * KEYS], sg,
                                    den[:, g % 2, :].unsqueeze(2).to_broadcast([P, 4, KEYS]), ALU.mult).then_inc(weighted, 1)

                for g in range(GROUPS + 1):
                    if g < GROUPS:
                        shift(g)
                    if g >= 1:
                        for u in (2 * g - 2, 2 * g - 1):
                            norm_sum(v, dve, m, s, u, 3 + u % 3)
                    if g < GROUPS:
                        weigh(g)
                    if g >= 1:
                        for u in (2 * g - 2, 2 * g - 1):
                            norm_scale(v, dve, s, u)


def cross_attend_0(nc, d, m):
    cross_attend(nc, d, m, 0)


def cross_attend_1(nc, d, m):
    cross_attend(nc, d, m, 1)



def slot_mixer(nc, d, m):
    with ExitStack() as scope:
        m.AL = scope.enter_context(nc.sbuf_tensor("AL", [P, TILES, B * SLOTS], F32))
        m.AT = scope.enter_context(nc.sbuf_tensor("AT", [P, TOK], F32))
        m.SO = scope.enter_context(nc.sbuf_tensor("SO", [P, D], F32))
        for part in SLOT_PARTS:
            part(nc, d, m)


def slot_route(nc, d, m):
    with ExitStack() as scope:
        sem = lambda n: new_semaphore(nc, m, f"sr_{n}")
        sb = lambda n, shape: scope.enter_context(nc.sbuf_tensor(f"sr_{n}", shape, F32))
        w1, w1m, w2, b2 = sb("w1", [P, KD, P]), sb("w1m", [P, KD, P]), sb("w2", [P, SLOTS]), sb("b2", [P, SLOTS])
        slots, tau, mean, bias = sb("slots", [SLOTS, D]), sb("tau", [P, 1]), sb("mean", [P, KD]), sb("bias", [P, 1])
        h, lg, rest = sb("h", [P, 2, BANK]), sb("lg", [P, 2, 4, SLOTS]), sb("rest", [P, 2, 4, SLOTS])
        top, ex, den = sb("top", [P, 2, 4, 8]), sb("ex", [P, 2, 4, SLOTS]), sb("den", [P, 2, 4])
        loaded, zeroed, step, summed, meaned, biasing, biased, hidden, active, routed, shifted, raised, weighted, turned, copied = (
            sem(n) for n in ("loaded", "zeroed", "step", "summed", "meaned", "biasing", "biased", "hidden", "active",
                             "routed", "shifted", "raised", "weighted", "turned", "copied"))
        tau_step = sem("tau")
        with nc.Block(no_gpsimd_drain=True) as block:
            @block.sync
            def _(sp):
                for dst, src in ((w1m[:, :, :], chunks(d["f_w1"][D:2 * D, :])), (w1[:, :, :], chunks(d["f_w1"][0:D, :])),
                                 (slots[:, :], d["slots2"][0:SLOTS, :]), (w2[:, :], d["f_w2"]), (b2[:, :], rows_of(d["f_b2"])),
                                 (tau[:, :], rows_of(d["f_tau"]))):
                    sp.dma_start(dst, src).then_inc(loaded, 16)

            @block.gpsimd
            def _(pool):
                pool.memset(m.AL[:, :, :], 0.0).then_inc(zeroed, 1)

            @block.tensor
            def _(t):
                t.wait_ge(loaded, 96)
                for k in range(KD):
                    ins = t.matmul(m.PS[:, 5, k:k + 1], slots[:, k * P:(k + 1) * P], m.ones[0:SLOTS, 0:1], start=True, stop=True)
                ins.then_inc(summed, 1)
                t.wait_ge(meaned, 1)
                for k in range(KD):
                    ins = t.matmul(m.PS[:, 4, 0:1], w1m[:, k, :], mean[:, k:k + 1], start=k == 0, stop=k == KD - 1)
                ins.then_inc(biasing, 1)

                def hide(g):
                    if g >= 2:
                        t.wait_ge(active, g - 1)
                    for k in range(KD):
                        ins = t.matmul(m.PS[:, g % 2, :], w1[:, k, :], m.XT[:, k, g * BANK:(g + 1) * BANK],
                                       start=k == 0, stop=k == KD - 1)
                    ins.then_inc(hidden, 1)

                def route(g):
                    t.wait_ge(active, g + 1)
                    if g >= 2:
                        t.wait_ge(step, R_STEPS * (g - 2) + 1)
                    for i in range(4):
                        ins = t.matmul(m.PS[:, 2 + g % 2, i * SLOTS:(i + 1) * SLOTS], h[:, g % 2, i * P:(i + 1) * P],
                                       w2[:, :], start=True, stop=True)
                    ins.then_inc(routed, 1)

                def collect(g):
                    t.wait_ge(weighted, g + 1)
                    if g >= 1:
                        t.wait_ge(copied, g)
                    else:
                        t.wait_ge(biased, 1)
                    for i in range(4):
                        ins = t.transpose(m.PS[:, 4, i * P:(i + 1) * P], m.AL[:, 4 * g + i, :], m.ident[:, :])
                    ins.then_inc(turned, 1)
                    for i in range(4 * g, 4 * g + 4):
                        first, last = i == 0, i == TILES - 1
                        t.matmul(m.PS[:, 6, 0:D], m.AL[:, i, :], m.X[:, i, :], start=first, stop=last)
                        t.matmul(m.PS[:, 7, 0:1], m.AL[:, i, :], m.ones[:, 0:1], start=first, stop=last)

                for g in range(GROUPS + 2):
                    if g < GROUPS:
                        hide(g)
                    if 1 <= g <= GROUPS:
                        route(g - 1)
                    if g >= 2:
                        collect(g - 2)

            @block.scalar
            def _(a):
                a.wait_ge(loaded, 96)
                a.activation(tau[:, :], tau[:, :], ACT.Abs).then_inc(tau_step, 1)
                a.wait_ge(summed, 1)
                a.activation(mean[:, :], m.PS[:, 5, 0:KD], ACT.Copy, scale=1.0 / SLOTS).then_inc(meaned, 1)
                a.wait_ge(biasing, 1)
                a.activation(bias[:, :], m.PS[:, 4, 0:1], ACT.Identity, bias=col(m, "f_b1")).then_inc(biased, 1)
                a.wait_ge(biased, 1)
                for g in range(GROUPS + 2):
                    if g < GROUPS:
                        a.wait_ge(hidden, g + 1)
                        if g >= 2:
                            a.wait_ge(routed, g - 1)
                        a.activation(h[:, g % 2, :], m.PS[:, g % 2, :], ACT.Gelu, bias=bias[:, 0:1]).then_inc(active, 1)
                    if 1 <= g <= GROUPS:
                        a.wait_ge(shifted, g)
                        e = ex[:, (g - 1) % 2, :, :]
                        a.activation(e, e, ACT.Exp).then_inc(raised, 1)
                    if g >= 2:
                        a.wait_ge(turned, g - 1)
                        a.activation(m.AT[:, (g - 2) * BANK:(g - 1) * BANK], m.PS[:, 4, :], ACT.Identity).then_inc(copied, 1)

            @block.vector
            def _(v):
                dve = Steps(v, step)
                v.wait_ge(loaded, 96)
                v.wait_ge(zeroed, 1)
                v.wait_ge(tau_step, 1)
                v.tensor_scalar(tau[:, :], tau[:, :], 0.1, None, ALU.add).then_inc(tau_step, 1)
                v.wait_ge(tau_step, 2)
                v.reciprocal(tau[:, :], tau[:, :]).then_inc(tau_step, 1)
                v.wait_ge(tau_step, 3)

                def pick(g):
                    v.wait_ge(routed, g + 1)
                    q, before = g % 2, dve.n
                    wide = lambda x: x.unsqueeze(2).to_broadcast([P, 4, SLOTS])
                    dve.chain(v.tensor_tensor(lg[:, q, :, :], m.PS[:, 2 + q, 0:4 * SLOTS].rearrange("p (i n) -> p i n", i=4),
                                              b2[:, :].unsqueeze(1).to_broadcast([P, 4, SLOTS]), ALU.add))
                    dve.chain(v.tensor_scalar(lg[:, q, :, :], lg[:, q, :, :], tau[:, 0:1], None, ALU.mult))
                    for i in range(4):
                        dve.mark(v.max(top[:, q, i, :], lg[:, q, i, :]))
                    dve.wait()
                    v.tensor_tensor(ex[:, q, :, :], lg[:, q, :, :], wide(top[:, q, :, 0]), ALU.subtract).then_inc(shifted, 1)
                    for i in range(4):
                        dve.mark(v.match_replace(rest[:, q, i, :], top[:, q, i, :], lg[:, q, i, :], LOW))
                    dve.wait()
                    dve.chain(v.tensor_tensor(rest[:, q, :, :], rest[:, q, :, :], lg[:, q, :, :], ALU.not_equal))
                    v.wait_ge(raised, g + 1)
                    dve.chain(v.tensor_tensor(ex[:, q, :, :], ex[:, q, :, :], rest[:, q, :, :], ALU.mult))
                    dve.chain(v.tensor_reduce(den[:, q, :], ex[:, q, :, :], AX.X, ALU.add))
                    dve.chain(v.reciprocal(den[:, q, :], den[:, q, :]))
                    b = g // 2
                    v.tensor_tensor(m.AL[:, 4 * g:4 * g + 4, b * SLOTS:(b + 1) * SLOTS], ex[:, q, :, :], wide(den[:, q, :]),
                                    ALU.mult).then_inc(weighted, 1)
                    assert dve.n - before == R_STEPS

                for g in range(GROUPS):
                    pick(g)


R_STEPS = 14


def slot_update(nc, d, m):
    R = B * SLOTS
    with ExitStack() as scope:
        sem = lambda n: new_semaphore(nc, m, f"su_{n}")
        sb = lambda n, shape: scope.enter_context(nc.sbuf_tensor(f"su_{n}", shape, F32))
        WihT, WhhT, slots, slotsT = sb("wih", [P, KD, 3 * D]), sb("whh", [P, KD, 3 * D]), sb("slots", [P, D]), sb("slotsT", [P, KD, R])
        bih, bhh = sb("bih", [P, 3 * D]), sb("bhh", [P, 3 * D])
        wq, wk, wv, wvp, wo = sb("wq", [P, KD, 64]), sb("wk", [P, KD, 64]), sb("wv", [P, KD, D]), sb("wvp", [P, KD, D]), sb("wo", [P, KD, D])
        bv, ln_g, ln_b, bvp, bo = (sb(n, [P, D]) for n in ("bv", "ln_g", "ln_b", "bvp", "bo"))
        den, si, siT, rz, hn, new, newT = sb("den", [P, 1]), sb("si", [P, D]), sb("siT", [P, KD, R]), sb("rz", [P, 2 * D]), sb("hn", [P, D]), sb("new", [P, D]), sb("newT", [P, KD, R])
        qT, kT, val, mx, ex, sm = sb("qT", [64, R]), sb("kT", [64, R]), sb("val", [P, D]), sb("mx", [P, 1]), sb("ex", [P, SLOTS]), sb("sm", [P, 1])
        AB, ABT, y, st, mv, std = sb("ab", [P, R]), sb("abT", [P, R]), sb("y", [P, D]), sb("st", [P, 6]), sb("mv", [P, 2]), sb("std", [P, 1])
        yT, sv, svT = sb("yT", [P, KD, R]), sb("sv", [P, D]), sb("svT", [P, KD, R])
        loaded, step, zeroed, bo_added = sem("loaded"), sem("step"), sem("zeroed"), sem("bo_added")
        names = ("si", "si_turned", "siT", "gates", "rz_in", "rz", "cell_in", "cell", "new", "new_turned", "newT", "qkv",
                 "qk", "val", "scores", "top", "exps", "ab", "ab_turned", "abT", "comm", "stats", "root", "y",
                 "y_turned", "yT", "values", "sv", "sv_turned", "svT", "out")
        made = {n: sem(n) for n in names}
        loads = ((slotsT[:, :, :], chunks(d["slotsT2"])), (WhhT[:, :, :], chunks(d["f_whhT"])), (WihT[:, :, :], chunks(d["f_wihT"])),
                 (bih[:, :], rows_of(d["f_bih"])), (bhh[:, :], rows_of(d["f_bhh"])), (slots[:, :], d["slots2"]),
                 (wq[:, :, :], chunks(d["f_wq"])), (wk[:, :, :], chunks(d["f_wk"])), (wv[:, :, :], chunks(d["f_wv"])),
                 (bv[:, :], rows_of(d["f_bv"])), (ln_g[:, :], rows_of(d["f_ln_g"])), (ln_b[:, :], rows_of(d["f_ln_b"])),
                 (wvp[:, :, :], chunks(d["f_wvp"])), (bvp[:, :], rows_of(d["f_bvp"])), (wo[:, :, :], chunks(d["f_wo"])),
                 (bo[:, :], rows_of(d["f_bo"])))
        with nc.Block(no_gpsimd_drain=True) as block:
            @block.sync
            def _(sp):
                for dst, src in loads:
                    sp.dma_start(dst, src).then_inc(loaded, 16)

            @block.gpsimd
            def _(pool):
                pool.memset(AB[:, :], 0.0).then_inc(zeroed, 1)
                pool.wait_ge(loaded, 16 * len(loads))
                pool.tensor_tensor(m.X[:, :, :], m.X[:, :, :], bo[:, :].unsqueeze(1).to_broadcast([P, TILES, D]),
                                   ALU.add).then_inc(bo_added, 1)

            @block.tensor
            def _(t):
                def turn(src, bank, done):
                    for k in range(KD):
                        ins = t.transpose(m.PS[:, bank, k * R:(k + 1) * R], src[:, k * P:(k + 1) * P], m.ident[:, :])
                    ins.then_inc(done, 1)

                t.wait_ge(loaded, 16 * len(loads))
                for k in range(KD):
                    t.matmul(m.PS[:, 3, 0:D], slotsT[:, k, :], WhhT[:, k, 2 * D:3 * D], start=k == 0, stop=k == KD - 1)
                for k in range(KD):
                    t.matmul(m.PS[:, 1, :], slotsT[:, k, :], WhhT[:, k, 0:2 * D], start=k == 0, stop=False)
                t.wait_ge(made["si"], 1)
                turn(si, 0, made["si_turned"])
                t.wait_ge(made["siT"], 1)
                for k in range(KD):
                    t.matmul(m.PS[:, 1, :], siT[:, k, :], WihT[:, k, 0:2 * D], start=False, stop=k == KD - 1)
                for k in range(KD):
                    ins = t.matmul(m.PS[:, 2, 0:D], siT[:, k, :], WihT[:, k, 2 * D:3 * D], start=k == 0, stop=k == KD - 1)
                ins.then_inc(made["gates"], 1)
                t.wait_ge(made["new"], 1)
                turn(new, 4, made["new_turned"])
                t.wait_ge(made["newT"], 1)
                for n, w in enumerate((wq, wk)):
                    for k in range(KD):
                        t.matmul(m.PS[0:64, 5, n * R:(n + 1) * R], w[:, k, :], newT[:, k, :], start=k == 0, stop=k == KD - 1)
                for k in range(KD):
                    ins = t.matmul(m.PS[:, 2, 0:D], newT[:, k, :], wv[:, k, :], start=k == 0, stop=k == KD - 1)
                ins.then_inc(made["qkv"], 1)
                t.wait_ge(made["qk"], 2)
                for b in range(B):
                    part = slice(b * SLOTS, (b + 1) * SLOTS)
                    ins = t.matmul(m.PS[part, 3, 0:SLOTS], qT[:, part], kT[:, part], start=True, stop=True)
                ins.then_inc(made["scores"], 1)
                t.wait_ge(made["ab"], 2)
                t.transpose(m.PS[:, 0, 0:R], AB[:, :], m.ident[:, :]).then_inc(made["ab_turned"], 1)
                t.wait_ge(made["abT"], 1)
                t.wait_ge(made["val"], 1)
                t.matmul(m.PS[:, 1, 0:D], ABT[:, :], val[:, :], start=True, stop=True).then_inc(made["comm"], 1)
                t.wait_ge(made["y"], 1)
                turn(y, 4, made["y_turned"])
                t.wait_ge(made["yT"], 1)
                for k in range(KD):
                    ins = t.matmul(m.PS[:, 2, 0:D], yT[:, k, :], wvp[:, k, :], start=k == 0, stop=k == KD - 1)
                ins.then_inc(made["values"], 1)
                t.wait_ge(made["sv"], 1)
                turn(sv, 5, made["sv_turned"])
                t.wait_ge(made["svT"], 1)
                for k in range(KD):
                    ins = t.matmul(m.PS[:, 3, 0:D], svT[:, k, :], wo[:, k, :], start=k == 0, stop=k == KD - 1)
                ins.then_inc(made["out"], 1)

            @block.scalar
            def _(a):
                def copy_turned(dst, bank, turned, done):
                    a.wait_ge(turned, 1)
                    a.activation(dst, m.PS[:, bank, 0:KD * R].rearrange("p (k r) -> p k r", k=KD), ACT.Identity).then_inc(done, 1)

                copy_turned(siT[:, :, :], 0, made["si_turned"], made["siT"])
                a.wait_ge(made["rz_in"], 1)
                a.activation(rz[:, :], rz[:, :], ACT.Sigmoid).then_inc(made["rz"], 1)
                a.wait_ge(made["cell_in"], 1)
                a.activation(hn[:, :], hn[:, :], ACT.Tanh).then_inc(made["cell"], 1)
                copy_turned(newT[:, :, :], 4, made["new_turned"], made["newT"])
                a.wait_ge(made["qkv"], 1)
                for n, (dst, bias) in enumerate(((qT, "f_bq"), (kT, "f_bk"))):
                    a.activation(dst[:, :], m.PS[0:64, 5, n * R:(n + 1) * R], ACT.Identity, bias=col(m, bias, 0, 64)).then_inc(made["qk"], 1)
                a.wait_ge(made["top"], 1)
                a.activation(ex[:, :], m.PS[:, 3, 0:SLOTS], ACT.Exp, bias=mx[:, 0:1], scale=0.125, accum_out=sm[:, 0:1]).then_inc(made["exps"], 1)
                a.wait_ge(made["ab_turned"], 1)
                a.activation(ABT[:, :], m.PS[:, 0, 0:R], ACT.Identity).then_inc(made["abT"], 1)
                a.wait_ge(made["stats"], 1)
                a.activation(std[:, :], mv[:, 1:2], ACT.Sqrt, bias=m.eps[:, 0:1]).then_inc(made["root"], 1)
                copy_turned(yT[:, :, :], 4, made["y_turned"], made["yT"])
                copy_turned(svT[:, :, :], 5, made["sv_turned"], made["svT"])

            @block.vector
            def _(v):
                dve = Steps(v, step)
                tt = v.tensor_tensor
                dve.chain(v.tensor_scalar(den[:, :], m.PS[:, 7, 0:1], 1e-8, None, ALU.add))
                dve.chain(v.reciprocal(den[:, :], den[:, :]))
                v.tensor_scalar(si[:, :], m.PS[:, 6, 0:D], den[:, 0:1], None, ALU.mult).then_inc(made["si"], 1)
                v.wait_ge(loaded, 16 * len(loads))
                dve.chain(tt(bih[:, 0:2 * D], bih[:, 0:2 * D], bhh[:, 0:2 * D], ALU.add))
                v.wait_ge(made["gates"], 1)
                tt(rz[:, :], m.PS[:, 1, :], bih[:, 0:2 * D], ALU.add).then_inc(made["rz_in"], 1)
                dve.mark(tt(hn[:, :], m.PS[:, 3, 0:D], bhh[:, 2 * D:3 * D], ALU.add))
                dve.chain(tt(y[:, :], m.PS[:, 2, 0:D], bih[:, 2 * D:3 * D], ALU.add))
                v.wait_ge(made["rz"], 1)
                dve.chain(tt(hn[:, :], hn[:, :], rz[:, 0:D], ALU.mult))
                tt(hn[:, :], hn[:, :], y[:, :], ALU.add).then_inc(made["cell_in"], 1)
                v.wait_ge(made["cell"], 1)
                dve.chain(tt(new[:, :], slots[:, :], hn[:, :], ALU.subtract))
                dve.chain(tt(new[:, :], new[:, :], rz[:, D:2 * D], ALU.mult))
                tt(new[:, :], new[:, :], hn[:, :], ALU.add).then_inc(made["new"], 1)
                v.wait_ge(made["qkv"], 1)
                tt(val[:, :], m.PS[:, 2, 0:D], bv[:, :], ALU.add).then_inc(made["val"], 1)
                v.wait_ge(made["scores"], 1)
                dve.chain(v.tensor_reduce(mx[:, :], m.PS[:, 3, 0:SLOTS], AX.X, ALU.max))
                v.tensor_scalar(mx[:, :], mx[:, :], -0.125, None, ALU.mult).then_inc(made["top"], 1)
                v.wait_ge(made["exps"], 1)
                v.wait_ge(zeroed, 1)
                dve.chain(v.reciprocal(sm[:, :], sm[:, :]))
                for b in range(B):
                    part = slice(b * SLOTS, (b + 1) * SLOTS)
                    v.tensor_scalar(AB[part, part], ex[part, :], sm[part, 0:1], None, ALU.mult).then_inc(made["ab"], 1)
                v.wait_ge(made["comm"], 1)
                v.wait_ge(made["new"], 1)
                dve.chain(tt(y[:, :], m.PS[:, 1, 0:D], new[:, :], ALU.add))
                dve.chain(v.bn_stats(st[:, :], y[:, :]))
                v.bn_aggr(mv[:, :], st[:, :]).then_inc(made["stats"], 1)
                v.wait_ge(made["root"], 1)
                dve.chain(v.reciprocal(std[:, :], std[:, :]))
                v.wait_ge(made["stats"], 1)
                dve.chain(v.tensor_scalar(y[:, :], y[:, :], mv[:, 0:1], std[:, 0:1], ALU.subtract, ALU.mult))
                dve.chain(tt(y[:, :], y[:, :], ln_g[:, :], ALU.mult))
                tt(y[:, :], y[:, :], ln_b[:, :], ALU.add).then_inc(made["y"], 1)
                v.wait_ge(made["values"], 1)
                tt(sv[:, :], m.PS[:, 2, 0:D], bvp[:, :], ALU.add).then_inc(made["sv"], 1)
                v.wait_ge(bo_added, 1)
                v.wait_ge(made["out"], 1)
                v.tensor_copy(m.SO[:, :], m.PS[:, 3, 0:D])


def slot_out(nc, d, m):
    banks = (4, 5)
    with ExitStack() as scope:
        s = norm_state(nc, m, scope, "so")
        step = new_semaphore(nc, m, "so_step")
        with nc.Block(no_gpsimd_drain=True) as block:
            @block.tensor
            def _(t):
                for u in range(UNITS + 2):
                    if u < UNITS:
                        if u >= 4:
                            t.wait_ge(s.summed, u - 3)
                        for i in range(2):
                            at = (2 * u + i) * P
                            ins = t.matmul(m.PS[:, u % 4, i * D:(i + 1) * D], m.AT[:, at:at + P], m.SO[:, :], start=True, stop=True)
                        ins.then_inc(s.out_done, 1)
                    if u >= 2:
                        norm_turn(t, m, s, u - 2, banks)

            @block.scalar
            def _(a):
                norm_scalar_side(a, m, s, banks)

            @block.vector
            def _(v):
                norm_vector_side(v, Steps(v, step), m, s)


SLOT_PARTS = [slot_route, slot_update, slot_out]


def norm_scalar_side(a, m, s, banks):
    for u in range(UNITS + 2):
        if u < UNITS:
            norm_root(a, m, s, u)
        if 1 <= u <= UNITS:
            norm_apply(a, m, s, u - 1)
        if u >= 2:
            norm_copy(a, m, s, u - 2, banks)


def norm_vector_side(v, dve, m, s):
    for u in range(UNITS + 1):
        if u < UNITS:
            norm_sum(v, dve, m, s, u, u % 4)
        if u >= 1:
            norm_scale(v, dve, s, u - 1)



def axis_attend(nc, d, m):
    J = TILES // B
    with ExitStack() as outer:
        OT = outer.enter_context(nc.sbuf_tensor("OT", [P, KD, TOK], F32))
        with ExitStack() as scope:
            sem = lambda n: new_semaphore(nc, m, f"aa_{n}")
            sb = lambda n, shape: scope.enter_context(nc.sbuf_tensor(f"aa_{n}", shape, F32))
            W, bias = sb("w", [P, KD, 3 * D]), sb("bias", [P, 3 * D])
            qk, val = sb("qk", [P, 2, B, 2 * D]), sb("val", [P, 2, B, D])
            prod, S, mx, den = sb("prod", [P, 2, B, B, D]), sb("s", [P, 2, B, B, HEADS]), sb("mx", [P, 2, B, HEADS]), sb("den", [P, 2, B, HEADS])
            pv, out = sb("pv", [P, B, B, D]), sb("out", [P, 2, B, D])
            loaded, step, projected, biased, shifted, raised, weighted, mixed, attended, turned, copied = (sem(n) for n in (
                "loaded", "step", "projected", "biased", "shifted", "raised", "weighted", "mixed", "attended", "turned", "copied"))
            OTv = OT[:, :, :].rearrange("p k (s j t) -> p k s j t", s=B, j=J)
            with nc.Block(no_gpsimd_drain=True) as block:
                @block.sync
                def _(sp):
                    sp.dma_start(W[:, :, :], chunks(d["a_inT"])).then_inc(loaded, 16)
                    sp.dma_start(bias[:, :], rows_of(d["a_in_b"])).then_inc(loaded, 16)

                @block.tensor
                def _(t):
                    def project(j):
                        if j >= 2:
                            t.wait_ge(biased, 3 * (j - 1))
                        at = 3 * (j % 2)
                        for s in range(B):
                            tile = (j + J * s) * P
                            for k in range(KD):
                                t.matmul(m.PS[:, at + s, :], m.XT[:, k, tile:tile + P], W[:, k, 0:2 * D], start=k == 0, stop=k == KD - 1)
                            for k in range(KD):
                                ins = t.matmul(m.PS[:, at + 2, s * D:(s + 1) * D], m.XT[:, k, tile:tile + P], W[:, k, 2 * D:3 * D],
                                               start=k == 0, stop=k == KD - 1)
                        ins.then_inc(projected, 1)

                    def turn(j):
                        t.wait_ge(attended, j + 1)
                        if j >= 2:
                            t.wait_ge(copied, j - 1)
                        for k in range(KD):
                            for s in range(B):
                                ins = t.transpose(m.PS[:, 6 + j % 2, (2 * k + s) * P:(2 * k + s + 1) * P],
                                                  out[:, j % 2, s, k * P:(k + 1) * P], m.ident[:, :])
                        ins.then_inc(turned, 1)

                    t.wait_ge(loaded, 32)
                    for j in range(J + 2):
                        if j < J:
                            project(j)
                        if j >= 2:
                            turn(j - 2)

                @block.scalar
                def _(a):
                    for j in range(J + 2):
                        if j < J:
                            a.wait_ge(shifted, j + 1)
                            a.activation(S[:, j % 2], S[:, j % 2], ACT.Exp, scale=float(HD) ** -0.5).then_inc(raised, 1)
                        if j >= 2:
                            a.wait_ge(turned, j - 1)
                            a.activation(OTv[:, :, :, j - 2, :], m.PS[:, 6 + j % 2, :].rearrange("p (k s t) -> p k s t", k=KD, s=B),
                                         ACT.Identity).then_inc(copied, 1)

                @block.gpsimd
                def _(pool):
                    for j in range(J):
                        pool.wait_ge(weighted, j + 1)
                        if j >= 1:
                            pool.wait_ge(attended, j)
                        for s in range(B):
                            pool.tensor_tensor(pv[:, s, :, :].rearrange("p t (h c) -> p t h c", h=HEADS),
                                               S[:, j % 2, s, :, :].unsqueeze(3).to_broadcast([P, B, HEADS, HD]),
                                               val[:, j % 2, :, :].rearrange("p t (h c) -> p t h c", h=HEADS), ALU.mult).then_inc(mixed, 1)
                        pool.wait_ge(mixed, 2 * (j + 1))
                        if j >= 2:
                            pool.wait_ge(turned, j - 1)
                        pool.tensor_tensor(out[:, j % 2], pv[:, :, 0, :], pv[:, :, 1, :], ALU.add).then_inc(attended, 1)

                @block.vector
                def _(v):
                    dve = Steps(v, step)
                    v.wait_ge(loaded, 32)

                    def score(j):
                        q = j % 2
                        v.wait_ge(projected, j + 1)
                        if j >= 2:
                            v.wait_ge(attended, j - 1)
                        v.tensor_tensor(qk[:, q, :, :], m.PS[:, 3 * q:3 * q + 2, :],
                                        bias[:, 0:2 * D].unsqueeze(1).to_broadcast([P, B, 2 * D]), ALU.add).then_inc(biased, 2)
                        v.tensor_tensor(val[:, q, :, :], m.PS[:, 3 * q + 2, :].rearrange("p (s n) -> p s n", s=B),
                                        bias[:, 2 * D:].unsqueeze(1).to_broadcast([P, B, D]), ALU.add).then_inc(biased, 1)
                        v.wait_ge(biased, 3 * (j + 1))
                        for s in range(B):
                            dve.mark(v.tensor_tensor(prod[:, q, s, :, :], qk[:, q, s, 0:D].unsqueeze(1).to_broadcast([P, B, D]),
                                                     qk[:, q, :, D:2 * D], ALU.mult))
                        dve.wait()
                        dve.chain(v.tensor_reduce(S[:, q].rearrange("p s t h -> p (s t h)"),
                                                  prod[:, q].rearrange("p s t (h c) -> p (s t h) c", h=HEADS), AX.X, ALU.add))
                        dve.chain(v.tensor_tensor(mx[:, q, :, :], S[:, q, :, 0, :], S[:, q, :, 1, :], ALU.max))
                        v.tensor_tensor(S[:, q], S[:, q], mx[:, q, :, :].unsqueeze(2).to_broadcast([P, B, B, HEADS]),
                                        ALU.subtract).then_inc(shifted, 1)

                    def weigh(j):
                        q = j % 2
                        v.wait_ge(raised, j + 1)
                        dve.chain(v.tensor_tensor(den[:, q, :, :], S[:, q, :, 0, :], S[:, q, :, 1, :], ALU.add))
                        dve.chain(v.reciprocal(den[:, q, :, :], den[:, q, :, :]))
                        v.tensor_tensor(S[:, q], S[:, q], den[:, q, :, :].unsqueeze(2).to_broadcast([P, B, B, HEADS]),
                                        ALU.mult).then_inc(weighted, 1)

                    for j in range(J + 1):
                        if j < J:
                            score(j)
                        if j >= 1:
                            weigh(j - 1)
        axis_out(nc, d, m, OT)


def axis_out(nc, d, m, OT):
    banks = (4, 5)
    with ExitStack() as scope:
        sem = lambda n: new_semaphore(nc, m, f"ao_{n}")
        W = scope.enter_context(nc.sbuf_tensor("ao_w", [P, KD, D], F32))
        bias = scope.enter_context(nc.sbuf_tensor("ao_bias", [P, D], F32))
        s = norm_state(nc, m, scope, "ao")
        loaded, step, biased = sem("loaded"), sem("step"), sem("biased")
        with nc.Block(no_gpsimd_drain=True) as block:
            @block.sync
            def _(sp):
                sp.dma_start(bias[:, :], rows_of(d["a_out_b"])).then_inc(loaded, 16)
                sp.dma_start(W[:, :, :], chunks(d["a_outT"])).then_inc(loaded, 16)

            @block.gpsimd
            def _(pool):
                pool.wait_ge(loaded, 32)
                for u in range(UNITS):
                    xu = m.X[:, 2 * u:2 * u + 2, :]
                    pool.tensor_tensor(xu, xu, bias[:, :].unsqueeze(1).to_broadcast([P, 2, D]), ALU.add).then_inc(biased, 1)

            @block.tensor
            def _(t):
                t.wait_ge(loaded, 32)
                for u in range(UNITS + 2):
                    if u < UNITS:
                        if u >= 4:
                            t.wait_ge(s.summed, u - 3)
                        for i in range(2):
                            at = (2 * u + i) * P
                            for k in range(KD):
                                ins = t.matmul(m.PS[:, u % 4, i * D:(i + 1) * D], OT[:, k, at:at + P], W[:, k, :],
                                               start=k == 0, stop=k == KD - 1)
                        ins.then_inc(s.out_done, 1)
                    if u >= 2:
                        norm_turn(t, m, s, u - 2, banks)

            @block.scalar
            def _(a):
                norm_scalar_side(a, m, s, banks)

            @block.vector
            def _(v):
                dve = Steps(v, step)
                for u in range(UNITS + 1):
                    if u < UNITS:
                        v.wait_ge(biased, u + 1)
                        norm_sum(v, dve, m, s, u, u % 4)
                    if u >= 1:
                        norm_scale(v, dve, s, u - 1)



def expert_weights(nc, m, mem):
    sb = lambda n, shape, dt=F32: mem.enter_context(nc.sbuf_tensor(n, shape, dt))
    m.XS = [sb(f"XT_{z}", [P, KD, TOK], F32R) for z in ("high", "low")]
    m.GU, m.DN = [sb(f"gu{h}", [P, KD, 2 * P]) for h in range(2)], [sb(f"dn{h}", [P, D]) for h in range(2)]
    m.GUS = [[sb(f"gu{h}{z}", [P, KD, 2 * P], F32R) for z in ("high", "low")] for h in range(2)]
    m.DNS = [[sb(f"dn{h}{z}", [P, D], F32R) for z in ("high", "low")] for h in range(2)]
    m.gate, m.score = sb("gate", [P, KD, EXPERTS]), sb("score", [P, TILES, EXPERTS])
    m.w_loaded, m.w_high, m.w_split = ([new_semaphore(nc, m, f"w_{n}{h}") for h in range(2)] for n in ("loaded", "high", "split"))
    m.gate_loaded, m.logits, m.x_high, m.x_low, m.scored = (
        new_semaphore(nc, m, n) for n in ("gate_loaded", "logits", "x_high", "x_low", "scored"))


def load_expert(sp, d, m, it, h):
    sp.dma_start(m.GU[h][:, :, :], d["guT"][2 * it + h].rearrange("(k p) n -> p k n", p=P)).then_inc(m.w_loaded[h], 16)
    sp.dma_start(m.DN[h][:, :], d["dnT"][2 * it + h]).then_inc(m.w_loaded[h], 16)


def weights_high(a, m, it, h):
    a.wait_ge(m.w_loaded[h], it * 32 + 32)
    for dst, src in ((m.GUS[h][0], m.GU[h]), (m.DNS[h][0], m.DN[h])):
        a.activation(dst[:], src[:], ACT.Copy).then_inc(m.w_high[h], 1)


def weights_low(pool, m, it, h):
    pool.wait_ge(m.w_high[h], 2 * it + 2)
    for dst, src in ((m.GUS[h], m.GU[h]), (m.DNS[h], m.DN[h])):
        pool.tensor_tensor(dst[1][:], src[:], dst[0][:].bitcast(F32), ALU.subtract).then_inc(m.w_split[h], 1)


def x_high(a, m, g):
    part = slice(g * BANK, (g + 1) * BANK)
    a.activation(m.XS[0][:, :, part], m.XT[:, :, part], ACT.Copy).then_inc(m.x_high, 1)


def x_low(pool, m, g):
    part = slice(g * BANK, (g + 1) * BANK)
    pool.wait_ge(m.x_high, g + 1)
    pool.tensor_tensor(m.XS[1][:, :, part], m.XT[:, :, part], m.XS[0][:, :, part].bitcast(F32),
                       ALU.subtract).then_inc(m.x_low, 1)


def gate_logits(t, m, g, bank):
    for i in range(4 * g, 4 * g + 4):
        for k in range(KD):
            ins = t.matmul(m.PS[:, bank, i * EXPERTS:(i + 1) * EXPERTS], m.XT[:, k, i * P:(i + 1) * P], m.gate[:, k, :],
                           start=k == 0, stop=k == KD - 1)
    ins.then_inc(m.logits, 1)


def experts(nc, d, m):
    ROUNDS = ALL_E // 2
    UPR = 2 * GROUPS
    GS = EXPERTS // GROUPS_E
    PARTS = ((0, 0), (0, 1), (1, 0))
    out = d["out"].rearrange("(i p) d -> p i d", p=P)
    with ExitStack() as scope:
        sem = lambda n: new_semaphore(nc, m, f"ex_{n}")
        sb = lambda n, shape, dt=F32: scope.enter_context(nc.sbuf_tensor(f"ex_{n}", shape, dt))
        C = sb("c", [P, TILES, EXPERTS])
        SI, H = sb("si", [P, 2, BANK]), sb("h", [P, 2, BANK])
        HS = [sb(f"h{z}", [P, 2, BANK], F32R) for z in ("high", "low")]
        ebias, biased_score = sb("ebias", [P, EXPERTS]), sb("biased", [P, TILES, EXPERTS])
        group, group_rest, group_top = sb("group", [P, TILES, 12]), sb("group_rest", [P, TILES, 12]), sb("group_top", [P, TILES, 8])
        masked, rest, top, den = sb("masked", [P, TILES, EXPERTS + 2]), sb("rest", [P, TILES, EXPERTS + 2]), sb("top", [P, TILES, 8]), sb("den", [P, TILES])
        s = norm_state(nc, m, scope, "ln")
        gu_done, silu_done, prod_done, high_done, h_done, down_done, acc_done = (
            sem(n) for n in ("gu", "silu", "prod", "high", "h", "down", "acc"))
        loaded, step, stored = sem("loaded"), sem("step"), sem("stored")
        with nc.Block(no_gpsimd_drain=True) as block:
            @block.sync
            def _(sp):
                sp.dma_start(ebias[:, :], rows_of(d["e_bias"])).then_inc(loaded, 16)
                with sp.Fori(1, ROUNDS) as it:
                    for h in range(2):
                        sp.wait_ge(m.w_split[h], 2 * it)
                        load_expert(sp, d, m, it, h)
                for u in range(0, UNITS, 2):
                    sp.wait_ge(s.normed, 2 * u + 4)
                    sp.dma_start(out[:, 2 * u:2 * u + 4, :], m.X[:, 2 * u:2 * u + 4, :]).then_inc(stored, 16)
                sp.wait_ge(stored, 16 * UNITS // 2)

            @block.gpsimd
            def _(pool):
                x_low(pool, m, GROUPS - 1)
                with pool.Fori(1, ROUNDS) as it:
                    for h in range(2):
                        weights_low(pool, m, it, h)

            @block.tensor
            def _(t):
                def gate_up(it, u, first=False):
                    h, g = divmod(u, GROUPS)
                    if g == 0:
                        t.wait_ge(m.w_split[h], 2 * it + 2)
                    if not first:
                        t.wait_ge(prod_done, it * UPR + (u - 1))
                    for part in range(2):
                        for k in range(KD):
                            for n, (w, x) in enumerate(PARTS):
                                ins = t.matmul(m.PS[:, 2 * part + u % 2, :], m.GUS[h][w][:, k, part * P:(part + 1) * P],
                                               m.XS[x][:, k, g * BANK:(g + 1) * BANK],
                                               start=k == 0 and n == 0, stop=k == KD - 1 and n == 2)
                    ins.then_inc(gu_done, 1)

                def down(it, u):
                    h = u // GROUPS
                    n = it * UPR + u
                    t.wait_ge(h_done, n + 1)
                    t.wait_ge(acc_done, n + 1)
                    for i in range(4):
                        for z, (a_, w) in enumerate(PARTS):
                            ins = t.matmul(m.PS[:, 4 + 2 * (u % 2) + i // 2, (i % 2) * D:(i % 2 + 1) * D],
                                           HS[a_][:, u % 2, i * P:(i + 1) * P], m.DNS[h][w][:, :], start=z == 0, stop=z == 2)
                    ins.then_inc(down_done, 1)

                def unit(it, u, ahead=True):
                    if u + 2 < UPR:
                        gate_up(it, u + 2)
                    elif ahead:
                        gate_up(it + 1, u + 2 - UPR)
                    down(it, u)

                t.wait_ge(m.x_low, GROUPS - 1)
                gate_up(0, 0, first=True)
                gate_up(0, 1, first=True)
                t.wait_ge(m.x_low, GROUPS)
                with t.Fori(0, ROUNDS - 1) as it:
                    for u in range(UPR):
                        unit(it, u)
                for u in range(UPR):
                    unit(ROUNDS - 1, u, ahead=False)

            @block.scalar
            def _(a):
                def silu(it, u):
                    a.wait_ge(gu_done, it * UPR + (u + 1))
                    a.activation(SI[:, u % 2, :], m.PS[:, u % 2, :], ACT.Silu).then_inc(silu_done, 1)

                def high(it, u):
                    a.wait_ge(prod_done, it * UPR + (u + 1))
                    a.activation(HS[0][:, u % 2, :], H[:, u % 2, :], ACT.Copy).then_inc(high_done, 1)

                def next_weights(it, h):
                    a.wait_ge(down_done, it * UPR - (UPR - GROUPS * (h + 1)))
                    weights_high(a, m, it, h)

                def turn(it, first=False, last=False):
                    for u in range(UPR):
                        if u + 1 < UPR:
                            silu(it, u + 1)
                        elif not last:
                            silu(it + 1, 0)
                        high(it, u)
                        if u == 0 and not first:
                            next_weights(it, 1)
                        if u == GROUPS and not last:
                            next_weights(it + 1, 0)

                silu(0, 0)
                turn(0, first=True)
                with a.Fori(1, ROUNDS - 1) as it:
                    turn(it)
                turn(ROUNDS - 1, last=True)
                for u in range(UNITS + 1):
                    if u < UNITS:
                        norm_root(a, m, s, u)
                    if u >= 1:
                        norm_apply(a, m, s, u - 1)

            @block.vector
            def _(v):
                dve = Steps(v, step)

                def product(it, u):
                    v.wait_ge(silu_done, it * UPR + (u + 1))
                    v.tensor_tensor(H[:, u % 2, :], m.PS[:, 2 + u % 2, :], SI[:, u % 2, :], ALU.mult).then_inc(prod_done, 1)

                def low(it, u):
                    v.wait_ge(high_done, it * UPR + (u + 1))
                    v.tensor_tensor(HS[1][:, u % 2, :], H[:, u % 2, :], HS[0][:, u % 2, :].bitcast(F32),
                                    ALU.subtract).then_inc(h_done, 1)

                def accumulate(it, u, half, shared=False):
                    h, g = divmod(u, GROUPS)
                    if half == 0:
                        v.wait_ge(down_done, it * UPR + (u + 1))
                    for i in (2 * half, 2 * half + 1):
                        x = m.X[:, 4 * g + i, :]
                        y = m.PS[:, 4 + 2 * (u % 2) + i // 2, (i % 2) * D:(i % 2 + 1) * D]
                        if shared:
                            ins = v.tensor_tensor(x, y, x, ALU.add)
                        else:
                            ins = v.scalar_tensor_tensor(x, y, C[:, 4 * g + i, bass.ds(it * 2 + (h - SHARED), 1)], x,
                                                         ALU.mult, ALU.add)
                    if half == 1:
                        ins.then_inc(acc_done, 1)

                def unit(it, u, shared=False, last=False):
                    nxt = (it, u + 1) if u + 1 < UPR else (it + 1, 0)
                    more = u + 1 < UPR or not last
                    if more:
                        product(*nxt)
                    accumulate(it, u, 0, shared)
                    if more:
                        low(*nxt)
                    accumulate(it, u, 1, shared)

                grouped = lambda x: x.rearrange("p i (g e) -> p i g e", g=GROUPS_E)

                def route(n):
                    if n == 0:
                        dve.chain(v.tensor_tensor(biased_score[:, :, :], m.score[:, :, :],
                                                  ebias[:, :].unsqueeze(1).to_broadcast([P, TILES, EXPERTS]), ALU.add))
                        dve.chain(v.tensor_reduce(group[:, :, 0:GROUPS_E], grouped(biased_score[:, :, :]), AX.X, ALU.max))
                        for i in range(TILES):
                            dve.mark(v.max(group_top[:, i, :], group[:, i, 0:GROUPS_E]))
                        dve.wait()
                    elif n == 1:
                        dve.chain(v.memset(group_top[:, :, TOP_GROUPS:8], LOW))
                        for i in range(TILES):
                            dve.mark(v.match_replace(group_rest[:, i, :], group_top[:, i, :], group[:, i, :], HIGH))
                        dve.wait()
                    elif n == 2:
                        dve.chain(v.tensor_tensor(group_rest[:, :, :], group_rest[:, :, :], group[:, :, :], ALU.not_equal))
                        dve.chain(v.tensor_tensor(grouped(masked[:, :, 0:EXPERTS]), grouped(biased_score[:, :, :]),
                                                  group_rest[:, :, 0:GROUPS_E].unsqueeze(3).to_broadcast([P, TILES, GROUPS_E, GS]),
                                                  ALU.mult))
                        dve.chain(v.tensor_scalar(masked[:, :, 0:EXPERTS], masked[:, :, 0:EXPERTS], 0.0, None, ALU.add))
                    elif n == 3:
                        for i in range(TILES):
                            dve.mark(v.max(top[:, i, :], masked[:, i, 0:EXPERTS]))
                        dve.wait()
                    elif n == 4:
                        dve.chain(v.memset(top[:, :, TOP_E:8], LOW))
                        for i in range(TILES):
                            dve.mark(v.match_replace(rest[:, i, :], top[:, i, :], masked[:, i, :], HIGH))
                        dve.wait()
                    elif n == 5:
                        dve.chain(v.tensor_tensor(rest[:, :, 0:EXPERTS], rest[:, :, 0:EXPERTS], masked[:, :, 0:EXPERTS], ALU.not_equal))
                        dve.chain(v.tensor_tensor(m.score[:, :, :], m.score[:, :, :], rest[:, :, 0:EXPERTS], ALU.mult))
                        dve.chain(v.tensor_reduce(den[:, :], m.score[:, :, :], AX.X, ALU.add))
                    elif n == 6:
                        dve.chain(v.tensor_scalar(den[:, :], den[:, :], 1e-20, None, ALU.add))
                        dve.chain(v.reciprocal(den[:, :], den[:, :]))
                        dve.chain(v.tensor_scalar(den[:, :], den[:, :], 2.5, None, ALU.mult))
                        dve.chain(v.tensor_tensor(C[:, :, :], m.score[:, :, :],
                                                  den[:, :].unsqueeze(2).to_broadcast([P, TILES, EXPERTS]), ALU.mult))

                v.sem_inc(acc_done, 2)
                dve.mark(v.memset(group[:, :, GROUPS_E:12], LOW))
                dve.mark(v.memset(masked[:, :, EXPERTS:EXPERTS + 2], LOW))
                product(0, 0)
                low(0, 0)
                v.wait_ge(loaded, 16)
                for u in range(UPR):
                    unit(0, u, shared=True)
                    route(u)
                with v.Fori(1, ROUNDS - 1) as it:
                    for u in range(UPR):
                        unit(it, u)
                for u in range(UPR):
                    unit(ROUNDS - 1, u, last=True)
                    if u >= GROUPS:
                        g = u - GROUPS
                        v.wait_ge(acc_done, ROUNDS * UPR - UPR + u + 3)
                        for n in (2 * g, 2 * g + 1):
                            norm_sum(v, dve, m, s, n, None)
                    if u >= UPR - 2:
                        done = UNITS // 2 if u == UPR - 2 else UNITS
                        for n in range(done - UNITS // 2, done):
                            norm_scale(v, dve, s, n)


STAGES = [hyena_prepare, hyena_convolve, hyena_out, cross_attend_0, slot_mixer, axis_attend,
          cross_attend_1, experts]


def build(nc, d):
    with ExitStack() as mem:
        m = Record()
        m.semaphores = []
        sb = lambda n, shape: mem.enter_context(nc.sbuf_tensor(n, shape, F32))
        m.X, m.XT = sb("X", [P, TILES, D]), sb("XT", [P, KD, TOK])
        m.ident, m.cols, m.eps, m.ones = sb("ident", [P, P]), sb("cols", [P, NCOLS]), sb("eps", [P, 1]), sb("ones", [P, P])
        m.PS = mem.enter_context(nc.psum_tensor("PS", [P, 8, BANK], F32))
        with ExitStack() as hyena:
            m.V = hyena.enter_context(nc.sbuf_tensor("V", [P, 3, BLOCKS, B * D], F32))
            m.FW, m.IV = (hyena.enter_context(nc.sbuf_tensor(n, [P, CLASSES, 3, P], F32)) for n in ("FW", "IV"))
            m.transforms_loaded = new_semaphore(nc, m, "transforms_loaded")
            m.H = m.X[:, :, :].rearrange("p i d -> p (i d)").rearrange("p (a n) -> p a n", n=BANK)
            for stage in STAGES[:3]:
                stage(nc, d, m)
        for stage in STAGES[3:5]:
            stage(nc, d, m)
        end_layer(nc, m)
        STAGES[5](nc, d, m)
        expert_weights(nc, m, mem)
        for stage in STAGES[6:]:
            stage(nc, d, m)


def constants():
    f4 = np.float32
    t = np.arange(L, dtype=f4) / f4(L - 1)
    bands = np.arange(EMB, dtype=f4)
    arg = ((t[:, None] * bands[None, :]).astype(f4) * f4(FREQ)).astype(f4)
    peT = np.sin(arg.astype(np.float64)).astype(f4).T
    negt = -t.reshape(BLOCKS, P).T
    p, r, c = np.arange(P)[:, None, None], np.arange(P)[None, None, :], np.arange(CLASSES)[None, :, None]
    turn = (p * (2 * (c + 16 * r) + 1)) % (4 * L) * (np.pi / (2 * L))
    forward = np.stack([np.cos(turn), np.sin(turn), -np.sin(turn)], axis=2)
    inverse = np.ascontiguousarray(forward.transpose(3, 1, 2, 0)) / (L * L)
    return {"peT": peT, "negt": negt, "forward": forward, "inverse": inverse, "ident": np.eye(P)}


def expert_gates(g):
    own = g["L1_ffn_experts_gate_up"].transpose(0, 2, 1)
    gate, up = (g[f"L1_ffn_shared_{n}_w"].reshape(SHARED, P, D) for n in ("gate", "up"))
    return np.concatenate([np.concatenate([gate, up], axis=1).transpose(0, 2, 1), own])


def expert_downs(g):
    own = g["L1_ffn_experts_down"].transpose(0, 2, 1)
    return np.concatenate([g["L1_ffn_shared_down_w"].T.reshape(SHARED, P, D), own])


def kernel(**inputs):
    import concourse.bacc as bacc
    from concourse.bass_utils import run_bass_kernel_spmd

    g = {k: np.asarray(v) for k, v in inputs.items()}
    cols = np.zeros((P, NCOLS), np.float32)
    for name, source in (("b_in", "L0_attn_b_in"), ("conv_b", "L0_attn_conv_b"), ("hy_b1", "L0_attn_b1"),
                         ("x0_bq", "L0_xattn_bq"), ("x0_bk", "L0_xattn_bk"), ("f_b1", "L0_ffn_b1"),
                         ("f_bq", "L0_ffn_bq"), ("f_bk", "L0_ffn_bk"), ("x1_bq", "L1_xattn_bq"), ("x1_bk", "L1_xattn_bk")):
        at, n = COLS[name]
        part = g[source].reshape(n, -1).T
        cols[:part.shape[0], at:at + n] = part
    at, n = COLS["conv_w"]
    cols[:, at:at + n] = g["L0_attn_conv_w"].reshape(6, P, 3).transpose(1, 0, 2).reshape(P, 18)
    x = g["x"].reshape(TOK, D)
    arrays = {
        "x": x, "xT": x.T, "cols": cols,
        "hy_w_inT": g["L0_attn_w_in"].T, "hy_w1T": g["L0_attn_w1"].T, "hy_w2T": g["L0_attn_w2"].T,
        "hy_b2": g["L0_attn_b2"], "hy_decay": g["L0_attn_filt_decay"].reshape(-1),
        "hy_fbias": g["L0_attn_filt_bias"].reshape(-1), "hy_w_outT": g["L0_attn_w_out"].T, "hy_b_out": g["L0_attn_b_out"],
        "ctx": g["ctx_1024"].reshape(B * KEYS, D), "ctxT": g["ctx_1024"].reshape(B * KEYS, D).T,
        "wkT0": g["L0_xattn_Wk"].T, "wq0": g["L0_xattn_Wq"], "wkT1": g["L1_xattn_Wk"].T, "wq1": g["L1_xattn_Wq"],
        "wvT": g["L1_xattn_Wv"].T, "bv": g["L1_xattn_bv"], "table": g["fside_BxSxS2_0"].reshape(TOK, KEYS),
        "betas": np.stack([g[f"L1_xattn_beta_{n}"].reshape(()) for n in ("risk", "prio", "impl")]),
        "slots2": np.tile(g["L0_ffn_slot_init"], (B, 1)), "slotsT2": np.tile(g["L0_ffn_slot_init"], (B, 1)).T,
        "f_wihT": g["L0_ffn_Wih"].T, "f_whhT": g["L0_ffn_Whh"].T,
        **{f"f_{n}": g[f"L0_ffn_{n}"] for n in ("w1", "w2", "b2", "tau", "bih", "bhh", "wq", "wk", "wv", "bv",
                                                "ln_g", "ln_b", "wvp", "bvp", "wo", "bo")},
        "a_inT": g["L1_attn_in_proj_w"].T, "a_in_b": g["L1_attn_in_proj_b"],
        "a_outT": g["L1_attn_out_proj_w"].T, "a_out_b": g["L1_attn_out_proj_b"],
        "gateT": g["L1_ffn_gate_weight"].T, "e_bias": g["L1_ffn_e_score_correction_bias"],
        "guT": expert_gates(g), "dnT": expert_downs(g),
        **constants(),
    }
    nc = bacc.Bacc("TRN2", target_bir_lowering=False, num_devices=1)
    d, fed = {}, {}
    for name, a in arrays.items():
        fed[f"in_{name}"] = np.ascontiguousarray(a, dtype=np.float32)
        d[name] = nc.dram_tensor(f"in_{name}", fed[f"in_{name}"].shape, F32, kind="ExternalInput").ap()
    d["out"] = nc.dram_tensor("out", (TOK, D), F32, kind="ExternalOutput").ap()
    build(nc, d)
    r = run_bass_kernel_spmd(nc, [fed], core_ids=[0])
    return r.results[0]["out"].reshape(B, L, D)
```

```python
from contextlib import ExitStack
import math

import numpy as np
import concourse.bass as bass
from concourse import mybir

F32 = mybir.dt.float32
F32R = mybir.dt.float32r
ALU = mybir.AluOpType
ACT = mybir.ActivationFunctionType
AX = mybir.AxisListType

B, L, D = 2, 1024, 256
TOK = B * L
P = 128
TILES = TOK // P
UNITS = TILES // 2
GROUPS = TILES // 4
KD = D // P
BANK = 512
BLOCKS = L // P
CLASSES = BLOCKS
KEYS = 64
SLOTS, TOP_SLOTS = 64, 8
HEADS, HD = 16, 16
EXPERTS, GROUPS_E, TOP_GROUPS, TOP_E = 32, 8, 4, 6
SHARED = 2
ALL_E = EXPERTS + SHARED
EMB = 33
WARM_UPS = 2
FREQ = 10.0
EPS = 1e-5
LOW, HIGH = -3.0e38, 3.0e38

COLS, _at = {}, 0
for _name, _n in (("b_in", 6), ("conv_w", 18), ("conv_b", 6), ("hy_b1", 1), ("x0_bq", 2), ("x0_bk", 2),
                  ("f_b1", 1), ("f_bq", 1), ("f_bk", 1), ("x1_bq", 2), ("x1_bk", 2)):
    COLS[_name] = (_at, _n)
    _at += _n
NCOLS = _at


class Record:
    pass


class Steps:

    def __init__(self, eng, sem):
        self.eng, self.sem, self.n = eng, sem, 0

    def mark(self, ins):
        ins.then_inc(self.sem, 1)
        self.n += 1
        return self.n

    def wait(self, value=None):
        self.eng.wait_ge(self.sem, self.n if value is None else value)

    def chain(self, ins):
        self.mark(ins)
        self.wait()


def new_semaphore(nc, m, name):
    m.semaphores.append(nc.alloc_semaphore(name))
    return m.semaphores[-1]


def end_layer(nc, m):
    nc.clear_and_free_semaphores(m.semaphores)
    m.semaphores = []
    nc.all_engine_barrier()


def weights(nc, m, scope, tag, parts, flat=None):
    at = 0
    w = Record()
    w.pairs = []
    w.by_name = {}
    for name, shape, source in parts:
        if flat is None:
            buffer = scope.enter_context(nc.sbuf_tensor(f"{tag}_{name}", shape, F32))[:]
        else:
            size = math.prod(shape[1:])
            buffer = flat[:, at:at + size]
            if len(shape) == 3:
                buffer = buffer.rearrange("p (k n) -> p k n", k=shape[1])
            at += size
        w.by_name[name] = buffer
        w.pairs.append((buffer, source))
    w.loaded = nc.alloc_semaphore(f"{tag}_loaded") if flat is not None else new_semaphore(nc, m, f"{tag}_loaded")
    w.count = 16 * len(parts)
    return w


def load(sp, w):
    for buffer, source in w.pairs:
        sp.dma_start(buffer, source).then_inc(w.loaded, 16)


def buffers(w, names):
    return [w.by_name[name] for name in names.split()]


def hyena_out_weights(nc, d, m, scope):
    m.w_hyena_out = weights(nc, m, scope, "ho", (("w", [P, KD, D], chunks(d["hy_w_outT"])),
                                                 ("bias", [P, D], rows_of(d["hy_b_out"]))))


def cross_weights(nc, d, m, scope, layer):
    parts = [("wkT", [P, KD, D], chunks(d[f"wkT{layer}"])), ("ctxT", [P, KD, B * KEYS], chunks(d["ctxT"])),
             ("wq", [P, KD, D], chunks(d[f"wq{layer}"]))]
    if layer:
        parts += [("wvT", [P, KD, D], chunks(d["wvT"])), ("bv", [P, D], rows_of(d["bv"])),
                  ("beta", [P, 3], rows_of(d["betas"])),
                  ("table", [P, TILES, KEYS], d["table"].rearrange("(i p) n -> p i n", p=P))]
    else:
        parts += [("val", [P, D], d["ctx"])]
    m.w_cross = w = weights(nc, m, scope, f"x{layer}", parts)
    sb = lambda n, shape: scope.enter_context(nc.sbuf_tensor(f"x{layer}_{n}", shape, F32))
    w.layer = layer
    w.KT = sb("kT", [P, KD, B * KEYS])
    w.A = sb("a", [P, KD + 1, B * KEYS])
    w.bq = sb("bq_wide", [P, KD, P])
    w.widened, w.keys, w.keyed, w.folded, w.ready = (new_semaphore(nc, m, f"x{layer}_{n}") for n in (
        "widened", "keys", "keyed", "folded", "ready"))


def widen_bq(pool, m):
    for e in range(KD):
        pool.tensor_scalar(m.w_cross.bq[:, e, :], m.ones[:, :], col(m, f"x{m.w_cross.layer}_bq", e), 0.0,
                           ALU.mult, ALU.add).then_inc(m.w_cross.widened, 1)


def make_keys(t, m, bank):
    w, BK = m.w_cross, B * KEYS
    WkT, ctxT = buffers(w, "wkT ctxT")
    t.wait_ge(w.loaded, w.count)
    for e in range(KD):
        for k in range(KD):
            ins = t.matmul(m.PS[:, bank, e * BK:(e + 1) * BK], WkT[:, k, e * P:(e + 1) * P], ctxT[:, k, :],
                           start=k == 0, stop=k == KD - 1)
    ins.then_inc(w.keys, 1)


def copy_keys(a, m, bank):
    w, BK = m.w_cross, B * KEYS
    a.wait_ge(w.keys, 1)
    for e in range(KD):
        a.activation(w.KT[:, e, :], m.PS[:, bank, e * BK:(e + 1) * BK], ACT.Identity,
                     bias=col(m, f"x{w.layer}_bk", e)).then_inc(w.keyed, 1)


def fold_queries(t, m, bank):
    w, BK = m.w_cross, B * KEYS
    Wq, = buffers(w, "wq")
    t.wait_ge(w.keyed, KD)
    t.wait_ge(w.widened, KD)
    for k in range(KD):
        for e in range(KD):
            t.matmul(m.PS[:, bank, k * BK:(k + 1) * BK], Wq[:, e, k * P:(k + 1) * P], w.KT[:, e, :],
                     start=e == 0, stop=e == KD - 1)
    for e in range(KD):
        ins = t.matmul(m.PS[:, bank, KD * BK:(KD + 1) * BK], w.bq[:, e, :], w.KT[:, e, :], start=e == 0, stop=e == KD - 1)
    ins.then_inc(w.folded, 1)


def copy_folded(a, m, bank):
    w, BK = m.w_cross, B * KEYS
    a.wait_ge(w.folded, 1)
    a.activation(w.A[:, :, :], m.PS[:, bank, 0:(KD + 1) * BK].rearrange("p (k n) -> p k n", k=KD + 1),
                 ACT.Identity).then_inc(w.ready, 1)


def slot_weights(nc, d, m, scope):
    R = B * SLOTS
    m.w_route = weights(nc, m, scope, "sr", (
        ("w1m", [P, KD, P], chunks(d["f_w1"][D:2 * D, :])), ("w1", [P, KD, P], chunks(d["f_w1"][0:D, :])),
        ("slots", [SLOTS, D], d["slots2"][0:SLOTS, :]), ("w2", [P, SLOTS], d["f_w2"]), ("b2", [P, SLOTS], rows_of(d["f_b2"])),
        ("tau", [P, 1], rows_of(d["f_tau"]))))
    m.w_update = weights(nc, m, scope, "su", (
        ("slotsT", [P, KD, R], chunks(d["slotsT2"])), ("whh", [P, KD, 3 * D], chunks(d["f_whhT"])),
        ("wih", [P, KD, 3 * D], chunks(d["f_wihT"])), ("bih", [P, 3 * D], rows_of(d["f_bih"])),
        ("bhh", [P, 3 * D], rows_of(d["f_bhh"])), ("slots", [P, D], d["slots2"]),
        ("wq", [P, KD, 64], chunks(d["f_wq"])), ("wk", [P, KD, 64], chunks(d["f_wk"])), ("wv", [P, KD, D], chunks(d["f_wv"])),
        ("bv", [P, D], rows_of(d["f_bv"])), ("ln_g", [P, D], rows_of(d["f_ln_g"])), ("ln_b", [P, D], rows_of(d["f_ln_b"])),
        ("wvp", [P, KD, D], chunks(d["f_wvp"])), ("bvp", [P, D], rows_of(d["f_bvp"])), ("wo", [P, KD, D], chunks(d["f_wo"])),
        ("bo", [P, D], rows_of(d["f_bo"]))))


def axis_weights(nc, d, m):
    fw, iv = (x[:, :, :, :].rearrange("p c z n -> p (c z n)") for x in (m.FW, m.IV))
    m.w_axis = weights(nc, m, None, "aa", (("w", [P, KD, 3 * D], chunks(d["a_inT"])),
                                           ("bias", [P, 3 * D], rows_of(d["a_in_b"]))), flat=fw)
    m.w_axis_out = weights(nc, m, None, "ao", (("w", [P, KD, D], chunks(d["a_outT"])),
                                               ("bias", [P, D], rows_of(d["a_out_b"]))), flat=iv)


def col(m, name, j=0, rows=P):
    at = COLS[name][0] + j
    return m.cols[0:rows, at:at + 1]


def rows_of(vector, n=P):
    return vector.rearrange("(o n) -> o n", o=1).to_broadcast([n, vector.shape[0]])


def chunks(matrix):
    return matrix.rearrange("(k p) n -> p k n", p=P)


def warm_up(t, m, bank, rhs, count=WARM_UPS):
    for _ in range(count):
        t.matmul(m.PS[:, bank, :], m.ident[:, :], rhs, start=True, stop=True)



def load_table(a, m, function):
    at = m.tables_loaded = m.tables_loaded + 1
    a.activation(m.unread[:, at:at + 1], m.eps[:, 0:1], function)


def norm_state(nc, m, scope, tag):
    s = Record()
    s.st = scope.enter_context(nc.sbuf_tensor(f"{tag}_st", [P, 2, 2, 6], F32))
    s.mv = scope.enter_context(nc.sbuf_tensor(f"{tag}_mv", [P, UNITS, 2, 2], F32))
    s.std = scope.enter_context(nc.sbuf_tensor(f"{tag}_std", [P, UNITS, 2], F32))
    s.rstd = scope.enter_context(nc.sbuf_tensor(f"{tag}_rstd", [P, UNITS, 2], F32))
    s.shift = scope.enter_context(nc.sbuf_tensor(f"{tag}_shift", [P, UNITS, 2], F32))
    s.out_done, s.summed, s.stats, s.root, s.scaled, s.normed_first, s.normed_second, s.turned, s.xt_done = (
        new_semaphore(nc, m, f"{tag}_{n}") for n in
        ("out_done", "summed", "stats", "root", "scaled", "normed_first", "normed_second", "turned", "xt_done"))
    return s


def norm_sum(v, dve, m, s, u, bank, first=lambda: None):
    x = m.X[:, 2 * u:2 * u + 2, :]
    if bank is not None:
        v.wait_ge(s.out_done, u + 1)
        first()
        v.tensor_tensor(x, m.PS[:, bank, :].rearrange("p (i d) -> p i d", i=2), x, ALU.add).then_inc(s.summed, 1)
        v.wait_ge(s.summed, u + 1)
    for i in range(2):
        dve.mark(v.bn_stats(s.st[:, u % 2, i, :], m.X[:, 2 * u + i, :]))
    dve.wait()
    for i in range(2):
        v.bn_aggr(s.mv[:, u, i, :], s.st[:, u % 2, i, :]).then_inc(s.stats, 1)


def norm_root(a, m, s, u):
    a.wait_ge(s.stats, 2 * u + 2)
    a.activation(s.std[:, u, :], s.mv[:, u, :, 1], ACT.Sqrt, bias=m.eps[:, 0:1]).then_inc(s.root, 1)


def norm_scale(v, dve, s, u):
    v.wait_ge(s.root, u + 1)
    dve.chain(v.reciprocal(s.rstd[:, u, :], s.std[:, u, :]))
    v.scalar_tensor_tensor(s.shift[:, u, :], s.mv[:, u, :, 0], -1.0, s.rstd[:, u, :],
                           ALU.mult, ALU.mult).then_inc(s.scaled, 1)


def norm_first(v, m, s, u):
    v.wait_ge(s.scaled, u + 1)
    x = m.X[:, 2 * u, :]
    v.tensor_scalar(x, x, s.rstd[:, u, 0:1], s.shift[:, u, 0:1], ALU.mult, ALU.add).then_inc(s.normed_first, 1)


def norm_second(a, m, s, u):
    a.wait_ge(s.scaled, u + 1)
    x = m.X[:, 2 * u + 1, :]
    a.activation(x, x, ACT.Identity, bias=s.shift[:, u, 1:2], scale=s.rstd[:, u, 1:2]).then_inc(s.normed_second, 1)


def wait_normed(eng, s, units):
    eng.wait_ge(s.normed_first, units)
    eng.wait_ge(s.normed_second, units)


def norm_turn(t, m, s, u, banks):
    wait_normed(t, s, u + 1)
    if u >= 2:
        t.wait_ge(s.xt_done, u - 1)
    out = m.PS[:, banks[u % 2], :].rearrange("p (k i t) -> p k i t", k=KD, i=2)
    for k in range(KD):
        for i in range(2):
            ins = t.transpose(out[:, k, i, :], m.X[:, 2 * u + i, k * P:(k + 1) * P], m.ident[:, :])
    ins.then_inc(s.turned, 1)


def norm_copy(a, m, s, u, banks):
    a.wait_ge(s.turned, u + 1)
    a.activation(m.XT[:, :, 2 * u * P:(2 * u + 2) * P],
                 m.PS[:, banks[u % 2], :].rearrange("p (k t) -> p k t", k=KD), ACT.Identity).then_inc(s.xt_done, 1)



PAIRS = CLASSES // 2
ORDERS = 2
ORDER = (0, 3, 1, 2)
UPDATES = (4, 6, 2, 0, 1, 3)
POOL_UPDATES = (5, 7)


def cos(a, j):
    return math.cos(math.pi * a * (2 * j + 1) / 16)


def sin(a, j):
    return math.sin(math.pi * a * (2 * j + 1) / 16)


def remade(o, a):
    return len(UPDATES) * (o - 1) + UPDATES.index(a) + 1


def source(m, tr):
    return (lambda a: m.V[:, 2, a, :]) if tr else (lambda a: m.H[:, a, :])


def convolution_state(nc, m, scope):
    cv = Record()
    sb = lambda n, shape: scope.enter_context(nc.sbuf_tensor(f"cv_{n}", shape, F32))
    SUMS = sb("sums", [P, 11, BANK])
    cv.W4, cv.PLUS, cv.MINUS, cv.C0, cv.S1, cv.S0, cv.C1 = (SUMS[:, i, :] for i in range(7))
    cv.OD = [SUMS[:, 7 + i, :] for i in range(4)]
    cv.G = [SUMS[:, i, :] for i in range(8)]
    cv.ODD = sb("odd", [P, 2, BANK])
    cv.T = sb("t", [P, 2, 4, BANK])
    UV = m.X[:, :, :].rearrange("p i d -> p (i d)").rearrange("p (s c r n) -> p s c r n", s=2, c=2, r=2)
    UF = cv.T[:, :, :, :].rearrange("p s (c r) n -> p s c r n", c=2)
    cv.U = lambda n: (UV if n >= PAIRS else UF)[:, n % 2]
    (cv.pstep, cv.h_ready, cv.evens_scaled, cv.odds_scaled, cv.mixed, cv.evened, cv.odd_summed, cv.folded, cv.halves,
     cv.spectra, cv.updated) = (new_semaphore(nc, m, f"cv_{n}") for n in (
         "pstep", "h_ready", "evens_scaled", "odds_scaled", "mixed", "evened", "odd_summed", "folded", "halves",
         "spectra", "updated"))
    return cv


def scale_evens(a, m, cv, tr):
    v = source(m, tr)
    if tr == 1:
        a.wait_ge(cv.evened, 2 * PAIRS)
    for dst, block_, factor in ((cv.W4, 4, math.sqrt(0.5)), (cv.S1, 6, sin(2, 0)), (cv.C1, 6, cos(2, 0))):
        if tr >= 2:
            a.wait_ge(cv.updated, remade(tr - 1, block_))
        a.activation(dst, v(block_), ACT.Copy, scale=factor).then_inc(cv.evens_scaled, 1)


def scale_odds(a, m, cv, k):
    tr, j = k // 2, k % 2
    v = source(m, tr)
    if tr >= 2:
        a.wait_ge(cv.updated, remade(tr - 1, 3))
    if k >= 1:
        a.wait_ge(cv.folded, 4 * k)
    for dst, block_, factor in ((cv.OD[0], 1, cos(1, j)), (cv.OD[1], 3, cos(3, j)),
                                (cv.OD[2], 1, -sin(1, j)), (cv.OD[3], 3, -sin(3, j))):
        a.activation(dst, v(block_), ACT.Copy, scale=factor).then_inc(cv.odds_scaled, 1)


def start_evens(pool, m, cv, tr):
    pool.wait_ge(cv.evens_scaled, 3 * tr + 1)
    if tr >= 2:
        pool.wait_ge(cv.updated, remade(tr - 1, 0))
    cv.own.mark(pool.tensor_tensor(cv.PLUS, source(m, tr)(0), cv.W4, ALU.add))
    cv.own.mark(pool.tensor_tensor(cv.MINUS, source(m, tr)(0), cv.W4, ALU.subtract))


def even_sums(pool, m, cv, n):
    if n % PAIRS == 0:
        cv.own.wait()
    if n % PAIRS in (0, 2):
        pool.wait_ge(cv.mixed, 4 * (n // PAIRS) + 2 + n % PAIRS)
    if n >= 2:
        pool.wait_ge(cv.spectra, 2 * (n - 1))
    re, im = (cv.U(n)[:, 1, z, :] for z in range(2))
    j = ORDER[n % PAIRS]
    base, c, s = (cv.PLUS, cv.C0, cv.S0) if j in (0, 3) else (cv.MINUS, cv.C1, cv.S1)
    pool.tensor_tensor(re, base, c, ALU.add if j < 2 else ALU.subtract).then_inc(cv.evened, 1)
    pool.tensor_tensor(im, s, cv.W4, ALU.add if j < 2 else ALU.subtract).then_inc(cv.evened, 1)


def mix_evens(v, m, cv, tr):
    src = source(m, tr)(2)
    v.wait_ge(cv.evens_scaled, 3 * tr + 3)
    if tr:
        v.wait_ge(cv.evened, 2 * PAIRS * tr)
    v.scalar_tensor_tensor(cv.C0, src, cos(2, 0), cv.S1, ALU.mult, ALU.add).then_inc(cv.mixed, 1)
    v.scalar_tensor_tensor(cv.S0, src, sin(2, 0), cv.C1, ALU.mult, ALU.add).then_inc(cv.mixed, 1)
    v.wait_ge(cv.mixed, 4 * tr + 2)
    v.scalar_tensor_tensor(cv.S1, src, cos(2, 0), cv.S1, ALU.mult, ALU.subtract).then_inc(cv.mixed, 1)
    v.scalar_tensor_tensor(cv.C1, src, sin(2, 0), cv.C1, ALU.mult, ALU.subtract).then_inc(cv.mixed, 1)


def sum_odds(v, m, cv, k):
    tr, j = k // 2, k % 2
    v.wait_ge(cv.odds_scaled, 4 * (k + 1))
    for dst, block_, factor in ((cv.OD[0], 5, cos(5, j)), (cv.OD[1], 7, cos(7, j)),
                                (cv.OD[2], 5, -sin(5, j)), (cv.OD[3], 7, -sin(7, j))):
        v.scalar_tensor_tensor(dst, source(m, tr)(block_), factor, dst, ALU.mult, ALU.add).then_inc(cv.odd_summed, 1)
    v.wait_ge(cv.odd_summed, 4 * (k + 1))


def split(v, m, cv, n):
    if n % 2 == 0:
        sum_odds(v, m, cv, n // 2)
    if n:
        v.wait_ge(cv.halves, 4 * n)
    for z in range(2):
        if n % 2 == 0:
            ins = v.tensor_tensor(cv.ODD[:, z, :], cv.OD[2 * z], cv.OD[2 * z + 1], ALU.add)
        else:
            ins = v.tensor_tensor(cv.ODD[:, z, :], cv.OD[3 - 2 * z], cv.OD[2 - 2 * z], ALU.subtract)
        ins.then_inc(cv.folded, 1)
    v.wait_ge(cv.folded, 2 * n + 2)
    v.wait_ge(cv.evened, 2 * n + 2)
    one, two = cv.U(n)[:, 0, :, :], cv.U(n)[:, 1, :, :]
    v.tensor_tensor(one[:, 0, :], two[:, 0, :], cv.ODD[:, 0, :], ALU.add).then_inc(cv.halves, 1)
    v.tensor_tensor(one[:, 1, :], cv.ODD[:, 1, :], two[:, 1, :], ALU.subtract).then_inc(cv.halves, 1)
    v.wait_ge(cv.halves, 4 * n + 2)
    v.tensor_tensor(two[:, 0, :], two[:, 0, :], cv.ODD[:, 0, :], ALU.subtract).then_inc(cv.halves, 1)
    v.tensor_tensor(two[:, 1, :], cv.ODD[:, 1, :], two[:, 1, :], ALU.add).then_inc(cv.halves, 1)



def hyena_prepare(nc, d, m):
    C = 3 * D // P
    H, cv = m.H, m.cv
    two_pi = 2 * math.pi
    hi = 6.28125
    mid = float(np.float32(two_pi - hi))
    lo = two_pi - hi - mid
    magic = 1.5 * 2.0 ** 23
    with ExitStack() as scope:
        sem = lambda n: new_semaphore(nc, m, f"pj_{n}")
        sb = lambda n, shape: scope.enter_context(nc.sbuf_tensor(f"pj_{n}", shape, F32))
        W, padded, taps = sb("w", [P, KD, 3 * D]), sb("padded", [P, 2, B, L + 2]), sb("taps", [P, 2, B, L])
        pe, w1, w2 = sb("pe", [EMB, L]), sb("w1", [EMB, 64]), sb("w2", [65, 2 * D])
        negt, rate, shift = sb("negt", [P, BLOCKS]), sb("rate", [P, 2 * D]), sb("shift", [P, 2 * D])
        arg, sine = sb("arg", [64, L]), sb("sine", [65, L])
        decay = cv.T[:, 0, :, :]
        turns = sine[0:64, :]
        loaded, xt_loaded, pads, eps_set = sem("loaded"), [sem(f"xt{g}") for g in range(GROUPS)], sem("pads"), sem("eps")
        product, biased, centre, tapped, turned = (sem(n) for n in (
            "product", "biased", "centre", "tapped", "turned"))
        placed = [sem(f"placed{b}") for b in range(B)]
        placing = lambda c, j: (m.V[:, c // 2, 4 * (j % 2):4 * (j % 2) + 4, (j // 2) * D + (c % 2) * P:(j // 2) * D + (c % 2 + 1) * P],
                                m.PS[:, 4 + j, :].rearrange("p (a c) -> p a c", a=4))
        first_loaded = sem("first_loaded")
        mlp_loaded, rate_loaded, out_loaded = sem("mlp_loaded"), sem("rate_loaded"), sem("out_loaded")
        one, hidden, step, reduced, sined, rated, decayed, drawn, filtered = (sem(n) for n in (
            "one", "hidden", "step", "reduced", "sined", "rated", "decayed", "drawn", "filtered"))
        xT = chunks(d["xT"])
        with nc.Block(no_gpsimd_drain=True) as block:
            @block.sync
            def _(sp):
                sp.dma_start(W[:, :, 0:P], chunks(d["hy_w_inT"])[:, :, 0:P]).then_inc(first_loaded, 16)
                sp.dma_start(m.XT[:, :, 0:BANK], xT[:, :, 0:BANK]).then_inc(xt_loaded[0], 16)
                sp.dma_start(W[:, :, P:], chunks(d["hy_w_inT"])[:, :, P:]).then_inc(loaded, 16)
                for g in range(1, GROUPS):
                    sp.dma_start(m.XT[:, :, g * BANK:(g + 1) * BANK],
                                 xT[:, :, g * BANK:(g + 1) * BANK]).then_inc(xt_loaded[g], 16)
                sp.dma_start(w2[0:64, :], d["hy_w2T"]).then_inc(out_loaded, 16)
                sp.dma_start(w2[64:65, :], d["hy_b2"].rearrange("(o n) -> o n", o=1)).then_inc(out_loaded, 16)
                sp.dma_start(shift[:, :], rows_of(d["hy_fbias"])).then_inc(out_loaded, 16)
                sp.dma_start(m.ident[:, :], d["ident"]).then_inc(loaded, 16)
                sp.dma_start(m.FW[:, :, :, :], d["forward"]).then_inc(m.transforms_loaded, 16)
                sp.dma_start(m.IV[:, :, :, :], d["inverse"]).then_inc(m.transforms_loaded, 16)

            @block.gpsimd
            def _(pool):
                pool.memset(padded[:, :, :, 0:1], 0.0).then_inc(pads, 1)
                pool.memset(padded[:, :, :, L + 1:L + 2], 0.0).then_inc(pads, 1)
                pool.memset(m.eps[:, :], EPS).then_inc(eps_set, 1)
                pool.memset(m.ones[:, :], 1.0).then_inc(eps_set, 1)
                pool.wait_ge(filtered, BLOCKS)
                pool.wait_ge(out_loaded, 48)
                pool.tensor_tensor(H[:, :, :], H[:, :, :], shift[:, :].unsqueeze(1).to_broadcast([P, BLOCKS, 2 * D]),
                                   ALU.add).then_inc(cv.h_ready, 1)
                cv.own = Steps(pool, cv.pstep)
                start_evens(pool, m, cv, 0)
                for n in range(2):
                    even_sums(pool, m, cv, n)

            @block.tensor
            def _(t):
                def project(c):
                    for g in range(GROUPS):
                        n = GROUPS * c + g
                        if c == 0:
                            t.wait_ge(xt_loaded[g], 16)
                        if n >= 4:
                            t.wait_ge(biased, n - 3)
                        for k in range(KD):
                            ins = t.matmul(m.PS[:, n % 4, :], W[:, k, c * P:(c + 1) * P],
                                           m.XT[:, k, g * BANK:(g + 1) * BANK], start=k == 0, stop=k == KD - 1)
                        ins.then_inc(product, 1)

                def turn(c):
                    t.wait_ge(tapped, 2 * c + 2)
                    for j in range(4):
                        n = 4 * c + j
                        if n >= 4:
                            t.wait_ge(placed[j // 2], 2 * c - 1 + j % 2)
                        else:
                            t.wait_ge(filtered, 5 + j)
                        for i in range(4):
                            at = (4 * (j % 2) + i) * P
                            ins = t.transpose(m.PS[:, 4 + j, i * P:(i + 1) * P],
                                              taps[:, c % 2, j // 2, at:at + P], m.ident[:, :])
                        ins.then_inc(turned, 1)

                t.wait_ge(mlp_loaded, 48)
                for g in range(2):
                    t.matmul(m.PS[0:64, 4 + g, :], w1[:, :], pe[:, g * BANK:(g + 1) * BANK],
                             start=True, stop=True).then_inc(hidden, 1)
                t.wait_ge(first_loaded, 16)
                project(0)
                t.wait_ge(loaded, 32)
                t.wait_ge(sined, 1)
                t.wait_ge(one, 1)
                t.wait_ge(out_loaded, 48)
                for a in range(BLOCKS):
                    if a >= 4:
                        t.wait_ge(filtered, a - 3)
                    t.matmul(m.PS[:, 4 + a % 4, :], sine[:, a * P:(a + 1) * P], w2[:, :],
                             start=True, stop=True).then_inc(drawn, 1)
                for c in range(C):
                    if c + 1 < C:
                        project(c + 1)
                    turn(c)

            @block.scalar
            def _(a):
                def decays(first):
                    for i in range(first, first + 4):
                        if i >= 4:
                            a.wait_ge(filtered, i - 3)
                        a.activation(decay[:, i % 4, :], rate[:, :], ACT.Exp, scale=negt[:, i:i + 1]).then_inc(decayed, 1)

                def bias(c):
                    for g in range(GROUPS):
                        a.wait_ge(product, GROUPS * c + g + 1)
                        if c >= 2 and g == 0:
                            a.wait_ge(tapped, 2 * c - 2)
                        at = 1 + BANK * (g % 2)
                        a.activation(padded[:, c % 2, g // 2, at:at + BANK], m.PS[:, (GROUPS * c + g) % 4, :],
                                     ACT.Identity, bias=col(m, "b_in", c)).then_inc(biased, 1)

                def place(c):
                    for j in (2, 3):
                        a.wait_ge(turned, 4 * c + j + 1)
                        dst, src = placing(c, j)
                        a.activation(dst, src, ACT.Identity).then_inc(placed[1], 1)

                a.dma_start(pe[:, :], d["peT"]).then_inc(mlp_loaded, 16)
                a.dma_start(w1[:, :], d["hy_w1T"]).then_inc(mlp_loaded, 16)
                a.dma_start(m.cols[:, :], d["cols"]).then_inc(mlp_loaded, 16)
                a.dma_start(rate[:, :], rows_of(d["hy_decay"])).then_inc(rate_loaded, 16)
                a.dma_start(negt[:, :], d["negt"]).then_inc(rate_loaded, 16)
                a.wait_ge(rate_loaded, 32)
                a.activation(rate[:, :], rate[:, :], ACT.Exp).then_inc(rated, 1)
                a.wait_ge(rated, 1)
                decays(0)
                a.wait_ge(reduced, 1)
                a.activation(sine[0:64, :], arg[:, :], ACT.Sin).then_inc(sined, 1)
                a.wait_ge(loaded, 32)
                for c in range(C):
                    bias(c)
                    if c == 0:
                        decays(4)
                    a.wait_ge(biased, GROUPS * c + GROUPS)
                    if c >= 2:
                        a.wait_ge(turned, 4 * (c - 1))
                    a.activation(taps[:, c % 2, :, :], padded[:, c % 2, :, 1:L + 1], ACT.Identity,
                                 bias=col(m, "conv_b", c), scale=col(m, "conv_w", 3 * c + 1)).then_inc(centre, 1)
                    if c == 1:
                        a.wait_ge(cv.h_ready, 1)
                        scale_evens(a, m, cv, 0)
                    if c == 2:
                        scale_odds(a, m, cv, 0)
                    if c >= 1:
                        place(c - 1)
                place(C - 1)

            @block.vector
            def _(v):
                dve = Steps(v, step)

                def tap(c):
                    v.wait_ge(centre, c + 1)
                    for n, j in enumerate((0, 2)):
                        if n:
                            v.wait_ge(tapped, 2 * c + 1)
                        v.scalar_tensor_tensor(taps[:, c % 2, :, :], padded[:, c % 2, :, j:j + L],
                                               col(m, "conv_w", 3 * c + j), taps[:, c % 2, :, :],
                                               ALU.mult, ALU.add).then_inc(tapped, 1)

                def place(c):
                    for j in (0, 1):
                        v.wait_ge(turned, 4 * c + j + 1)
                        dst, src = placing(c, j)
                        v.tensor_copy(dst, src).then_inc(placed[0], 1)

                v.memset(sine[64:65, :], 1.0).then_inc(one, 1)
                v.wait_ge(hidden, 2)
                v.wait_ge(mlp_loaded, 48)
                dve.chain(v.tensor_scalar(arg[:, :], m.PS[0:64, 4:6, :], col(m, "hy_b1", 0, 64), FREQ,
                                          ALU.add, ALU.mult))
                dve.chain(v.tensor_scalar(turns, arg[:, :], 1 / two_pi, magic, ALU.mult, ALU.add))
                dve.chain(v.tensor_scalar(turns, turns, magic, None, ALU.subtract))
                for part in (hi, mid, lo):
                    dve.chain(v.scalar_tensor_tensor(arg[:, :], turns, -part, arg[:, :], ALU.mult, ALU.add))
                pi = float(np.nextafter(np.float32(math.pi), np.float32(0)))
                v.tensor_scalar(arg[:, :], arg[:, :], -pi, pi, ALU.max, ALU.min).then_inc(reduced, 1)
                for a in range(BLOCKS):
                    v.wait_ge(drawn, a + 1)
                    v.wait_ge(decayed, a + 1)
                    v.tensor_tensor(H[:, a, :], m.PS[:, 4 + a % 4, :], decay[:, a % 4, :], ALU.mult).then_inc(filtered, 1)
                v.wait_ge(pads, 2)
                v.wait_ge(loaded, 32)
                tap(0)
                for c in range(C):
                    if c + 1 < C:
                        tap(c + 1)
                    place(c)
                    if c == 1:
                        mix_evens(v, m, cv, 0)
                    if c in (2, 3):
                        split(v, m, cv, c - 2)



def hyena_convolve(nc, d, m):
    cv = m.cv
    U, OD, G, T = cv.U, cv.OD, cv.G, cv.T
    evened, folded, halves, spectra, updated = cv.evened, cv.folded, cv.halves, cv.spectra, cv.updated
    Y = m.XT[:, :, :].rearrange("p k t -> p (k t)").rearrange("p (a n) -> p a n", n=BANK)
    SUM_OPS = (ALU.add, ALU.subtract, ALU.subtract, ALU.add)
    FIRSTS = ((4, 0, lambda j: cos(4, j)), (6, 1, lambda j: cos(6, j)), (2, 1, lambda j: cos(2, j)), (1, 4, lambda j: cos(1, j)),
              (3, 6, lambda j: cos(3, j)), (5, 4, lambda j: cos(5, j)), (7, 6, lambda j: cos(7, j)), (0, 0, lambda j: 1.0))
    SECONDS = ((4, 3, lambda j: -sin(4, j)), (6, 2, lambda j: -sin(6, j)), (2, 2, lambda j: -sin(2, j)), (1, 5, lambda j: sin(1, j)),
               (3, 7, lambda j: -sin(3, j)), (5, 5, lambda j: sin(5, j)), (7, 7, lambda j: -sin(7, j)))
    mine = lambda terms: [x for x in terms if x[0] not in POOL_UPDATES]
    theirs = lambda terms: [x for x in terms if x[0] in POOL_UPDATES]
    PER_ORDER = len(SECONDS) + len(mine(FIRSTS)) + len(mine(SECONDS))
    with ExitStack() as scope:
        sem = lambda n: new_semaphore(nc, m, f"cv_{n}")
        sb = lambda n, shape: scope.enter_context(nc.sbuf_tensor(f"cv_{n}", shape, F32))
        FW, IV = m.FW, m.IV
        HS = sb("hs", [P, CLASSES, 2, 2 * D])
        Z = sb("z", [P, 2, 2, BANK])
        Q = sb("q", [P, 2, 4, BANK])
        order_step = sem("order_step")
        kept, products, joined, inverses, held, sums, combined, started, scaled, pool_added, added, pool_updated = (
            sem(n) for n in ("kept", "products", "joined", "inverses", "held", "sums", "combined", "started", "scaled",
                             "pool_added", "added", "pool_updated"))

        def combine(eng, k, which):
            eng.wait_ge(sums, 8 * (k + 1))
            if k:
                eng.wait_ge(added, PER_ORDER * (k // 2) + len(SECONDS) * (k % 2))
                eng.wait_ge(started, len(FIRSTS) * ((k + 1) // 2))
                if k > 1:
                    eng.wait_ge(scaled, 4 * (k // 2))
            one, two = ([Q[:, i, z, :] for z in range(4)] for i in range(2))
            terms = ((one[0], ALU.add, two[0]), (one[0], ALU.subtract, two[0]),
                     (one[2], ALU.add, two[2]), (one[2], ALU.subtract, two[2]),
                     (one[1], ALU.subtract, two[3]), (two[1], ALU.subtract, one[3]),
                     (one[1], ALU.add, two[3]), (two[1], ALU.add, one[3]))
            for to in which:
                x, op, y = terms[to]
                eng.tensor_tensor(G[to], x, y, op).then_inc(combined, 1)

        classes = lambda n: (ORDER[n % PAIRS], CLASSES - 1 - ORDER[n % PAIRS])
        with nc.Block(no_gpsimd_drain=True) as block:
            @block.sync
            def _(sp):
                load(sp, m.w_hyena_out)
                sp.wait_ge(spectra, 2 * PAIRS * (ORDERS + 1))
                x = d["x"].rearrange("(i p) d -> p i d", p=P)
                for g in range(GROUPS):
                    sp.dma_start(m.X[:, 4 * g:4 * g + 4, :], x[:, 4 * g:4 * g + 4, :]).then_inc(m.x_loaded[g], 16)

            @block.tensor
            def _(t):
                def complex_product(bank, M, c, re, im, sign):
                    plus, minus = (1, 2) if sign > 0 else (2, 1)
                    t.matmul(m.PS[:, bank, :], M[:, c, 0, :], re, start=True, stop=False)
                    t.matmul(m.PS[:, bank, :], M[:, c, minus, :], im, start=False, stop=True)
                    t.matmul(m.PS[:, bank + 1, :], M[:, c, 0, :], im, start=True, stop=False)
                    return t.matmul(m.PS[:, bank + 1, :], M[:, c, plus, :], re, start=False, stop=True)

                def forward(n):
                    for i, c in enumerate(classes(n)):
                        t.wait_ge(halves, 4 * n + 2 * i + 2)
                        if 0 < n <= PAIRS:
                            t.wait_ge(kept, 4 * n - 2 + 2 * i)
                        elif n > PAIRS:
                            t.wait_ge(products, 8 * (n - PAIRS) - 4 + 4 * i)
                        complex_product(2 * i, FW, c, U(n)[:, i, 0, :], U(n)[:, i, 1, :], -1).then_inc(spectra, 1)

                def inverse(r):
                    for i, c in enumerate(classes(r)):
                        t.wait_ge(joined, 4 * r + 2 * i + 2)
                        if r >= 1:
                            t.wait_ge(held, 4 * r - 2 + 2 * i)
                        complex_product(4 + 2 * i, IV, c, T[:, i, 0, :], T[:, i, 2, :], 1).then_inc(inverses, 1)

                t.wait_ge(m.transforms_loaded, 32)
                for n in range(PAIRS):
                    forward(n)
                for o in range(ORDERS):
                    if o:
                        t.wait_ge(products, 8 * PAIRS * o)
                        t.wait_ge(cv.mixed, 4 * (o + 1) + 4)
                        warm_up(t, m, 0, m.FW[:, 0:2, 0:2, :])
                    for s in range(PAIRS + 1):
                        if s < PAIRS:
                            forward(PAIRS * (o + 1) + s)
                        if s >= 1:
                            inverse(PAIRS * o + s - 1)
                t.wait_ge(products, 8 * PAIRS * ORDERS)
                t.wait_ge(added, PER_ORDER * ORDERS)
                warm_up(t, m, 0, m.FW[:, 0:2, 0:2, :])

            @block.scalar
            def _(a):
                def keep(n):
                    for i, c in enumerate(classes(n)):
                        a.wait_ge(spectra, 2 * n + i + 1)
                        for r in range(2):
                            a.activation(HS[:, c, r, :], m.PS[:, 2 * i + r, :], ACT.Identity).then_inc(kept, 1)

                def hold(r):
                    for i in range(2):
                        a.wait_ge(inverses, 2 * r + i + 1)
                        if r >= 1 and i == 0:
                            a.wait_ge(sums, 4 * r)
                        for z in range(2):
                            a.activation(Z[:, i, z, :], m.PS[:, 4 + 2 * i + z, :], ACT.Identity).then_inc(held, 1)

                def start_sums(o):
                    a.wait_ge(combined, 16 * o + 8)
                    for block_, g, factor in FIRSTS:
                        a.activation(Y[:, block_, :], G[g], ACT.Copy, scale=factor(0)).then_inc(started, 1)

                def scale_last(o):
                    a.wait_ge(combined, 16 * o + 16)
                    for n, (block_, g, factor) in enumerate(theirs(FIRSTS) + theirs(SECONDS)):
                        a.activation(T[:, 0, n, :], G[g], ACT.Copy, scale=factor(1)).then_inc(scaled, 1)

                scale_odds(a, m, cv, 1)
                keep(0)
                keep(1)
                keep(2)
                scale_evens(a, m, cv, 1)
                scale_odds(a, m, cv, 2)
                keep(3)
                for o in range(ORDERS):
                    if o:
                        a.wait_ge(scaled, 4 * o)
                        scale_evens(a, m, cv, o + 1)
                        scale_odds(a, m, cv, 2 * (o + 1))
                    scale_odds(a, m, cv, 2 * (o + 1) + 1)
                    for s in range(PAIRS):
                        hold(PAIRS * o + s)
                        if s == 2:
                            start_sums(o)
                    scale_last(o)

            @block.gpsimd
            def _(pool):
                cv.own = Steps(pool, order_step)

                def join(r):
                    for i in range(2):
                        pool.wait_ge(products, 8 * r + 4 * i + 4)
                        pool.tensor_tensor(T[:, i, 0, :], T[:, i, 0, :], T[:, i, 1, :], ALU.subtract).then_inc(joined, 1)
                        pool.tensor_tensor(T[:, i, 2, :], T[:, i, 2, :], T[:, i, 3, :], ALU.add).then_inc(joined, 1)

                def sum_pair(r, which=(0, 1, 2, 3)):
                    pool.wait_ge(held, 4 * (r + 1))
                    if r >= 2:
                        pool.wait_ge(combined, 8 * (r // 2))
                    for to in which:
                        pool.tensor_tensor(Q[:, r % 2, to, :], Z[:, 0, to // 2, :], Z[:, 1, to // 2, :],
                                           SUM_OPS[to]).then_inc(sums, 1)

                for n in (2, 3):
                    even_sums(pool, m, cv, n)
                for o in range(ORDERS):
                    n, r = PAIRS * (o + 1), PAIRS * o
                    start_evens(pool, m, cv, o + 1)
                    even_sums(pool, m, cv, n)
                    even_sums(pool, m, cv, n + 1)
                    join(r)
                    even_sums(pool, m, cv, n + 2)
                    join(r + 1)
                    even_sums(pool, m, cv, n + 3)
                    sum_pair(r)
                    join(r + 2)
                    join(r + 3)
                    sum_pair(r + 2, (0, 2))
                    sum_pair(r + 3, (0, 2))
                    combine(pool, 2 * o + 1, (6, 7))
                    for n in range(4):
                        block_ = Y[:, POOL_UPDATES[n % 2], :]
                        pool.wait_ge(scaled, 4 * o + n + 1)
                        if n < 2:
                            pool.wait_ge(added, PER_ORDER * o + len(SECONDS))
                        else:
                            pool.wait_ge(pool_added, 4 * o + n - 1)
                        pool.tensor_tensor(block_, block_, T[:, 0, n, :], ALU.add).then_inc(pool_added, 1)
                    pool.wait_ge(pool_added, 4 * (o + 1))
                    for a in POOL_UPDATES:
                        pool.tensor_tensor(m.V[:, 2, a, :], Y[:, a, :], m.V[:, o, a, :], ALU.mult).then_inc(pool_updated, 1)

            @block.vector
            def _(v):
                def multiply(r):
                    o = r // PAIRS
                    if r == 0:
                        v.wait_ge(kept, 4 * PAIRS)
                    for i, c in enumerate(classes(r)):
                        v.wait_ge(spectra, 2 * (PAIRS + r) + i + 1)
                        if r >= 1:
                            v.wait_ge(inverses, 2 * r - 1 + i)
                        h = [HS[:, c, z, o * D:(o + 1) * D].unsqueeze(1).to_broadcast([P, B, D]) for z in range(2)]
                        for to, (vz, hz) in enumerate(((0, 0), (1, 1), (0, 1), (1, 0))):
                            v.tensor_tensor(T[:, i, to, :].rearrange("p (b n) -> p b n", b=B),
                                            m.PS[:, 2 * i + vz, :].rearrange("p (b n) -> p b n", b=B),
                                            h[hz], ALU.mult).then_inc(products, 1)

                def sum_too(r, which):
                    v.wait_ge(held, 4 * (r + 1))
                    if r >= 2:
                        v.wait_ge(combined, 8 * (r // 2))
                    for to in which:
                        v.tensor_tensor(Q[:, r % 2, to, :], Z[:, 0, to // 2, :], Z[:, 1, to // 2, :],
                                        SUM_OPS[to]).then_inc(sums, 1)

                def gather(k):
                    o, j = divmod(k, 2)
                    v.wait_ge(combined, 8 * (k + 1))
                    if j:
                        for block_, g, factor in mine(FIRSTS):
                            v.scalar_tensor_tensor(Y[:, block_, :], G[g], factor(j), Y[:, block_, :],
                                                   ALU.mult, ALU.add).then_inc(added, 1)
                    for n, (block_, g, factor) in enumerate(mine(SECONDS) if j else SECONDS):
                        if j:
                            v.wait_ge(added, PER_ORDER * o + len(SECONDS) + n + 1)
                        else:
                            v.wait_ge(started, len(FIRSTS) * o + n + 1)
                        v.scalar_tensor_tensor(Y[:, block_, :], G[g], factor(j), Y[:, block_, :],
                                               ALU.mult, ALU.add).then_inc(added, 1)

                def update(o):
                    v.wait_ge(added, PER_ORDER * (o + 1))
                    for a in UPDATES:
                        v.tensor_tensor(m.V[:, 2, a, :], Y[:, a, :], m.V[:, o, a, :], ALU.mult).then_inc(updated, 1)
                    v.wait_ge(updated, len(UPDATES) * (o + 1))
                    v.wait_ge(pool_updated, len(POOL_UPDATES) * (o + 1))

                for n in (2, 3):
                    split(v, m, cv, n)
                for o in range(ORDERS):
                    at = PAIRS * (o + 1)
                    mix_evens(v, m, cv, o + 1)
                    split(v, m, cv, at)
                    split(v, m, cv, at + 1)
                    multiply(at - PAIRS)
                    split(v, m, cv, at + 2)
                    multiply(at - PAIRS + 1)
                    split(v, m, cv, at + 3)
                    multiply(at - PAIRS + 2)
                    r = PAIRS * o
                    sum_too(r + 1, (0, 1, 2, 3))
                    combine(v, 2 * o, range(8))
                    multiply(r + 3)
                    sum_too(r + 2, (1, 3))
                    gather(2 * o)
                    sum_too(r + 3, (1, 3))
                    combine(v, 2 * o + 1, range(6))
                    gather(2 * o + 1)
                    update(o)


def hyena_out(nc, d, m):
    banks = (4, 5)
    with ExitStack() as scope:
        sem = lambda n: new_semaphore(nc, m, f"ho_{n}")
        W, bias = buffers(m.w_hyena_out, "w bias")
        loaded, count = m.w_hyena_out.loaded, m.w_hyena_out.count
        s = norm_state(nc, m, scope, "ho")
        step, biased, vturned, vcopied = (sem(n) for n in ("step", "biased", "vturned", "vcopied"))
        with nc.Block(no_gpsimd_drain=True) as block:
            @block.sync
            def _(sp):
                load(sp, m.w_cross)

            @block.gpsimd
            def _(pool):
                pool.wait_ge(loaded, count)
                for u in range(UNITS):
                    pool.wait_ge(m.x_loaded[u // 2], 16)
                    xu = m.X[:, 2 * u:2 * u + 2, :]
                    pool.tensor_tensor(xu, xu, bias[:, :].unsqueeze(1).to_broadcast([P, 2, D]), ALU.add).then_inc(biased, 1)
                widen_bq(pool, m)

            @block.tensor
            def _(t):
                def turn(u):
                    if u >= 2:
                        t.wait_ge(vcopied, u - 1)
                    b, a = u // 4, 2 * (u % 4)
                    for k in range(KD):
                        for i in range(2):
                            at = b * D + k * P
                            ins = t.transpose(m.PS[:, 6 + u % 2, (2 * k + i) * P:(2 * k + i + 1) * P],
                                              m.V[:, 2, a + i, at:at + P], m.ident[:, :])
                    ins.then_inc(vturned, 1)

                def project(u):
                    t.wait_ge(vcopied, u + 1)
                    if u >= 4:
                        t.wait_ge(s.summed, u - 3)
                    for i in range(2):
                        for k in range(KD):
                            ins = t.matmul(m.PS[:, u % 4, i * D:(i + 1) * D],
                                           m.XT[:, k, (2 * u + i) * P:(2 * u + i + 1) * P], W[:, k, :],
                                           start=k == 0, stop=k == KD - 1)
                    ins.then_inc(s.out_done, 1)

                t.wait_ge(loaded, count)
                for u in range(UNITS + 3):
                    if u < UNITS:
                        turn(u)
                    if 1 <= u <= UNITS:
                        project(u - 1)
                    if u >= 3:
                        norm_turn(t, m, s, u - 3, banks)
                    if u == UNITS:
                        t.wait_ge(s.summed, UNITS - 2)
                        make_keys(t, m, 0)
                    if u == UNITS + 1:
                        fold_queries(t, m, 1)
                wait_normed(t, s, UNITS)
                warm_up(t, m, 2, m.X[:, 0:2, :], 1)

            @block.scalar
            def _(a):
                for u in range(UNITS + 3):
                    if u < UNITS:
                        a.wait_ge(vturned, u + 1)
                        a.activation(m.XT[:, :, 2 * u * P:(2 * u + 2) * P],
                                     m.PS[:, 6 + u % 2, :].rearrange("p (k t) -> p k t", k=KD),
                                     ACT.Identity).then_inc(vcopied, 1)
                    if 1 <= u <= UNITS:
                        norm_root(a, m, s, u - 1)
                    if 2 <= u <= UNITS + 1:
                        norm_second(a, m, s, u - 2)
                    if u >= 3:
                        norm_copy(a, m, s, u - 3, banks)
                    if u == UNITS:
                        copy_keys(a, m, 0)
                    if u == UNITS + 1:
                        copy_folded(a, m, 1)

            @block.vector
            def _(v):
                dve = Steps(v, step)
                for u in range(UNITS + 1):
                    if u < UNITS:
                        v.wait_ge(biased, u + 1)
                        norm_sum(v, dve, m, s, u, u % 4)
                    if u >= 1:
                        norm_scale(v, dve, s, u - 1)
                        norm_first(v, m, s, u - 1)



def cross_attend(nc, d, m, layer):
    BK = B * KEYS
    tag = f"x{layer}"
    turn_banks = (6, 7)
    with ExitStack() as scope:
        sem = lambda n: new_semaphore(nc, m, f"{tag}_{n}")
        sb = lambda n, shape: scope.enter_context(nc.sbuf_tensor(f"{tag}_{n}", shape, F32))
        ctxT, A = m.w_cross.by_name["ctxT"], m.w_cross.A
        loaded, count = m.w_cross.loaded, m.w_cross.count
        S, mx, den = sb("s", [P, GROUPS, 4, KEYS]), sb("mx", [P, GROUPS, 4]), sb("den", [P, GROUPS, 4])
        W, WT = sb("w", [P, TILES, BK]), sb("wT", [P, 2, BANK])
        s = norm_state(nc, m, scope, tag)
        zeroed, step, scored, shifted, raised, weighted, wturned, wcopied = (sem(n) for n in (
            "zeroed", "step", "scored", "shifted", "raised", "weighted", "wturned", "wcopied"))
        if layer:
            VAL = sb("val", [P, D])
            WvT, bv, beta, table = buffers(m.w_cross, "wvT bv beta table")
            biased, valued, betas, tabled = sem("biased"), sem("valued"), sem("betas"), sem("tabled")
        else:
            VAL, = buffers(m.w_cross, "val")
        with nc.Block(no_gpsimd_drain=True) as block:
            @block.sync
            def _(sp):
                if layer:
                    sp.dma_start(m.gate[:, :, :], chunks(d["gateT"])).then_inc(m.gate_loaded, 16)
                    for h in range(2):
                        load_expert(sp, d, m, 0, h)
                else:
                    load(sp, m.w_route)
                    load(sp, m.w_update)

            @block.gpsimd
            def _(pool):
                if not layer:
                    pool.memset(W[:, :, :], 0.0).then_inc(zeroed, 1)
                else:
                    pool.wait_ge(loaded, count)
                    pool.tensor_tensor(beta[:, 0:1], beta[:, 0:1], beta[:, 1:2], ALU.add).then_inc(betas, 1)
                    pool.wait_ge(betas, 1)
                    pool.tensor_tensor(beta[:, 0:1], beta[:, 0:1], beta[:, 2:3], ALU.subtract).then_inc(betas, 1)
                    pool.wait_ge(betas, 2)
                    pool.tensor_scalar(table[:, :, :], table[:, :, :], beta[:, 0:1], 0.0, ALU.mult, ALU.add).then_inc(tabled, 1)
                    pool.memset(W[:, :, :], 0.0).then_inc(zeroed, 1)
                    for h in range(2):
                        weights_low(pool, m, 0, h)
                    for g in range(GROUPS - 1):
                        x_low(pool, m, g)

            @block.tensor
            def _(t):
                if layer:
                    t.wait_ge(loaded, count)
                    for k in range(KD):
                        ins = t.matmul(m.PS[:, 3, 0:D], ctxT[:, k, :], WvT[:, k, :], start=k == 0, stop=k == KD - 1)
                    ins.then_inc(valued, 1)

                def scores(g):
                    if g >= 2:
                        t.wait_ge(shifted, g - 1)
                    b = g // 2
                    for i in range(4):
                        out = m.PS[:, g % 2, i * KEYS:(i + 1) * KEYS]
                        at = (4 * g + i) * P
                        for k in range(KD):
                            ins = t.matmul(out, m.XT[:, k, at:at + P], A[:, k, b * KEYS:(b + 1) * KEYS],
                                           start=k == 0, stop=k == KD - 1)
                    ins.then_inc(scored, 1)

                def attend(g):
                    t.wait_ge(weighted, g + 1)
                    if g >= 1:
                        t.wait_ge(wcopied, g)
                    for i in range(4):
                        ins = t.transpose(m.PS[:, 2, i * P:(i + 1) * P], W[:, 4 * g + i, :], m.ident[:, :])
                    ins.then_inc(wturned, 1)
                    t.wait_ge(wcopied, g + 1)
                    for u in (2 * g, 2 * g + 1):
                        if u >= 3:
                            t.wait_ge(s.summed, u - 2)
                        for i in range(2):
                            at = (2 * (u % 2) + i) * P
                            ins = t.matmul(m.PS[:, 3 + u % 3, i * D:(i + 1) * D], WT[:, g % 2, at:at + P], VAL[:, :],
                                           start=True, stop=True)
                        ins.then_inc(s.out_done, 1)

                t.wait_ge(m.w_cross.ready, 1)
                for g in range(GROUPS):
                    scores(g)
                warm_up(t, m, 2, m.XT[:, 0, 0:BANK])
                if layer:
                    t.wait_ge(biased, 1)
                else:
                    t.wait_ge(loaded, count)
                for g in range(GROUPS + 2):
                    if g < GROUPS:
                        attend(g)
                    if 1 <= g <= GROUPS:
                        for u in (2 * g - 2, 2 * g - 1):
                            norm_turn(t, m, s, u, turn_banks)
                    if layer and g >= 2:
                        t.wait_ge(m.gate_loaded, 16)
                        t.wait_ge(shifted, GROUPS)
                        t.wait_ge(s.xt_done, 2 * g - 2)
                        gate_logits(t, m, g - 2, 0)

            @block.scalar
            def _(a):
                if layer:
                    for h in range(2):
                        weights_high(a, m, 0, h)
                for g in range(GROUPS):
                    a.wait_ge(shifted, g + 1)
                    a.activation(S[:, g, :, :], S[:, g, :, :], ACT.Exp).then_inc(raised, 1)
                load_table(a, m, ACT.Sqrt)
                for g in range(GROUPS + 2):
                    if g < GROUPS:
                        a.wait_ge(wturned, g + 1)
                        a.activation(WT[:, g % 2, :], m.PS[:, 2, :], ACT.Identity).then_inc(wcopied, 1)
                    if g >= 2:
                        for u in (2 * g - 4, 2 * g - 3):
                            norm_copy(a, m, s, u, turn_banks)
                        if layer:
                            a.wait_ge(s.xt_done, 2 * g - 2)
                            x_high(a, m, g - 2)
                    if 1 <= g <= GROUPS:
                        for u in (2 * g - 2, 2 * g - 1):
                            norm_root(a, m, s, u)
                        for u in (2 * g - 2, 2 * g - 1):
                            norm_second(a, m, s, u)
                if layer:
                    a.wait_ge(m.logits, GROUPS)
                    a.activation(m.score[:, :, :], m.PS[:, 0, :].rearrange("p (i e) -> p i e", i=TILES),
                                 ACT.Sigmoid).then_inc(m.scored, 1)

            @block.vector
            def _(v):
                dve = Steps(v, step)
                if layer:
                    v.wait_ge(loaded, count)
                    v.wait_ge(valued, 1)
                    v.tensor_tensor(VAL[:, :], m.PS[:, 3, 0:D], bv[:, :], ALU.add).then_inc(biased, 1)
                    v.wait_ge(tabled, 1)
                v.wait_ge(m.w_cross.ready, 1)

                def shift(g):
                    v.wait_ge(scored, g + 1)
                    sg = S[:, g, :, :]
                    raw = m.PS[:, g % 2, 0:4 * KEYS].rearrange("p (i n) -> p i n", i=4)
                    b = g // 2
                    dve.chain(v.tensor_tensor(sg, raw, A[:, KD:, b * KEYS:(b + 1) * KEYS].to_broadcast([P, 4, KEYS]), ALU.add))
                    raw = sg
                    if layer:
                        dve.chain(v.scalar_tensor_tensor(sg, raw, float(D) ** -0.5, table[:, 4 * g:4 * g + 4, :],
                                                         ALU.mult, ALU.add))
                    dve.chain(v.tensor_reduce(mx[:, g, :], raw, AX.X, ALU.max))
                    v.tensor_tensor(sg, raw, mx[:, g, :].unsqueeze(2).to_broadcast([P, 4, KEYS]),
                                    ALU.subtract).then_inc(shifted, 1)

                def weigh(g):
                    v.wait_ge(raised, g + 1)
                    sg, b = S[:, g, :, :], g // 2
                    dve.chain(v.tensor_reduce(den[:, g, :], sg, AX.X, ALU.add))
                    dve.chain(v.reciprocal(den[:, g, :], den[:, g, :]))
                    v.tensor_tensor(W[:, 4 * g:4 * g + 4, b * KEYS:(b + 1) * KEYS], sg,
                                    den[:, g, :].unsqueeze(2).to_broadcast([P, 4, KEYS]), ALU.mult).then_inc(weighted, 1)

                for g in range(GROUPS):
                    shift(g)
                v.wait_ge(zeroed, 1)
                weigh(0)
                weigh(1)
                for g in range(GROUPS):
                    for u in (2 * g, 2 * g + 1):
                        norm_sum(v, dve, m, s, u, 3 + u % 3)
                    if g + 2 < GROUPS:
                        weigh(g + 2)
                    for u in (2 * g, 2 * g + 1):
                        norm_scale(v, dve, s, u)
                    for u in (2 * g, 2 * g + 1):
                        norm_first(v, m, s, u)



def slot_mixer(nc, d, m):
    with ExitStack() as scope:
        m.AL = scope.enter_context(nc.sbuf_tensor("AL", [P, TILES, B * SLOTS], F32))
        m.AT = scope.enter_context(nc.sbuf_tensor("AT", [P, TOK], F32))
        m.SO = scope.enter_context(nc.sbuf_tensor("SO", [P, D], F32))
        for part in SLOT_PARTS:
            part(nc, d, m)


def slot_route(nc, d, m):
    with ExitStack() as scope:
        sem = lambda n: new_semaphore(nc, m, f"sr_{n}")
        sb = lambda n, shape: scope.enter_context(nc.sbuf_tensor(f"sr_{n}", shape, F32))
        w1, w1m, w2, b2, slots, tau = buffers(m.w_route, "w1 w1m w2 b2 slots tau")
        loaded, count = m.w_route.loaded, m.w_route.count
        mean, bias = sb("mean", [P, KD]), sb("bias", [P, 1])
        h, lg, rest = sb("h", [P, 2, BANK]), sb("lg", [P, 2, 4, SLOTS]), sb("rest", [P, 2, 4, SLOTS])
        top, ex, den = sb("top", [P, 2, 4, 8]), sb("ex", [P, 2, 4, SLOTS]), sb("den", [P, 2, 4])
        zeroed, step, summed, meaned, biasing, biased, hidden, active, routed, shifted, raised, weighted, turned, copied = (
            sem(n) for n in ("zeroed", "step", "summed", "meaned", "biasing", "biased", "hidden", "active",
                             "routed", "shifted", "raised", "weighted", "turned", "copied"))
        tau_step = sem("tau")
        with nc.Block(no_gpsimd_drain=True) as block:
            @block.sync
            def _(sp):
                load(sp, m.w_axis)

            @block.gpsimd
            def _(pool):
                pool.memset(m.AL[:, :, :], 0.0).then_inc(zeroed, 1)

            @block.tensor
            def _(t):
                t.wait_ge(loaded, count)
                for k in range(KD):
                    ins = t.matmul(m.PS[:, 5, k:k + 1], slots[:, k * P:(k + 1) * P], m.ones[0:SLOTS, 0:1], start=True, stop=True)
                ins.then_inc(summed, 1)
                t.wait_ge(meaned, 1)
                for k in range(KD):
                    ins = t.matmul(m.PS[:, 4, 0:1], w1m[:, k, :], mean[:, k:k + 1], start=k == 0, stop=k == KD - 1)
                ins.then_inc(biasing, 1)

                def hide(g):
                    if g >= 2:
                        t.wait_ge(active, g - 1)
                    for k in range(KD):
                        ins = t.matmul(m.PS[:, g % 2, :], w1[:, k, :], m.XT[:, k, g * BANK:(g + 1) * BANK],
                                       start=k == 0, stop=k == KD - 1)
                    ins.then_inc(hidden, 1)

                def route(g):
                    t.wait_ge(active, g + 1)
                    if g >= 2:
                        t.wait_ge(step, R_STEPS * (g - 2) + 1)
                    for i in range(4):
                        ins = t.matmul(m.PS[:, 2 + g % 2, i * SLOTS:(i + 1) * SLOTS], h[:, g % 2, i * P:(i + 1) * P],
                                       w2[:, :], start=True, stop=True)
                    ins.then_inc(routed, 1)

                def collect(g):
                    t.wait_ge(weighted, g + 1)
                    if g >= 1:
                        t.wait_ge(copied, g)
                    else:
                        t.wait_ge(biased, 1)
                    for i in range(4):
                        ins = t.transpose(m.PS[:, 4, i * P:(i + 1) * P], m.AL[:, 4 * g + i, :], m.ident[:, :])
                    ins.then_inc(turned, 1)
                    for i in range(4 * g, 4 * g + 4):
                        first, last = i == 0, i == TILES - 1
                        t.matmul(m.PS[:, 6, 0:D], m.AL[:, i, :], m.X[:, i, :], start=first, stop=last)
                        t.matmul(m.PS[:, 7, 0:1], m.AL[:, i, :], m.ones[:, 0:1], start=first, stop=last)

                for g in range(GROUPS + 3):
                    if g < GROUPS:
                        hide(g)
                    if 1 <= g <= GROUPS:
                        route(g - 1)
                    if g >= 3:
                        collect(g - 3)

            @block.scalar
            def _(a):
                a.wait_ge(loaded, count)
                a.activation(tau[:, :], tau[:, :], ACT.Abs).then_inc(tau_step, 1)
                a.wait_ge(summed, 1)
                a.activation(mean[:, :], m.PS[:, 5, 0:KD], ACT.Copy, scale=1.0 / SLOTS).then_inc(meaned, 1)
                a.wait_ge(biasing, 1)
                a.activation(bias[:, :], m.PS[:, 4, 0:1], ACT.Identity, bias=col(m, "f_b1")).then_inc(biased, 1)
                a.wait_ge(biased, 1)
                load_table(a, m, ACT.Gelu)
                for g in range(GROUPS + 2):
                    if g < GROUPS:
                        a.wait_ge(hidden, g + 1)
                        if g >= 2:
                            a.wait_ge(routed, g - 1)
                        a.activation(h[:, g % 2, :], m.PS[:, g % 2, :], ACT.Gelu, bias=bias[:, 0:1]).then_inc(active, 1)
                    if 1 <= g <= GROUPS:
                        a.wait_ge(shifted, g)
                        e = ex[:, (g - 1) % 2, :, :]
                        a.activation(e, e, ACT.Exp).then_inc(raised, 1)
                    if g >= 2:
                        a.wait_ge(turned, g - 1)
                        a.activation(m.AT[:, (g - 2) * BANK:(g - 1) * BANK], m.PS[:, 4, :], ACT.Identity).then_inc(copied, 1)

            @block.vector
            def _(v):
                dve = Steps(v, step)
                v.wait_ge(loaded, count)
                v.wait_ge(zeroed, 1)
                v.wait_ge(tau_step, 1)
                v.tensor_scalar(tau[:, :], tau[:, :], 0.1, None, ALU.add).then_inc(tau_step, 1)
                v.wait_ge(tau_step, 2)
                v.reciprocal(tau[:, :], tau[:, :]).then_inc(tau_step, 1)
                v.wait_ge(tau_step, 3)

                def pick(g):
                    v.wait_ge(routed, g + 1)
                    q, before = g % 2, dve.n
                    wide = lambda x: x.unsqueeze(2).to_broadcast([P, 4, SLOTS])
                    dve.chain(v.tensor_tensor(lg[:, q, :, :], m.PS[:, 2 + q, 0:4 * SLOTS].rearrange("p (i n) -> p i n", i=4),
                                              b2[:, :].unsqueeze(1).to_broadcast([P, 4, SLOTS]), ALU.add))
                    dve.chain(v.tensor_scalar(lg[:, q, :, :], lg[:, q, :, :], tau[:, 0:1], None, ALU.mult))
                    for i in range(4):
                        dve.mark(v.max(top[:, q, i, :], lg[:, q, i, :]))
                    dve.wait()
                    v.tensor_tensor(ex[:, q, :, :], lg[:, q, :, :], wide(top[:, q, :, 0]), ALU.subtract).then_inc(shifted, 1)
                    for i in range(4):
                        dve.mark(v.match_replace(rest[:, q, i, :], top[:, q, i, :], lg[:, q, i, :], LOW))
                    dve.wait()
                    dve.chain(v.tensor_tensor(rest[:, q, :, :], rest[:, q, :, :], lg[:, q, :, :], ALU.not_equal))
                    v.wait_ge(raised, g + 1)
                    dve.chain(v.tensor_tensor(ex[:, q, :, :], ex[:, q, :, :], rest[:, q, :, :], ALU.mult))
                    dve.chain(v.tensor_reduce(den[:, q, :], ex[:, q, :, :], AX.X, ALU.add))
                    dve.chain(v.reciprocal(den[:, q, :], den[:, q, :]))
                    b = g // 2
                    v.tensor_tensor(m.AL[:, 4 * g:4 * g + 4, b * SLOTS:(b + 1) * SLOTS], ex[:, q, :, :], wide(den[:, q, :]),
                                    ALU.mult).then_inc(weighted, 1)
                    assert dve.n - before == R_STEPS

                for g in range(GROUPS):
                    pick(g)


R_STEPS = 14


def slot_update(nc, d, m):
    R = B * SLOTS
    with ExitStack() as scope:
        sem = lambda n: new_semaphore(nc, m, f"su_{n}")
        sb = lambda n, shape: scope.enter_context(nc.sbuf_tensor(f"su_{n}", shape, F32))
        WihT, WhhT, slots, slotsT, bih, bhh = buffers(m.w_update, "wih whh slots slotsT bih bhh")
        wq, wk, wv, wvp, wo = buffers(m.w_update, "wq wk wv wvp wo")
        bv, ln_g, ln_b, bvp, bo = buffers(m.w_update, "bv ln_g ln_b bvp bo")
        loaded, count = m.w_update.loaded, m.w_update.count
        den, si, siT, rz, hn, new, newT = sb("den", [P, 1]), sb("si", [P, D]), sb("siT", [P, KD, R]), sb("rz", [P, 2 * D]), sb("hn", [P, D]), sb("new", [P, D]), sb("newT", [P, KD, R])
        qT, kT, val, mx, ex, sm = sb("qT", [64, R]), sb("kT", [64, R]), sb("val", [P, D]), sb("mx", [P, 1]), sb("ex", [P, SLOTS]), sb("sm", [P, 1])
        AB, ABT, y, st, mv, std = sb("ab", [P, R]), sb("abT", [P, R]), sb("y", [P, D]), sb("st", [P, 6]), sb("mv", [P, 2]), sb("std", [P, 1])
        yT, sv, svT = sb("yT", [P, KD, R]), sb("sv", [P, D]), sb("svT", [P, KD, R])
        step, zeroed, bo_added = sem("step"), sem("zeroed"), sem("bo_added")
        names = ("si", "si_turned", "siT", "gates", "rz_in", "rz", "cell_in", "cell", "new", "new_turned", "newT", "qkv",
                 "qk", "val", "scores", "top", "exps", "ab", "ab_turned", "abT", "comm", "stats", "root", "y",
                 "y_turned", "yT", "values", "sv", "sv_turned", "svT", "out")
        made = {n: sem(n) for n in names}
        with nc.Block(no_gpsimd_drain=True) as block:
            @block.gpsimd
            def _(pool):
                pool.memset(AB[:, :], 0.0).then_inc(zeroed, 1)
                pool.wait_ge(loaded, count)
                pool.tensor_tensor(m.X[:, :, :], m.X[:, :, :], bo[:, :].unsqueeze(1).to_broadcast([P, TILES, D]),
                                   ALU.add).then_inc(bo_added, 1)

            @block.tensor
            def _(t):
                def turn(src, bank, done):
                    for k in range(KD):
                        ins = t.transpose(m.PS[:, bank, k * R:(k + 1) * R], src[:, k * P:(k + 1) * P], m.ident[:, :])
                    ins.then_inc(done, 1)

                t.wait_ge(loaded, count)
                for k in range(KD):
                    t.matmul(m.PS[:, 3, 0:D], slotsT[:, k, :], WhhT[:, k, 2 * D:3 * D], start=k == 0, stop=k == KD - 1)
                for k in range(KD):
                    t.matmul(m.PS[:, 1, :], slotsT[:, k, :], WhhT[:, k, 0:2 * D], start=k == 0, stop=False)
                t.wait_ge(made["si"], 1)
                turn(si, 0, made["si_turned"])
                t.wait_ge(made["siT"], 1)
                for k in range(KD):
                    t.matmul(m.PS[:, 1, :], siT[:, k, :], WihT[:, k, 0:2 * D], start=False, stop=k == KD - 1)
                for k in range(KD):
                    ins = t.matmul(m.PS[:, 2, 0:D], siT[:, k, :], WihT[:, k, 2 * D:3 * D], start=k == 0, stop=k == KD - 1)
                ins.then_inc(made["gates"], 1)
                warm_up(t, m, 6, m.AT[:, 0:BANK], 3)
                t.wait_ge(made["new"], 1)
                turn(new, 4, made["new_turned"])
                t.wait_ge(made["newT"], 1)
                for n, w in enumerate((wq, wk)):
                    for k in range(KD):
                        t.matmul(m.PS[0:64, 5, n * R:(n + 1) * R], w[:, k, :], newT[:, k, :], start=k == 0, stop=k == KD - 1)
                for k in range(KD):
                    ins = t.matmul(m.PS[:, 2, 0:D], newT[:, k, :], wv[:, k, :], start=k == 0, stop=k == KD - 1)
                ins.then_inc(made["qkv"], 1)
                t.wait_ge(made["qk"], 2)
                for b in range(B):
                    part = slice(b * SLOTS, (b + 1) * SLOTS)
                    ins = t.matmul(m.PS[part, 3, 0:SLOTS], qT[:, part], kT[:, part], start=True, stop=True)
                ins.then_inc(made["scores"], 1)
                t.wait_ge(made["ab"], 2)
                t.transpose(m.PS[:, 0, 0:R], AB[:, :], m.ident[:, :]).then_inc(made["ab_turned"], 1)
                t.wait_ge(made["abT"], 1)
                t.wait_ge(made["val"], 1)
                t.matmul(m.PS[:, 1, 0:D], ABT[:, :], val[:, :], start=True, stop=True).then_inc(made["comm"], 1)
                warm_up(t, m, 6, m.AT[:, 0:BANK])
                t.wait_ge(made["y"], 1)
                turn(y, 4, made["y_turned"])
                t.wait_ge(made["yT"], 1)
                for k in range(KD):
                    ins = t.matmul(m.PS[:, 2, 0:D], yT[:, k, :], wvp[:, k, :], start=k == 0, stop=k == KD - 1)
                ins.then_inc(made["values"], 1)
                t.wait_ge(made["sv"], 1)
                turn(sv, 5, made["sv_turned"])
                t.wait_ge(made["svT"], 1)
                for k in range(KD):
                    ins = t.matmul(m.PS[:, 3, 0:D], svT[:, k, :], wo[:, k, :], start=k == 0, stop=k == KD - 1)
                ins.then_inc(made["out"], 1)

            @block.scalar
            def _(a):
                def copy_turned(dst, bank, turned, done):
                    a.wait_ge(turned, 1)
                    a.activation(dst, m.PS[:, bank, 0:KD * R].rearrange("p (k r) -> p k r", k=KD), ACT.Identity).then_inc(done, 1)

                copy_turned(siT[:, :, :], 0, made["si_turned"], made["siT"])
                a.wait_ge(made["rz_in"], 1)
                a.activation(rz[:, :], rz[:, :], ACT.Sigmoid).then_inc(made["rz"], 1)
                a.wait_ge(made["cell_in"], 1)
                a.activation(hn[:, :], hn[:, :], ACT.Tanh).then_inc(made["cell"], 1)
                load_table(a, m, ACT.Exp)
                copy_turned(newT[:, :, :], 4, made["new_turned"], made["newT"])
                a.wait_ge(made["qkv"], 1)
                for n, (dst, bias) in enumerate(((qT, "f_bq"), (kT, "f_bk"))):
                    a.activation(dst[:, :], m.PS[0:64, 5, n * R:(n + 1) * R], ACT.Identity, bias=col(m, bias, 0, 64)).then_inc(made["qk"], 1)
                a.wait_ge(made["top"], 1)
                a.activation(ex[:, :], m.PS[:, 3, 0:SLOTS], ACT.Exp, bias=mx[:, 0:1], scale=0.125, accum_out=sm[:, 0:1]).then_inc(made["exps"], 1)
                a.wait_ge(made["ab_turned"], 1)
                a.activation(ABT[:, :], m.PS[:, 0, 0:R], ACT.Identity).then_inc(made["abT"], 1)
                a.wait_ge(made["stats"], 1)
                a.activation(std[:, :], mv[:, 1:2], ACT.Sqrt, bias=m.eps[:, 0:1]).then_inc(made["root"], 1)
                copy_turned(yT[:, :, :], 4, made["y_turned"], made["yT"])
                copy_turned(svT[:, :, :], 5, made["sv_turned"], made["svT"])

            @block.vector
            def _(v):
                dve = Steps(v, step)
                tt = v.tensor_tensor
                dve.chain(v.tensor_scalar(den[:, :], m.PS[:, 7, 0:1], 1e-8, None, ALU.add))
                dve.chain(v.reciprocal(den[:, :], den[:, :]))
                v.tensor_scalar(si[:, :], m.PS[:, 6, 0:D], den[:, 0:1], None, ALU.mult).then_inc(made["si"], 1)
                v.wait_ge(loaded, count)
                dve.chain(tt(bih[:, 0:2 * D], bih[:, 0:2 * D], bhh[:, 0:2 * D], ALU.add))
                v.wait_ge(made["gates"], 1)
                tt(rz[:, :], m.PS[:, 1, :], bih[:, 0:2 * D], ALU.add).then_inc(made["rz_in"], 1)
                dve.mark(tt(hn[:, :], m.PS[:, 3, 0:D], bhh[:, 2 * D:3 * D], ALU.add))
                dve.chain(tt(y[:, :], m.PS[:, 2, 0:D], bih[:, 2 * D:3 * D], ALU.add))
                v.wait_ge(made["rz"], 1)
                dve.chain(tt(hn[:, :], hn[:, :], rz[:, 0:D], ALU.mult))
                tt(hn[:, :], hn[:, :], y[:, :], ALU.add).then_inc(made["cell_in"], 1)
                v.wait_ge(made["cell"], 1)
                dve.chain(tt(new[:, :], slots[:, :], hn[:, :], ALU.subtract))
                dve.chain(tt(new[:, :], new[:, :], rz[:, D:2 * D], ALU.mult))
                tt(new[:, :], new[:, :], hn[:, :], ALU.add).then_inc(made["new"], 1)
                v.wait_ge(made["qkv"], 1)
                tt(val[:, :], m.PS[:, 2, 0:D], bv[:, :], ALU.add).then_inc(made["val"], 1)
                v.wait_ge(made["scores"], 1)
                dve.chain(v.tensor_reduce(mx[:, :], m.PS[:, 3, 0:SLOTS], AX.X, ALU.max))
                v.tensor_scalar(mx[:, :], mx[:, :], -0.125, None, ALU.mult).then_inc(made["top"], 1)
                v.wait_ge(made["exps"], 1)
                v.wait_ge(zeroed, 1)
                dve.chain(v.reciprocal(sm[:, :], sm[:, :]))
                for b in range(B):
                    part = slice(b * SLOTS, (b + 1) * SLOTS)
                    v.tensor_scalar(AB[part, part], ex[part, :], sm[part, 0:1], None, ALU.mult).then_inc(made["ab"], 1)
                v.wait_ge(made["comm"], 1)
                v.wait_ge(made["new"], 1)
                dve.chain(tt(y[:, :], m.PS[:, 1, 0:D], new[:, :], ALU.add))
                dve.chain(v.bn_stats(st[:, :], y[:, :]))
                v.bn_aggr(mv[:, :], st[:, :]).then_inc(made["stats"], 1)
                v.wait_ge(made["root"], 1)
                dve.chain(v.reciprocal(std[:, :], std[:, :]))
                v.wait_ge(made["stats"], 1)
                dve.chain(v.tensor_scalar(y[:, :], y[:, :], mv[:, 0:1], std[:, 0:1], ALU.subtract, ALU.mult))
                dve.chain(tt(y[:, :], y[:, :], ln_g[:, :], ALU.mult))
                tt(y[:, :], y[:, :], ln_b[:, :], ALU.add).then_inc(made["y"], 1)
                v.wait_ge(made["values"], 1)
                tt(sv[:, :], m.PS[:, 2, 0:D], bvp[:, :], ALU.add).then_inc(made["sv"], 1)
                v.wait_ge(bo_added, 1)
                v.wait_ge(made["out"], 1)
                v.tensor_copy(m.SO[:, :], m.PS[:, 3, 0:D])


def slot_out(nc, d, m):
    banks = (4, 5)
    with ExitStack() as scope:
        s = norm_state(nc, m, scope, "so")
        step = new_semaphore(nc, m, "so_step")
        with nc.Block(no_gpsimd_drain=True) as block:
            @block.tensor
            def _(t):
                for u in range(UNITS + 2):
                    if u < UNITS:
                        if u >= 4:
                            t.wait_ge(s.summed, u - 3)
                        for i in range(2):
                            at = (2 * u + i) * P
                            ins = t.matmul(m.PS[:, u % 4, i * D:(i + 1) * D], m.AT[:, at:at + P], m.SO[:, :], start=True, stop=True)
                        ins.then_inc(s.out_done, 1)
                    if u >= 2:
                        norm_turn(t, m, s, u - 2, banks)
                wait_normed(t, s, UNITS)
                warm_up(t, m, 2, m.X[:, 0:2, :], 1)

            @block.scalar
            def _(a):
                norm_scalar_side(a, m, s, banks)

            @block.vector
            def _(v):
                norm_vector_side(v, Steps(v, step), m, s)


SLOT_PARTS = [slot_route, slot_update, slot_out]


def norm_scalar_step(a, m, s, u, banks):
    if u < UNITS:
        norm_root(a, m, s, u)
    if 1 <= u <= UNITS:
        norm_second(a, m, s, u - 1)
    if u >= 2:
        norm_copy(a, m, s, u - 2, banks)


def norm_scalar_side(a, m, s, banks):
    for u in range(UNITS + 2):
        norm_scalar_step(a, m, s, u, banks)


def norm_vector_side(v, dve, m, s):
    for u in range(UNITS + 1):
        if u < UNITS:
            norm_sum(v, dve, m, s, u, u % 4)
        if u >= 1:
            norm_scale(v, dve, s, u - 1)
            norm_first(v, m, s, u - 1)



def axis_attend(nc, d, m):
    J = TILES // B
    with ExitStack() as outer:
        OT = outer.enter_context(nc.sbuf_tensor("OT", [P, KD, TOK], F32))
        with ExitStack() as scope:
            sem = lambda n: new_semaphore(nc, m, f"aa_{n}")
            sb = lambda n, shape: scope.enter_context(nc.sbuf_tensor(f"aa_{n}", shape, F32))
            W, bias = buffers(m.w_axis, "w bias")
            loaded, count = m.w_axis.loaded, m.w_axis.count
            qk, val = sb("qk", [P, 2, B, 2 * D]), sb("val", [P, 3, B, D])
            prod, S, mx, den = sb("prod", [P, 2, B, B, D]), sb("s", [P, 3, B, B, HEADS]), sb("mx", [P, 2, B, HEADS]), sb("den", [P, 2, B, HEADS])
            pv, out = sb("pv", [P, B, B, D]), sb("out", [P, 3, B, D])
            step, projected, biased, shifted, raised, weighted, mixed, attended, turned, copied = (sem(n) for n in (
                "step", "projected", "biased", "shifted", "raised", "weighted", "mixed", "attended", "turned", "copied"))
            mixed_last, attended_last = sem("mixed_last"), sem("attended_last")
            OTv = OT[:, :, :].rearrange("p k (s j t) -> p k s j t", s=B, j=J)
            with nc.Block(no_gpsimd_drain=True) as block:
                @block.sync
                def _(sp):
                    load(sp, m.w_axis_out)
                    load(sp, m.w_cross)

                @block.tensor
                def _(t):
                    def project(j):
                        if j >= 2:
                            t.wait_ge(biased, 3 * (j - 1))
                        at = 3 * (j % 2)
                        for s in range(B):
                            tile = (j + J * s) * P
                            for k in range(KD):
                                t.matmul(m.PS[:, at + s, :], m.XT[:, k, tile:tile + P], W[:, k, 0:2 * D], start=k == 0, stop=k == KD - 1)
                            for k in range(KD):
                                ins = t.matmul(m.PS[:, at + 2, s * D:(s + 1) * D], m.XT[:, k, tile:tile + P], W[:, k, 2 * D:3 * D],
                                               start=k == 0, stop=k == KD - 1)
                        ins.then_inc(projected, 1)

                    def turn(j):
                        if j < J - 1:
                            t.wait_ge(attended, j + 1)
                        else:
                            t.wait_ge(attended_last, 1)
                        if j >= 2:
                            t.wait_ge(copied, j - 1)
                        for k in range(KD):
                            for s in range(B):
                                ins = t.transpose(m.PS[:, 6 + j % 2, (2 * k + s) * P:(2 * k + s + 1) * P],
                                                  out[:, j % 3, s, k * P:(k + 1) * P], m.ident[:, :])
                        ins.then_inc(turned, 1)

                    t.wait_ge(loaded, count)
                    for j in range(J + 3):
                        if j < J:
                            project(j)
                        if j == J + 1:
                            t.wait_ge(biased, 3 * J)
                            t.wait_ge(weighted, J - 1)
                            warm_up(t, m, 0, W[:, 0, 0:BANK])
                        if j >= 3:
                            turn(j - 3)

                @block.scalar
                def _(a):
                    for j in range(J + 3):
                        if j < J:
                            a.wait_ge(shifted, j + 1)
                            a.activation(S[:, j % 3], S[:, j % 3], ACT.Exp, scale=float(HD) ** -0.5).then_inc(raised, 1)
                        if j >= 3:
                            a.wait_ge(turned, j - 2)
                            a.activation(OTv[:, :, :, j - 3, :], m.PS[:, 6 + (j - 3) % 2, :].rearrange("p (k s t) -> p k s t", k=KD, s=B),
                                         ACT.Identity).then_inc(copied, 1)

                @block.gpsimd
                def _(pool):
                    for j in range(J - 1):
                        pool.wait_ge(weighted, j + 1)
                        if j >= 1:
                            pool.wait_ge(attended, j)
                        for s in range(B):
                            pool.tensor_tensor(pv[:, s, :, :].rearrange("p t (h c) -> p t h c", h=HEADS),
                                               S[:, j % 3, s, :, :].unsqueeze(3).to_broadcast([P, B, HEADS, HD]),
                                               val[:, j % 3, :, :].rearrange("p t (h c) -> p t h c", h=HEADS), ALU.mult).then_inc(mixed, 1)
                        pool.wait_ge(mixed, 2 * (j + 1))
                        if j >= 3:
                            pool.wait_ge(turned, j - 2)
                        pool.tensor_tensor(out[:, j % 3], pv[:, :, 0, :], pv[:, :, 1, :], ALU.add).then_inc(attended, 1)

                @block.vector
                def _(v):
                    dve = Steps(v, step)
                    v.wait_ge(loaded, count)

                    def score(j):
                        q = j % 2
                        v.wait_ge(projected, j + 1)
                        if j >= 3:
                            v.wait_ge(attended, j - 2)
                        v.tensor_tensor(qk[:, q, :, :], m.PS[:, 3 * q:3 * q + 2, :],
                                        bias[:, 0:2 * D].unsqueeze(1).to_broadcast([P, B, 2 * D]), ALU.add).then_inc(biased, 2)
                        v.tensor_tensor(val[:, j % 3, :, :], m.PS[:, 3 * q + 2, :].rearrange("p (s n) -> p s n", s=B),
                                        bias[:, 2 * D:].unsqueeze(1).to_broadcast([P, B, D]), ALU.add).then_inc(biased, 1)
                        v.wait_ge(biased, 3 * (j + 1))
                        for s in range(B):
                            dve.mark(v.tensor_tensor(prod[:, q, s, :, :], qk[:, q, s, 0:D].unsqueeze(1).to_broadcast([P, B, D]),
                                                     qk[:, q, :, D:2 * D], ALU.mult))
                        dve.wait()
                        dve.chain(v.tensor_reduce(S[:, j % 3].rearrange("p s t h -> p (s t h)"),
                                                  prod[:, q].rearrange("p s t (h c) -> p (s t h) c", h=HEADS), AX.X, ALU.add))
                        dve.chain(v.tensor_tensor(mx[:, q, :, :], S[:, j % 3, :, 0, :], S[:, j % 3, :, 1, :], ALU.max))
                        v.tensor_tensor(S[:, j % 3], S[:, j % 3], mx[:, q, :, :].unsqueeze(2).to_broadcast([P, B, B, HEADS]),
                                        ALU.subtract).then_inc(shifted, 1)

                    def weigh(j):
                        q = j % 2
                        v.wait_ge(raised, j + 1)
                        dve.chain(v.tensor_tensor(den[:, q, :, :], S[:, j % 3, :, 0, :], S[:, j % 3, :, 1, :], ALU.add))
                        dve.chain(v.reciprocal(den[:, q, :, :], den[:, q, :, :]))
                        v.tensor_tensor(S[:, j % 3], S[:, j % 3], den[:, q, :, :].unsqueeze(2).to_broadcast([P, B, B, HEADS]),
                                        ALU.mult).then_inc(weighted, 1)

                    def mix_last():
                        j, pv = J - 1, prod[:, (J - 1) % 2]
                        v.wait_ge(weighted, j + 1)
                        for s in range(B):
                            v.tensor_tensor(pv[:, s, :, :].rearrange("p t (h c) -> p t h c", h=HEADS),
                                            S[:, j % 3, s, :, :].unsqueeze(3).to_broadcast([P, B, HEADS, HD]),
                                            val[:, j % 3, :, :].rearrange("p t (h c) -> p t h c", h=HEADS), ALU.mult).then_inc(mixed_last, 1)
                        v.wait_ge(mixed_last, 2)
                        v.wait_ge(turned, j - 2)
                        v.tensor_tensor(out[:, j % 3], pv[:, :, 0, :], pv[:, :, 1, :], ALU.add).then_inc(attended_last, 1)

                    for j in range(J + 1):
                        if j < J:
                            score(j)
                        if j >= 1:
                            weigh(j - 1)
                    mix_last()
        axis_out(nc, d, m, OT)


def axis_out(nc, d, m, OT):
    banks = (4, 5)
    with ExitStack() as scope:
        sem = lambda n: new_semaphore(nc, m, f"ao_{n}")
        W, bias = buffers(m.w_axis_out, "w bias")
        loaded, count = m.w_axis_out.loaded, m.w_axis_out.count
        s = norm_state(nc, m, scope, "ao")
        step, biased = sem("step"), sem("biased")
        with nc.Block(no_gpsimd_drain=True) as block:
            @block.gpsimd
            def _(pool):
                pool.wait_ge(loaded, count)
                for u in range(UNITS):
                    xu = m.X[:, 2 * u:2 * u + 2, :]
                    pool.tensor_tensor(xu, xu, bias[:, :].unsqueeze(1).to_broadcast([P, 2, D]), ALU.add).then_inc(biased, 1)
                widen_bq(pool, m)

            @block.tensor
            def _(t):
                t.wait_ge(loaded, count)
                for u in range(UNITS + 2):
                    if u < UNITS:
                        if u >= 4:
                            t.wait_ge(s.summed, u - 3)
                        for i in range(2):
                            at = (2 * u + i) * P
                            for k in range(KD):
                                ins = t.matmul(m.PS[:, u % 4, i * D:(i + 1) * D], OT[:, k, at:at + P], W[:, k, :],
                                               start=k == 0, stop=k == KD - 1)
                        ins.then_inc(s.out_done, 1)
                    if u >= 2:
                        norm_turn(t, m, s, u - 2, banks)
                    if u == 2:
                        make_keys(t, m, 6)
                    if u == 4:
                        fold_queries(t, m, 7)
                wait_normed(t, s, UNITS)
                warm_up(t, m, 2, m.X[:, 0:2, :], 1)

            @block.scalar
            def _(a):
                for u in range(UNITS + 2):
                    norm_scalar_step(a, m, s, u, banks)
                    if u == 2:
                        copy_keys(a, m, 6)
                    if u == 4:
                        copy_folded(a, m, 7)

            @block.vector
            def _(v):
                dve = Steps(v, step)
                for u in range(UNITS + 1):
                    if u < UNITS:
                        v.wait_ge(biased, u + 1)
                        norm_sum(v, dve, m, s, u, u % 4)
                    if u >= 1:
                        norm_scale(v, dve, s, u - 1)
                        norm_first(v, m, s, u - 1)



def expert_weights(nc, m, mem):
    sb = lambda n, shape, dt=F32: mem.enter_context(nc.sbuf_tensor(n, shape, dt))
    m.XS = [sb(f"XT_{z}", [P, KD, TOK], F32R) for z in ("high", "low")]
    m.GU, m.DN = [sb(f"gu{h}", [P, KD, 2 * P]) for h in range(2)], [sb(f"dn{h}", [P, D]) for h in range(2)]
    m.GUS = [[sb(f"gu{h}{z}", [P, KD, 2 * P], F32R) for z in ("high", "low")] for h in range(2)]
    m.DNS = [[sb(f"dn{h}{z}", [P, D], F32R) for z in ("high", "low")] for h in range(2)]
    m.gate, m.score = sb("gate", [P, KD, EXPERTS]), sb("score", [P, TILES, EXPERTS])
    m.w_loaded, m.w_high, m.w_split = ([new_semaphore(nc, m, f"w_{n}{h}") for h in range(2)] for n in ("loaded", "high", "split"))
    m.gate_loaded, m.logits, m.x_high, m.x_low, m.scored = (
        new_semaphore(nc, m, n) for n in ("gate_loaded", "logits", "x_high", "x_low", "scored"))


def load_expert(sp, d, m, it, h):
    sp.dma_start(m.GU[h][:, :, :], d["guT"][2 * it + h].rearrange("(k p) n -> p k n", p=P)).then_inc(m.w_loaded[h], 16)
    sp.dma_start(m.DN[h][:, :], d["dnT"][2 * it + h]).then_inc(m.w_loaded[h], 16)


def weights_high(a, m, it, h):
    a.wait_ge(m.w_loaded[h], it * 32 + 32)
    for dst, src in ((m.GUS[h][0], m.GU[h]), (m.DNS[h][0], m.DN[h])):
        a.activation(dst[:], src[:], ACT.Copy).then_inc(m.w_high[h], 1)


def weights_low(pool, m, it, h):
    pool.wait_ge(m.w_high[h], 2 * it + 2)
    for dst, src in ((m.GUS[h], m.GU[h]), (m.DNS[h], m.DN[h])):
        pool.tensor_tensor(dst[1][:], src[:], dst[0][:].bitcast(F32), ALU.subtract).then_inc(m.w_split[h], 1)


def x_high(a, m, g):
    part = slice(g * BANK, (g + 1) * BANK)
    a.activation(m.XS[0][:, :, part], m.XT[:, :, part], ACT.Copy).then_inc(m.x_high, 1)


def x_low(pool, m, g):
    part = slice(g * BANK, (g + 1) * BANK)
    pool.wait_ge(m.x_high, g + 1)
    pool.tensor_tensor(m.XS[1][:, :, part], m.XT[:, :, part], m.XS[0][:, :, part].bitcast(F32),
                       ALU.subtract).then_inc(m.x_low, 1)


def gate_logits(t, m, g, bank):
    for i in range(4 * g, 4 * g + 4):
        for k in range(KD):
            ins = t.matmul(m.PS[:, bank, i * EXPERTS:(i + 1) * EXPERTS], m.XT[:, k, i * P:(i + 1) * P], m.gate[:, k, :],
                           start=k == 0, stop=k == KD - 1)
    ins.then_inc(m.logits, 1)


def experts(nc, d, m):
    ROUNDS = ALL_E // 2
    UPR = 2 * GROUPS
    GS = EXPERTS // GROUPS_E
    PARTS = ((0, 0), (0, 1), (1, 0))
    out = d["out"].rearrange("(i p) d -> p i d", p=P)
    with ExitStack() as scope:
        sem = lambda n: new_semaphore(nc, m, f"ex_{n}")
        sb = lambda n, shape, dt=F32: scope.enter_context(nc.sbuf_tensor(f"ex_{n}", shape, dt))
        C = sb("c", [P, TILES, EXPERTS])
        SI, H = sb("si", [P, 2, BANK]), sb("h", [P, 2, BANK])
        HS = [sb(f"h{z}", [P, 2, BANK], F32R) for z in ("high", "low")]
        ebias, biased_score = sb("ebias", [P, EXPERTS]), sb("biased", [P, TILES, EXPERTS])
        group, group_rest, group_top = sb("group", [P, TILES, 12]), sb("group_rest", [P, TILES, 12]), sb("group_top", [P, TILES, 8])
        masked, rest, top, den = sb("masked", [P, TILES, EXPERTS + 2]), sb("rest", [P, TILES, EXPERTS + 2]), sb("top", [P, TILES, 8]), sb("den", [P, TILES])
        s = norm_state(nc, m, scope, "ln")
        gu_done, silu_done, prod_done, high_done, h_done, down_done, acc_done = (
            sem(n) for n in ("gu", "silu", "prod", "high", "h", "down", "acc"))
        loaded, step, stored = sem("loaded"), sem("step"), sem("stored")
        with nc.Block(no_gpsimd_drain=True) as block:
            @block.sync
            def _(sp):
                sp.dma_start(ebias[:, :], rows_of(d["e_bias"])).then_inc(loaded, 16)
                with sp.Fori(1, ROUNDS) as it:
                    for h in range(2):
                        sp.wait_ge(m.w_split[h], 2 * it)
                        load_expert(sp, d, m, it, h)
                for u in range(0, UNITS, 2):
                    wait_normed(sp, s, u + 2)
                    sp.dma_start(out[:, 2 * u:2 * u + 4, :], m.X[:, 2 * u:2 * u + 4, :]).then_inc(stored, 16)
                sp.wait_ge(stored, 16 * UNITS // 2)

            @block.gpsimd
            def _(pool):
                x_low(pool, m, GROUPS - 1)
                with pool.Fori(1, ROUNDS) as it:
                    for h in range(2):
                        weights_low(pool, m, it, h)
                for u in range(UNITS - 2):
                    norm_first(pool, m, s, u)

            @block.tensor
            def _(t):
                def gate_up(it, u, first=False):
                    h, g = divmod(u, GROUPS)
                    if g == 0:
                        t.wait_ge(m.w_split[h], 2 * it + 2)
                    if not first:
                        t.wait_ge(prod_done, it * UPR + (u - 1))
                    for part in range(2):
                        for k in range(KD):
                            for n, (w, x) in enumerate(PARTS):
                                ins = t.matmul(m.PS[:, 2 * part + u % 2, :], m.GUS[h][w][:, k, part * P:(part + 1) * P],
                                               m.XS[x][:, k, g * BANK:(g + 1) * BANK],
                                               start=k == 0 and n == 0, stop=k == KD - 1 and n == 2)
                    ins.then_inc(gu_done, 1)

                def down(it, u):
                    h = u // GROUPS
                    n = it * UPR + u
                    t.wait_ge(h_done, n + 1)
                    t.wait_ge(acc_done, n + 1)
                    for i in range(4):
                        for z, (a_, w) in enumerate(PARTS):
                            ins = t.matmul(m.PS[:, 4 + 2 * (u % 2) + i // 2, (i % 2) * D:(i % 2 + 1) * D],
                                           HS[a_][:, u % 2, i * P:(i + 1) * P], m.DNS[h][w][:, :], start=z == 0, stop=z == 2)
                    ins.then_inc(down_done, 1)

                def unit(it, u, ahead=True):
                    if u + 2 < UPR:
                        gate_up(it, u + 2)
                    elif ahead:
                        gate_up(it + 1, u + 2 - UPR)
                    down(it, u)

                t.wait_ge(m.x_low, GROUPS - 1)
                gate_up(0, 0, first=True)
                gate_up(0, 1, first=True)
                t.wait_ge(m.x_low, GROUPS)
                with t.Fori(0, ROUNDS - 1) as it:
                    for u in range(UPR):
                        unit(it, u)
                for u in range(UPR):
                    unit(ROUNDS - 1, u, ahead=False)

            @block.scalar
            def _(a):
                def silu(it, u):
                    a.wait_ge(gu_done, it * UPR + (u + 1))
                    a.activation(SI[:, u % 2, :], m.PS[:, u % 2, :], ACT.Silu).then_inc(silu_done, 1)

                def high(it, u):
                    a.wait_ge(prod_done, it * UPR + (u + 1))
                    a.activation(HS[0][:, u % 2, :], H[:, u % 2, :], ACT.Copy).then_inc(high_done, 1)

                def next_weights(it, h):
                    a.wait_ge(down_done, it * UPR - (UPR - GROUPS * (h + 1)))
                    weights_high(a, m, it, h)

                def turn(it, first=False, last=False):
                    for u in range(UPR):
                        if u + 1 < UPR:
                            silu(it, u + 1)
                        elif not last:
                            silu(it + 1, 0)
                        high(it, u)
                        if u == 0 and not first:
                            next_weights(it, 1)
                        if u == GROUPS and not last:
                            next_weights(it + 1, 0)

                silu(0, 0)
                turn(0, first=True)
                with a.Fori(1, ROUNDS - 1) as it:
                    turn(it)
                turn(ROUNDS - 1, last=True)
                for u in range(UNITS - 2):
                    norm_root(a, m, s, u)
                for u in range(UNITS):
                    if u == UNITS - 4:
                        norm_root(a, m, s, UNITS - 2)
                        norm_root(a, m, s, UNITS - 1)
                    norm_second(a, m, s, u)

            @block.vector
            def _(v):
                dve = Steps(v, step)

                def product(it, u):
                    v.wait_ge(silu_done, it * UPR + (u + 1))
                    v.tensor_tensor(H[:, u % 2, :], m.PS[:, 2 + u % 2, :], SI[:, u % 2, :], ALU.mult).then_inc(prod_done, 1)

                def low(it, u):
                    v.wait_ge(high_done, it * UPR + (u + 1))
                    v.tensor_tensor(HS[1][:, u % 2, :], H[:, u % 2, :], HS[0][:, u % 2, :].bitcast(F32),
                                    ALU.subtract).then_inc(h_done, 1)

                def accumulate(it, u, half, shared=False):
                    h, g = divmod(u, GROUPS)
                    if half == 0:
                        v.wait_ge(down_done, it * UPR + (u + 1))
                    for i in (2 * half, 2 * half + 1):
                        x = m.X[:, 4 * g + i, :]
                        y = m.PS[:, 4 + 2 * (u % 2) + i // 2, (i % 2) * D:(i % 2 + 1) * D]
                        if shared:
                            ins = v.tensor_tensor(x, y, x, ALU.add)
                        else:
                            ins = v.scalar_tensor_tensor(x, y, C[:, 4 * g + i, bass.ds(it * 2 + (h - SHARED), 1)], x,
                                                         ALU.mult, ALU.add)
                    if half == 1:
                        ins.then_inc(acc_done, 1)

                def unit(it, u, shared=False, last=False):
                    nxt = (it, u + 1) if u + 1 < UPR else (it + 1, 0)
                    more = u + 1 < UPR or not last
                    if more:
                        product(*nxt)
                    accumulate(it, u, 0, shared)
                    if more:
                        low(*nxt)
                    accumulate(it, u, 1, shared)

                grouped = lambda x: x.rearrange("p i (g e) -> p i g e", g=GROUPS_E)

                def route(n):
                    if n == 0:
                        dve.chain(v.tensor_tensor(biased_score[:, :, :], m.score[:, :, :],
                                                  ebias[:, :].unsqueeze(1).to_broadcast([P, TILES, EXPERTS]), ALU.add))
                        dve.chain(v.tensor_reduce(group[:, :, 0:GROUPS_E], grouped(biased_score[:, :, :]), AX.X, ALU.max))
                        for i in range(TILES):
                            dve.mark(v.max(group_top[:, i, :], group[:, i, 0:GROUPS_E]))
                        dve.wait()
                    elif n == 1:
                        dve.chain(v.memset(group_top[:, :, TOP_GROUPS:8], LOW))
                        for i in range(TILES):
                            dve.mark(v.match_replace(group_rest[:, i, :], group_top[:, i, :], group[:, i, :], HIGH))
                        dve.wait()
                    elif n == 2:
                        dve.chain(v.tensor_tensor(group_rest[:, :, :], group_rest[:, :, :], group[:, :, :], ALU.not_equal))
                        dve.chain(v.tensor_tensor(grouped(masked[:, :, 0:EXPERTS]), grouped(biased_score[:, :, :]),
                                                  group_rest[:, :, 0:GROUPS_E].unsqueeze(3).to_broadcast([P, TILES, GROUPS_E, GS]),
                                                  ALU.mult))
                        dve.chain(v.tensor_scalar(masked[:, :, 0:EXPERTS], masked[:, :, 0:EXPERTS], 0.0, None, ALU.add))
                    elif n == 3:
                        for i in range(TILES):
                            dve.mark(v.max(top[:, i, :], masked[:, i, 0:EXPERTS]))
                        dve.wait()
                    elif n == 4:
                        dve.chain(v.memset(top[:, :, TOP_E:8], LOW))
                        for i in range(TILES):
                            dve.mark(v.match_replace(rest[:, i, :], top[:, i, :], masked[:, i, :], HIGH))
                        dve.wait()
                    elif n == 5:
                        dve.chain(v.tensor_tensor(rest[:, :, 0:EXPERTS], rest[:, :, 0:EXPERTS], masked[:, :, 0:EXPERTS], ALU.not_equal))
                        dve.chain(v.tensor_tensor(m.score[:, :, :], m.score[:, :, :], rest[:, :, 0:EXPERTS], ALU.mult))
                        dve.chain(v.tensor_reduce(den[:, :], m.score[:, :, :], AX.X, ALU.add))
                    elif n == 6:
                        dve.chain(v.tensor_scalar(den[:, :], den[:, :], 1e-20, None, ALU.add))
                        dve.chain(v.reciprocal(den[:, :], den[:, :]))
                        dve.chain(v.tensor_scalar(den[:, :], den[:, :], 2.5, None, ALU.mult))
                        dve.chain(v.tensor_tensor(C[:, :, :], m.score[:, :, :],
                                                  den[:, :].unsqueeze(2).to_broadcast([P, TILES, EXPERTS]), ALU.mult))

                def norm_group(g):
                    v.wait_ge(acc_done, ROUNDS * UPR - GROUPS + g + 3)
                    for u in (2 * g, 2 * g + 1):
                        norm_sum(v, dve, m, s, u, None)

                def scale_units(first, end):
                    v.wait_ge(s.root, end)
                    dve.chain(v.reciprocal(s.rstd[:, first:end, :], s.std[:, first:end, :]))
                    v.scalar_tensor_tensor(s.shift[:, first:end, :], s.mv[:, first:end, :, 0], -1.0, s.rstd[:, first:end, :],
                                           ALU.mult, ALU.mult).then_inc(s.scaled, end - first)

                v.sem_inc(acc_done, 2)
                dve.mark(v.memset(group[:, :, GROUPS_E:12], LOW))
                dve.mark(v.memset(masked[:, :, EXPERTS:EXPERTS + 2], LOW))
                product(0, 0)
                low(0, 0)
                v.wait_ge(loaded, 16)
                for u in range(UPR):
                    unit(0, u, shared=True)
                    route(u)
                with v.Fori(1, ROUNDS - 1) as it:
                    for u in range(UPR):
                        unit(it, u)
                for u in range(UPR):
                    unit(ROUNDS - 1, u, last=True)
                    if u == GROUPS:
                        norm_group(0)
                    if u == UPR - 2:
                        norm_group(1)
                        norm_group(2)
                        scale_units(0, UNITS // 2)
                    if u == UPR - 1:
                        scale_units(UNITS // 2, UNITS - 2)
                        norm_group(GROUPS - 1)
                scale_units(UNITS - 2, UNITS)
                v.wait_ge(s.normed_first, UNITS - 2)
                for u in (UNITS - 2, UNITS - 1):
                    norm_first(v, m, s, u)


def build(nc, d):
    with ExitStack() as mem:
        m = Record()
        m.semaphores = []
        sb = lambda n, shape: mem.enter_context(nc.sbuf_tensor(n, shape, F32))
        m.X, m.XT = sb("X", [P, TILES, D]), sb("XT", [P, KD, TOK])
        m.ident, m.cols, m.eps, m.ones = sb("ident", [P, P]), sb("cols", [P, NCOLS]), sb("eps", [P, 1]), sb("ones", [P, P])
        m.unread, m.tables_loaded = sb("unread", [P, 8]), -1
        m.PS = mem.enter_context(nc.psum_tensor("PS", [P, 8, BANK], F32))
        m.FW, m.IV = sb("FW", [P, CLASSES, 3, P]), sb("IV", [P, CLASSES, 3, P])
        with ExitStack() as hyena:
            m.transforms_loaded = new_semaphore(nc, m, "transforms_loaded")
            m.x_loaded = [new_semaphore(nc, m, f"x_loaded{g}") for g in range(GROUPS)]
            m.V = hyena.enter_context(nc.sbuf_tensor("V", [P, 3, BLOCKS, B * D], F32))
            m.H = m.X[:, :, :].rearrange("p i d -> p (i d)").rearrange("p (a n) -> p a n", n=BANK)
            hyena_out_weights(nc, d, m, hyena)
            with ExitStack() as convolution:
                m.cv = convolution_state(nc, m, convolution)
                hyena_prepare(nc, d, m)
                hyena_convolve(nc, d, m)
            cross_weights(nc, d, m, hyena, 0)
            hyena_out(nc, d, m)
            slot_weights(nc, d, m, hyena)
            cross_attend(nc, d, m, 0)
            axis_weights(nc, d, m)
            slot_mixer(nc, d, m)
        end_layer(nc, m)
        cross_weights(nc, d, m, mem, 1)
        axis_attend(nc, d, m)
        expert_weights(nc, m, mem)
        cross_attend(nc, d, m, 1)
        experts(nc, d, m)


def constants():
    f4 = np.float32
    t = np.arange(L, dtype=f4) / f4(L - 1)
    bands = np.arange(EMB, dtype=f4)
    arg = ((t[:, None] * bands[None, :]).astype(f4) * f4(FREQ)).astype(f4)
    peT = np.sin(arg.astype(np.float64)).astype(f4).T
    negt = -t.reshape(BLOCKS, P).T
    p, r, c = np.arange(P)[:, None, None], np.arange(P)[None, None, :], np.arange(CLASSES)[None, :, None]
    turn = (p * (2 * (c + 16 * r) + 1)) % (4 * L) * (np.pi / (2 * L))
    forward = np.stack([np.cos(turn), np.sin(turn), -np.sin(turn)], axis=2)
    inverse = np.ascontiguousarray(forward.transpose(3, 1, 2, 0)) / (L * L)
    return {"peT": peT, "negt": negt, "forward": forward, "inverse": inverse, "ident": np.eye(P)}


def expert_gates(g):
    own = g["L1_ffn_experts_gate_up"].transpose(0, 2, 1)
    gate, up = (g[f"L1_ffn_shared_{n}_w"].reshape(SHARED, P, D) for n in ("gate", "up"))
    return np.concatenate([np.concatenate([gate, up], axis=1).transpose(0, 2, 1), own])


def expert_downs(g):
    own = g["L1_ffn_experts_down"].transpose(0, 2, 1)
    return np.concatenate([g["L1_ffn_shared_down_w"].T.reshape(SHARED, P, D), own])


def kernel(**inputs):
    import concourse.bacc as bacc
    from concourse.bass_utils import run_bass_kernel_spmd

    g = {k: np.asarray(v) for k, v in inputs.items()}
    cols = np.zeros((P, NCOLS), np.float32)
    for name, source in (("b_in", "L0_attn_b_in"), ("conv_b", "L0_attn_conv_b"), ("hy_b1", "L0_attn_b1"),
                         ("x0_bq", "L0_xattn_bq"), ("x0_bk", "L0_xattn_bk"), ("f_b1", "L0_ffn_b1"),
                         ("f_bq", "L0_ffn_bq"), ("f_bk", "L0_ffn_bk"), ("x1_bq", "L1_xattn_bq"), ("x1_bk", "L1_xattn_bk")):
        at, n = COLS[name]
        part = g[source].reshape(n, -1).T
        cols[:part.shape[0], at:at + n] = part
    at, n = COLS["conv_w"]
    cols[:, at:at + n] = g["L0_attn_conv_w"].reshape(6, P, 3).transpose(1, 0, 2).reshape(P, 18)
    x = g["x"].reshape(TOK, D)
    arrays = {
        "x": x, "xT": x.T, "cols": cols,
        "hy_w_inT": g["L0_attn_w_in"].T, "hy_w1T": g["L0_attn_w1"].T, "hy_w2T": g["L0_attn_w2"].T,
        "hy_b2": g["L0_attn_b2"], "hy_decay": g["L0_attn_filt_decay"].reshape(-1),
        "hy_fbias": g["L0_attn_filt_bias"].reshape(-1), "hy_w_outT": g["L0_attn_w_out"].T, "hy_b_out": g["L0_attn_b_out"],
        "ctx": g["ctx_1024"].reshape(B * KEYS, D), "ctxT": g["ctx_1024"].reshape(B * KEYS, D).T,
        "wkT0": g["L0_xattn_Wk"].T, "wq0": g["L0_xattn_Wq"], "wkT1": g["L1_xattn_Wk"].T, "wq1": g["L1_xattn_Wq"],
        "wvT": g["L1_xattn_Wv"].T, "bv": g["L1_xattn_bv"], "table": g["fside_BxSxS2_0"].reshape(TOK, KEYS),
        "betas": np.stack([g[f"L1_xattn_beta_{n}"].reshape(()) for n in ("risk", "prio", "impl")]),
        "slots2": np.tile(g["L0_ffn_slot_init"], (B, 1)), "slotsT2": np.tile(g["L0_ffn_slot_init"], (B, 1)).T,
        "f_wihT": g["L0_ffn_Wih"].T, "f_whhT": g["L0_ffn_Whh"].T,
        **{f"f_{n}": g[f"L0_ffn_{n}"] for n in ("w1", "w2", "b2", "tau", "bih", "bhh", "wq", "wk", "wv", "bv",
                                                "ln_g", "ln_b", "wvp", "bvp", "wo", "bo")},
        "a_inT": g["L1_attn_in_proj_w"].T, "a_in_b": g["L1_attn_in_proj_b"],
        "a_outT": g["L1_attn_out_proj_w"].T, "a_out_b": g["L1_attn_out_proj_b"],
        "gateT": g["L1_ffn_gate_weight"].T, "e_bias": g["L1_ffn_e_score_correction_bias"],
        "guT": expert_gates(g), "dnT": expert_downs(g),
        **constants(),
    }
    nc = bacc.Bacc("TRN2", target_bir_lowering=False, num_devices=1)
    d, fed = {}, {}
    for name, a in arrays.items():
        fed[f"in_{name}"] = np.ascontiguousarray(a, dtype=np.float32)
        d[name] = nc.dram_tensor(f"in_{name}", fed[f"in_{name}"].shape, F32, kind="ExternalInput").ap()
    d["out"] = nc.dram_tensor("out", (TOK, D), F32, kind="ExternalOutput").ap()
    build(nc, d)
    r = run_bass_kernel_spmd(nc, [fed], core_ids=[0])
    return r.results[0]["out"].reshape(B, L, D)
```
